# Optimizing a Trainium2 kernel written in Bass

```python
import numpy as np
import jax
import jax.numpy as jnp

def _softmax(x, axis=-1):
    return jax.nn.softmax(x, axis=axis)

def _gelu(x):
    return jax.nn.gelu(x, approximate=True)

def _silu(x):
    return jax.nn.silu(x)

def _sigmoid(x):
    return jax.nn.sigmoid(x)

def _layernorm(x, axis=-1, eps=1e-05):
    m = jnp.mean(x, axis=axis, keepdims=True)
    v = jnp.var(x, axis=axis, keepdims=True)
    return (x - m) / jnp.sqrt(v + eps)

def _scatter_add(tgt, idx, src, axis=0):
    return tgt.at[idx].add(src)

def _segment_sum(src, seg, n):
    return jax.ops.segment_sum(src, seg, n)
kernel_name = 'mk_gnn_preln_d2_gnn_r64_c13e15'

def setup_inputs(seed: int=0):
    np.random.seed(seed)
    _w = jnp.asarray

    def _rec_inputs():
        import jax
        import jax.numpy as jnp
        _gk = jax.random.key(seed)
        x = 8.953e-05 + 1 * jax.random.normal(jax.random.fold_in(_gk, 1), (100000, 32), jnp.float32)
        src = jax.random.randint(jax.random.fold_in(_gk, 2), (25000,), 0, 100000, jnp.int32)
        dst = jax.random.randint(jax.random.fold_in(_gk, 3), (25000,), 0, 100000, jnp.int32)
        _o = jnp.argsort(dst, stable=True)
        src = src[_o]
        dst = dst[_o]
        edge_attr_3 = 0.000844983 + 0.999762 * jax.random.normal(jax.random.fold_in(_gk, 11), (25000, 3), jnp.float32)
        edge_weight = jax.random.uniform(jax.random.fold_in(_gk, 13), (25000,), jnp.float32, 0.0, 1)
        return (x, src, dst, edge_attr_3, edge_weight)
    x, src, dst, edge_attr_3, edge_weight = _rec_inputs()

    def _L0_gnn_setup():
        import jax, jax.numpy as jnp
        import numpy as np
        from math import factorial, pi, sqrt
        MUL = 8
        RS = [(MUL, 0), (MUL, 1)]
        N_NODES = 20000
        N_EDGES = 10000
        FEAT_DIM = sum((m * (2 * l + 1) for m, l in RS))
        R_DIM = sum((mo * mi * (2 * min(lo, li) + 1) for mo, lo in RS for mi, li in RS))
        HIDDEN = 64

        def _cg(j1, j2, j3, m1, m2, m3):
            if m1 + m2 != m3:
                return 0.0
            f = factorial
            pre = sqrt((2 * j3 + 1) * f(j3 + j1 - j2) * f(j3 - j1 + j2) * f(j1 + j2 - j3) / f(j1 + j2 + j3 + 1))
            pre *= sqrt(f(j3 + m3) * f(j3 - m3) * f(j1 - m1) * f(j1 + m1) * f(j2 - m2) * f(j2 + m2))
            kmin = max(0, j2 - j3 - m1, j1 - j3 + m2)
            kmax = min(j1 + j2 - j3, j1 - m1, j2 + m2)
            s = 0.0
            for k in range(kmin, kmax + 1):
                s += (-1) ** k / (f(k) * f(j1 + j2 - j3 - k) * f(j1 - m1 - k) * f(j2 + m2 - k) * f(j3 - j2 + m1 + k) * f(j3 - j1 - m2 + k))
            return pre * s

        def _w3j_complex(l1, l2, l3):
            w = np.zeros((2 * l1 + 1, 2 * l2 + 1, 2 * l3 + 1))
            for m1 in range(-l1, l1 + 1):
                for m2 in range(-l2, l2 + 1):
                    m3 = -(m1 + m2)
                    if abs(m3) <= l3:
                        w[m1 + l1, m2 + l2, m3 + l3] = (-1) ** (l1 - l2 - m3) / sqrt(2 * l3 + 1) * _cg(l1, l2, l3, m1, m2, -m3)
            return w

        def _A(l):
            A = np.zeros((2 * l + 1, 2 * l + 1), dtype=complex)
            A[l, l] = 1.0
            for m in range(1, l + 1):
                A[l + m, l + m] = (-1) ** m / sqrt(2)
                A[l + m, l - m] = 1.0 / sqrt(2)
                A[l - m, l - m] = 1j / sqrt(2)
                A[l - m, l + m] = -1j * (-1) ** m / sqrt(2)
            return A

        def real_w3j(l1, l2, l3):
            wc = _w3j_complex(l1, l2, l3).astype(complex)
            wr = np.einsum('abc,ma,nb,oc->mno', wc, _A(l1).conj(), _A(l2).conj(), _A(l3).conj())
            i = int(np.argmax(np.abs(wr)))
            ph = wr.flat[i] / abs(wr.flat[i])
            wr = wr / ph
            assert np.abs(wr.imag).max() < 1e-10
            return np.real(wr).astype(np.float32)
        _W3J = {}
        for _mo, _lo in RS:
            for _mi, _li in RS:
                for _lf in range(abs(_lo - _li), _lo + _li + 1):
                    if (_lo, _lf, _li) not in _W3J:
                        _W3J[_lo, _lf, _li] = jnp.asarray(real_w3j(_lo, _lf, _li))
        _NORM = []
        for _mo, _lo in RS:
            _num = sum((mi * (2 * min(_lo, li) + 1) for mi, li in RS))
            _NORM.append(sqrt(4.0 * pi) * sqrt(2.0 * _lo + 1.0) / sqrt(_num))
        _F_OFFS = [0] + list(np.cumsum([mi * (2 * li + 1) for mi, li in RS]))

        def spherical_harmonics(rel_vec):
            r = rel_vec / jnp.linalg.norm(rel_vec, axis=-1, keepdims=True)
            x, y, z = (r[:, 0], r[:, 1], r[:, 2])
            y0 = jnp.full_like(x, 0.5 / sqrt(pi))[:, None]
            c1 = sqrt(3.0 / (4.0 * pi))
            y1 = c1 * jnp.stack([y, z, x], axis=-1)
            c2a = 0.5 * sqrt(15.0 / pi)
            c2b = 0.25 * sqrt(5.0 / pi)
            c2c = 0.25 * sqrt(15.0 / pi)
            y2 = jnp.stack([c2a * x * y, c2a * y * z, c2b * (3.0 * z * z - 1.0), c2a * x * z, c2c * (x * x - y * y)], axis=-1)
            return jnp.concatenate([y0, y1, y2], axis=-1)
        key = jax.random.key(seed)
        ks = jax.random.split(key, 6)
        features = jax.random.normal(ks[0], (N_NODES, FEAT_DIM), dtype=jnp.float32)
        abs_distances = jax.random.uniform(ks[1], (N_EDGES,), dtype=jnp.float32, minval=0.1, maxval=1.0)
        rel_vec = jax.random.normal(ks[2], (N_EDGES, 3), dtype=jnp.float32)
        edge_index = jax.random.randint(ks[3], (2, N_EDGES), 0, N_NODES, dtype=jnp.int32)
        w1 = jax.random.normal(ks[4], (1, HIDDEN), dtype=jnp.float32)
        b1 = jnp.zeros((HIDDEN,), jnp.float32)
        w2 = jax.random.normal(ks[5], (HIDDEN, R_DIM), dtype=jnp.float32) / sqrt(HIDDEN)
        b2 = jnp.zeros((R_DIM,), jnp.float32)
        return {'features': features, 'abs_distances': abs_distances, 'rel_vec': rel_vec, 'edge_index': edge_index, 'w1': w1, 'b1': b1, 'w2': w2, 'b2': b2}
    _L0_gnn_all = _L0_gnn_setup()
    _L0_gnn_in = {k: v for k, v in _L0_gnn_all.items() if k in ('w1', 'b1', 'w2', 'b2')}
    del _L0_gnn_all

    def _L1_gnn_setup():
        import jax, jax.numpy as jnp
        import numpy as np
        N_NODES = 50000
        DEG = 16
        N_HEAD = 4
        F_IN = 32
        F_OUT = 32
        key = jax.random.key(seed)
        k_h, k_w, k_fw, k_fb = jax.random.split(key, 4)
        h = jax.random.normal(k_h, (N_NODES, F_IN), dtype=jnp.float32)
        src = jnp.repeat(jnp.arange(N_NODES, dtype=jnp.int64), DEG)
        offs = (jnp.arange(DEG, dtype=jnp.int64) + 1) * 97
        dst = (src.reshape(N_NODES, DEG) + offs[None, :]).reshape(-1) % N_NODES
        edge_index = jnp.stack([src, dst], axis=0)
        gain = 1.414
        bound_w = gain * np.sqrt(6.0 / (F_IN + F_OUT))
        w = jax.random.uniform(k_w, (N_HEAD, F_IN, F_OUT), jnp.float32, -bound_w, bound_w)
        bound_fc = np.sqrt(1.0 / (2 * F_OUT))
        fc_w = jax.random.uniform(k_fw, (1, 2 * F_OUT), jnp.float32, -bound_fc, bound_fc)
        fc_b = jax.random.uniform(k_fb, (1,), jnp.float32, -bound_fc, bound_fc)
        bias = jnp.zeros((F_OUT,), jnp.float32)
        return {'h': h, 'edge_index': edge_index, 'w': w, 'fc_w': fc_w, 'fc_b': fc_b, 'bias': bias}
    _L1_gnn_all = _L1_gnn_setup()
    _L1_gnn_in = {k: v for k, v in _L1_gnn_all.items() if k in ('w', 'fc_w', 'fc_b', 'bias')}
    del _L1_gnn_all
    return {'x': x, 'src': src, 'dst': dst, 'edge_attr_3': edge_attr_3, 'edge_weight': edge_weight, 'L0_gnn_w1': _L0_gnn_in['w1'], 'L0_gnn_b1': _L0_gnn_in['b1'], 'L0_gnn_w2': _L0_gnn_in['w2'], 'L0_gnn_b2': _L0_gnn_in['b2'], 'L1_gnn_w': _L1_gnn_in['w'], 'L1_gnn_fc_w': _L1_gnn_in['fc_w'], 'L1_gnn_fc_b': _L1_gnn_in['fc_b'], 'L1_gnn_bias': _L1_gnn_in['bias']}

def reference(x, src, dst, edge_attr_3, edge_weight, L0_gnn_w1, L0_gnn_b1, L0_gnn_w2, L0_gnn_b2, L1_gnn_w, L1_gnn_fc_w, L1_gnn_fc_b, L1_gnn_bias):
    import jax
    import jax.numpy as jnp

    def _L0_gnn_ref(features, abs_distances, rel_vec, edge_index, w1, b1, w2, b2):
        import jax, jax.numpy as jnp
        import numpy as np
        from math import factorial, pi, sqrt
        MUL = 8
        RS = [(MUL, 0), (MUL, 1)]
        N_NODES = 20000
        N_EDGES = 10000
        FEAT_DIM = sum((m * (2 * l + 1) for m, l in RS))
        R_DIM = sum((mo * mi * (2 * min(lo, li) + 1) for mo, lo in RS for mi, li in RS))
        HIDDEN = 64

        def _cg(j1, j2, j3, m1, m2, m3):
            if m1 + m2 != m3:
                return 0.0
            f = factorial
            pre = sqrt((2 * j3 + 1) * f(j3 + j1 - j2) * f(j3 - j1 + j2) * f(j1 + j2 - j3) / f(j1 + j2 + j3 + 1))
            pre *= sqrt(f(j3 + m3) * f(j3 - m3) * f(j1 - m1) * f(j1 + m1) * f(j2 - m2) * f(j2 + m2))
            kmin = max(0, j2 - j3 - m1, j1 - j3 + m2)
            kmax = min(j1 + j2 - j3, j1 - m1, j2 + m2)
            s = 0.0
            for k in range(kmin, kmax + 1):
                s += (-1) ** k / (f(k) * f(j1 + j2 - j3 - k) * f(j1 - m1 - k) * f(j2 + m2 - k) * f(j3 - j2 + m1 + k) * f(j3 - j1 - m2 + k))
            return pre * s

        def _w3j_complex(l1, l2, l3):
            w = np.zeros((2 * l1 + 1, 2 * l2 + 1, 2 * l3 + 1))
            for m1 in range(-l1, l1 + 1):
                for m2 in range(-l2, l2 + 1):
                    m3 = -(m1 + m2)
                    if abs(m3) <= l3:
                        w[m1 + l1, m2 + l2, m3 + l3] = (-1) ** (l1 - l2 - m3) / sqrt(2 * l3 + 1) * _cg(l1, l2, l3, m1, m2, -m3)
            return w

        def _A(l):
            A = np.zeros((2 * l + 1, 2 * l + 1), dtype=complex)
            A[l, l] = 1.0
            for m in range(1, l + 1):
                A[l + m, l + m] = (-1) ** m / sqrt(2)
                A[l + m, l - m] = 1.0 / sqrt(2)
                A[l - m, l - m] = 1j / sqrt(2)
                A[l - m, l + m] = -1j * (-1) ** m / sqrt(2)
            return A

        def real_w3j(l1, l2, l3):
            wc = _w3j_complex(l1, l2, l3).astype(complex)
            wr = np.einsum('abc,ma,nb,oc->mno', wc, _A(l1).conj(), _A(l2).conj(), _A(l3).conj())
            i = int(np.argmax(np.abs(wr)))
            ph = wr.flat[i] / abs(wr.flat[i])
            wr = wr / ph
            assert np.abs(wr.imag).max() < 1e-10
            return np.real(wr).astype(np.float32)
        _W3J = {}
        for _mo, _lo in RS:
            for _mi, _li in RS:
                for _lf in range(abs(_lo - _li), _lo + _li + 1):
                    if (_lo, _lf, _li) not in _W3J:
                        _W3J[_lo, _lf, _li] = jnp.asarray(real_w3j(_lo, _lf, _li))
        _NORM = []
        for _mo, _lo in RS:
            _num = sum((mi * (2 * min(_lo, li) + 1) for mi, li in RS))
            _NORM.append(sqrt(4.0 * pi) * sqrt(2.0 * _lo + 1.0) / sqrt(_num))
        _F_OFFS = [0] + list(np.cumsum([mi * (2 * li + 1) for mi, li in RS]))

        def spherical_harmonics(rel_vec):
            r = rel_vec / jnp.linalg.norm(rel_vec, axis=-1, keepdims=True)
            x, y, z = (r[:, 0], r[:, 1], r[:, 2])
            y0 = jnp.full_like(x, 0.5 / sqrt(pi))[:, None]
            c1 = sqrt(3.0 / (4.0 * pi))
            y1 = c1 * jnp.stack([y, z, x], axis=-1)
            c2a = 0.5 * sqrt(15.0 / pi)
            c2b = 0.25 * sqrt(5.0 / pi)
            c2c = 0.25 * sqrt(15.0 / pi)
            y2 = jnp.stack([c2a * x * y, c2a * y * z, c2b * (3.0 * z * z - 1.0), c2a * x * z, c2c * (x * x - y * y)], axis=-1)
            return jnp.concatenate([y0, y1, y2], axis=-1)
        src, dst = (edge_index[0], edge_index[1])
        R = jax.nn.relu(abs_distances[:, None] @ w1 + b1) @ w2 + b2
        Y = spherical_harmonics(rel_vec)
        Fj = features[src]
        E = Fj.shape[0]
        msg_blocks = []
        r_off = 0
        for i, (mo, lo) in enumerate(RS):
            acc = jnp.zeros((E, mo, 2 * lo + 1), dtype=features.dtype)
            for j, (mi, li) in enumerate(RS):
                n_lf = 2 * min(lo, li) + 1
                sz = mo * mi * n_lf
                Rb = R[:, r_off:r_off + sz].reshape(E, mo, mi, n_lf)
                r_off += sz
                Fb = Fj[:, _F_OFFS[j]:_F_OFFS[j + 1]].reshape(E, mi, 2 * li + 1)
                for k, lf in enumerate(range(abs(lo - li), lo + li + 1)):
                    C = _W3J[lo, lf, li]
                    Yf = Y[:, lf * lf:(lf + 1) * (lf + 1)]
                    acc = acc + _NORM[i] * jnp.einsum('euv,ef,evi,ofi->euo', Rb[..., k], Yf, Fb, C)
            msg_blocks.append(acc.reshape(E, -1))
        msg = jnp.concatenate(msg_blocks, axis=-1)
        out = jnp.zeros((features.shape[0], msg.shape[1]), dtype=features.dtype)
        out = out.at[dst].add(msg)
        return out

    def _L1_gnn_ref(h, edge_index, w, fc_w, fc_b, bias):
        import jax, jax.numpy as jnp
        import numpy as np
        N_NODES = 50000
        DEG = 16
        N_HEAD = 4
        F_IN = 32
        F_OUT = 32
        n_head, f_in, f_out = w.shape
        n = h.shape[0]
        src, dst = (edge_index[0], edge_index[1])
        hp = jnp.einsum('nf,hfo->hno', h, w)
        w_src = fc_w[0, :f_out]
        w_dst = fc_w[0, f_out:]
        a_src = jnp.einsum('hnf,f->hn', hp, w_src)
        a_dst = jnp.einsum('hnf,f->hn', hp, w_dst)
        e = a_src[:, src] + a_dst[:, dst] + fc_b[0]
        e = jax.nn.leaky_relu(e, negative_slope=0.2)
        seg_max = jax.ops.segment_max(e.T, src, num_segments=n)
        e = jnp.exp(e - seg_max.T[:, src])
        seg_sum = jax.ops.segment_sum(e.T, src, num_segments=n)
        att = e / seg_sum.T[:, src]
        msg = att[:, :, None] * hp[:, dst, :]
        agg = jax.vmap(lambda m: jax.ops.segment_sum(m, src, num_segments=n))(msg)
        out = agg.mean(axis=0) + bias
        return out
    edge_index = jnp.stack([src, dst])
    h = jnp.maximum(_layernorm(x, axis=-1), 0.0)
    x = x + _L0_gnn_ref(h, edge_weight, edge_attr_3, edge_index, L0_gnn_w1, L0_gnn_b1, L0_gnn_w2, L0_gnn_b2)
    h = jnp.maximum(_layernorm(x, axis=-1), 0.0)
    x = x + _L1_gnn_ref(h, edge_index, L1_gnn_w, L1_gnn_fc_w, L1_gnn_fc_b, L1_gnn_bias)
    return x

_drawn_inputs = setup_inputs


def setup_inputs(seed=0):
    import zlib

    import numpy as np

    out = dict(_drawn_inputs(seed))
    spreads = {'L0_gnn_b1': (0.0, 0.33), 'L0_gnn_b2': (0.0, 0.1), 'L1_gnn_bias': (0.0, 0.1)}
    factors = {'L1_gnn_fc_w': 6.459}
    for name, (base, spread) in spreads.items():
        noise = np.random.default_rng([zlib.crc32(name.encode()), seed]).standard_normal(out[name].shape)
        drawn = base * np.exp(spread * noise) if base else spread * noise
        out[name] = jnp.asarray(drawn.astype(out[name].dtype))
    for name, factor in factors.items():
        out[name] = (out[name] * factor).astype(out[name].dtype)
    return out
```

```python
from contextlib import ExitStack
from math import sqrt

import numpy as np

import concourse.bass as bass
from concourse import mybir

P = 128
F32 = mybir.dt.float32
I32 = mybir.dt.int32
ALU = mybir.AluOpType
ACT = mybir.ActivationFunctionType
AX = mybir.AxisListType

NODES = 100000
EDGES = 25000
FEAT = 32
MUL = 8
HIDDEN = 64
HEADS = 4
RADIAL = 6 * MUL * MUL
COLS = -(-EDGES // P)
GROUP = 14
HALF = GROUP // 2
CHUNKS = COLS // GROUP
SLOTS = P * COLS
SORT_COLS = 256
SORT_BITS = 15
BIG = 1.0e30
EPS = 1e-5
RECORD = 8
DMA = 16
GATHERED = DMA * GROUP

W16 = 2 * MUL
NA = W16 * W16
NB = W16 * MUL
K_00 = 1 / 4
K_01 = 1 / 4
K_10 = sqrt(3 / 32)
K_110 = 1 / (4 * sqrt(2))
K_111 = sqrt(3) / 8
K_112R = 3 / 8
K_112I = -1 / 8

FILL_P = 80
FILL_ROWS = 125
FILLS = NODES // FILL_P // FILL_ROWS


def sort_plan():
    col_bits = SORT_COLS.bit_length() - 1
    plan, steps, half, turns = [], 4, 0, []
    for k in range(1, SORT_BITS + 1):
        plan.append(("flip", k))
        steps += len(flips_of(k))

        def turn():
            plan.append(("turn", None))
            turns.append((steps, half))
            return steps + 1

        def compare(distance):
            plan.append(("compare", distance))
            return steps + 7, 1 - half

        if k > col_bits:
            steps = turn()
            for j in range(k - 1, col_bits - 1, -1):
                steps, half = compare(1 << (j - col_bits))
            steps = turn()
        for j in range(min(k, col_bits) - 1, -1, -1):
            steps, half = compare(1 << j)
    return plan, steps, half, turns


def flips_of(k, keys=None):
    if keys is None:
        return [None] * (2 if 1 < k <= 8 else 1)
    if k == 1:
        return [(keys.rearrange("p (a u b) -> p a u b", u=2, b=2)[:, :, 1], None)]
    if k < 8:
        v = keys.rearrange("p (a u v b) -> p a u v b", u=2, v=2, b=1 << (k - 1))
        return [(v[:, :, 0, 1], None), (v[:, :, 1, 0], None)]
    if k == 8:
        return [(keys[:, 0:P], 0), (keys[:, P:], 1)]
    return [(keys, k - 7)]


SORT_PLAN, SORT_STEPS, SORT_END, SORT_TURNS = sort_plan()


def graph_layers(nc, x, src, dst, attr, ew, w1, b1, w2, b2, w, fcw, fcb, bias, eye, posn, flips, out):
    assert CHUNKS * GROUP == COLS and CHUNKS % 2 == 0 and FILLS % 2 == 0 and FILLS < CHUNKS
    with ExitStack() as ctx:
        def sb(name, shape, dt=F32):
            return ctx.enter_context(nc.sbuf_tensor(name, shape, dt))

        def sem(name):
            return ctx.enter_context(nc.semaphore(name))

        nodes1 = nc.dram_tensor("nodes1", [NODES + SLOTS, FEAT], F32).ap()
        key_pad = nc.dram_tensor("key_pad", [P * SORT_COLS + 1], F32).ap()
        pay_dram = nc.dram_tensor("pay_dram", [P * SORT_COLS], F32).ap()
        records = nc.dram_tensor("records", [SLOTS, RECORD], F32).ap()
        dist_row = nc.dram_tensor("dist_row", [COLS, P], F32).ap()

        ident = sb("ident", [P, P])
        pos = sb("pos", [P, COLS])
        flip = sb("flip", [P, 9])
        eps = sb("eps", [P, 1])
        ones32 = sb("ones32", [P, FEAT])
        w1c = sb("w1c", [HIDDEN, 1])
        b1c = sb("b1c", [HIDDEN, 1])
        w2raw = sb("w2raw", [HIDDEN + 1, RADIAL])
        w2p = sb("w2p", [HIDDEN + 1, RADIAL])
        w2t = sb("w2t", [HIDDEN + 1, MUL, MUL])
        wrep = sb("wrep", [P, HEADS, FEAT])
        wmul = sb("wmul", [P, 2, HEADS, FEAT])
        fcw_b = sb("fcw_b", [P, 2 * FEAT])
        fcb_b = sb("fcb_b", [P, 1])
        bias_b = sb("bias_b", [P, FEAT])
        u_all = sb("u_all", [P, 2, HEADS])
        ublk = sb("ublk", [P, 2, 4 * HEADS])
        wstk_raw = sb("wstk_raw", [P, FEAT])
        wstk = sb("wstk", [P, FEAT])

        src_i = sb("src_i", [P, COLS], I32)
        dst_ext_i = sb("dst_ext_i", [P, COLS + 2], I32)
        dist = sb("dist", [P, COLS])
        vec = sb("vec", [P, COLS, 3])
        vsq = sb("vsq", [P, COLS, 3])
        vn = sb("vn", [P, 3, COLS])
        src_f = sb("src_f", [P, COLS])
        dst_f = sb("dst_f", [P, COLS])
        dst_ext = sb("dst_ext", [P, COLS + 2])
        idx_src = sb("idx_src", [P, COLS], I32)
        idx_dst = sb("idx_dst", [P, COLS], I32)
        idx_tmp = sb("idx_tmp", [P, COLS])
        r5 = sb("r5", [P, COLS, 5])
        same = sb("same", [P, COLS])
        last = sb("last", [P, COLS])
        opened = sb("opened", [P, COLS])
        distT = sb("distT", [P, 2, P])

        stage = sb("stage", [P, 2, 2, GROUP], I32)
        rowring = sb("rowring", [P, 2, GROUP, FEAT])

        def carver(arena):
            at = [0]

            def carve(shape, parts=P):
                n = int(np.prod(shape))
                names = "abcd"[:len(shape)]
                flat = arena[0:parts, at[0]:at[0] + n]
                at[0] += n
                return flat.rearrange(f"p ({' '.join(names)}) -> p {' '.join(names)}",
                                      **dict(zip(names, shape)))
            return carve

        arena0 = sb("arena0", [P, 7504])
        carve = carver(arena0)
        xring = carve([2, GROUP, FEAT])
        xc = carve([2, GROUP, FEAT])
        sq = carve([2, GROUP, FEAT])
        h0 = carve([2, GROUP, FEAT])
        z = carve([2, GROUP, W16])
        V = carve([2, GROUP, W16 * 3]).rearrange("p b t (w o) -> p b t w o", o=3)
        f1e = carve([2, GROUP, MUL * 5]).rearrange("p b t (v o) -> p b t v o", o=5)
        crs = carve([3, GROUP, MUL * 3]).rearrange("p b t (v o) -> p b t v o", o=3)
        carve = carver(arena0)
        lring = carve([2, 2 * GROUP, FEAT])
        hT = carve([2, 2 * P])
        E = carve([COLS, HEADS])
        soft = carve([4, COLS, HEADS])
        wT = carve([2, 4 * P])

        arena1 = sb("arena1", [P, 4 * GROUP * P])
        carve = carver(arena1)
        hidden = carve([2, GROUP * P], HIDDEN + 1)
        distb = carve([2, GROUP * P], HIDDEN)
        carve = carver(arena1)
        lxc = carve([2 * GROUP, FEAT])
        lsq = carve([2 * GROUP, FEAT])
        lh = carve([2, 2 * GROUP, FEAT])
        weighted = carve([2, GROUP, P])

        prods = sb("prods", [P, 2 * HALF * (NA + 3 * NB)])
        prodA = prods[:, 0:2 * HALF * NA].rearrange("p (h t w u) -> p h t w u", h=2, t=HALF, w=W16)
        prodB = prods[:, 2 * HALF * NA:].rearrange("p (h t w u) -> p h t w u", h=2, t=HALF, w=W16)
        vsq = prods[:, 0:3 * COLS].rearrange("p (c o) -> p c o", o=3)
        vn = prods[:, 3 * COLS:6 * COLS].rearrange("p (k c) -> p k c", k=3)
        record = prods[:, 0:RECORD * COLS].rearrange("p (c k) -> p c k", k=RECORD)
        fill = prods[0:FILL_P, 0:2 * FILL_ROWS * FEAT].rearrange("p (b n) -> p b n", b=2)

        mean = sb("mean", [P, 2, 2 * GROUP])
        lsum = sb("lsum", [P, 2, 2 * GROUP])
        vsum = sb("vsum", [P, 2, 2 * GROUP])
        std = sb("std", [P, 2, 2 * GROUP])
        rstd = sb("rstd", [P, 2, 2 * GROUP])
        qr = sb("qr", [P, 2, HALF, MUL, 3])
        msg = sb("msg", [P, COLS, FEAT])
        carry = sb("carry", [P, FEAT])
        openrep = sb("openrep", [P, FEAT])
        openT = sb("openT", [FEAT, P])
        chain = sb("chain", [FEAT, P + 1])

        pairs = sb("pairs", [P, 2, 2, SORT_COLS])
        skey, spay = pairs[:, :, 0], pairs[:, :, 1]
        gt = sb("gt", [P, P])
        dpay = sb("dpay", [P, P])
        key_ext = sb("key_ext", [P, COLS + 2])
        pay = sb("pay", [P, COLS])
        idx_dst_s = sb("idx_dst_s", [P, COLS], I32)
        idx_out = sb("idx_out", [P, COLS], I32)
        more = sb("more", [P, COLS])
        negopen = sb("negopen", [P, 2, COLS])
        before = sb("before", [1, 1])
        unsorted = sb("unsorted", [P, 1])
        unsorted_1 = sb("unsorted_1", [1, 1])
        flag = sb("flag", [1, 1], I32)
        record_ring = sb("record_ring", [P, 2, GROUP, RECORD])

        xsb = sb("xsb", [P, COLS, FEAT])
        hd = msg
        lgt = sb("lgt", [P, GROUP * HEADS])
        negs = sb("negs", [P, 2, COLS])
        openR = sb("openR", [P, COLS])
        ends = sb("ends", [P, 4, HEADS])
        endT = sb("endT", [HEADS, 2, P])
        ladder = sb("ladder", [HEADS, 2, P + 1])
        join = sb("join", [P, 2, HEADS])

        psM = ctx.enter_context(nc.psum_tensor("psM", [P, 4, 512], F32))
        psR = ctx.enter_context(nc.psum_tensor("psR", [P, 2, 512], F32))
        psT = ctx.enter_context(nc.psum_tensor("psT", [P, 512], F32))
        psX = ctx.enter_context(nc.psum_tensor("psX", [P, 512], F32))

        prefilled, edges_in, weights_in, copied = map(sem, ("prefilled", "edges_in", "weights_in", "copied"))
        floats, edge_vals = map(sem, ("floats", "edge_vals"))
        before_out, r_record_out, r_record_there = map(sem, ("before_out", "r_record_out", "r_record_there"))
        compared, flag_turned, flagged = map(sem, ("compared", "flag_turned", "flagged"))
        r_sorting, r_sort_turned, r_built, r_stored, r_order_in, r_indexed, r_staged, r_unpacked = map(
            sem, ("r_sorting", "r_sort_turned", "r_built", "r_stored", "r_order_in", "r_indexed", "r_staged",
                  "r_unpacked"))
        r_in = [sem("r_in0"), sem("r_in1")]
        prep, acts = sem("prep"), sem("acts")
        vsq_done, vnorm, vstd, idx_src_ready = map(sem, ("vsq_done", "vnorm", "vstd", "idx_src_ready"))
        w2_ready, lweights = sem("w2_ready"), sem("lweights")
        dist_turned, dist_copied, dist_stored = map(sem, ("dist_turned", "dist_copied", "dist_stored"))
        pool_turn, staged = sem("pool_turn"), sem("staged")
        x_in = [sem("x_in0"), sem("x_in1")]
        summed, meaned, centered, squared, varsummed, stded, rstded, normed = map(
            sem, ("summed", "meaned", "centered", "squared", "varsummed", "stded", "rstded", "normed"))
        spread, dotp, dotted, crossed, vectored = map(sem, ("spread", "dotp", "dotted", "crossed", "vectored"))
        dist_bc = [sem("dist_bc0"), sem("dist_bc1")]
        hid_ready, radial_ready, prod_done, preadded, reduced, q_done, posted = map(
            sem, ("hid_ready", "radial_ready", "prod_done", "preadded", "reduced", "q_done", "posted"))
        scanned, ends_turned, chained, carried, fixed = map(
            sem, ("scanned", "ends_turned", "chained", "carried", "fixed"))
        act_turn, rows_ready = sem("act_turn"), sem("rows_ready")
        rows_out = [sem("rows_out0"), sem("rows_out1")]
        sorting, sort_turned, sorted_out, srcorder_in, idx_ready = map(
            sem, ("sorting", "sort_turned", "sorted_out", "srcorder_in", "idx_ready"))
        l_in = [sem("l_in0"), sem("l_in1")]
        l_summed, l_meaned, l_centered, l_squared, l_varsummed, l_stded, l_rstded, l_normed = map(
            sem, ("l_summed", "l_meaned", "l_centered", "l_squared", "l_varsummed", "l_stded", "l_rstded",
                  "l_normed"))
        l_saved, l_based, l_turned, l_hT, l_logits, l_biased, l_logged = map(
            sem, ("l_saved", "l_based", "l_turned", "l_hT", "l_logits", "l_biased", "l_logged"))
        fill_in = [sem("fill_in0"), sem("fill_in1")]
        fill_added = sem("fill_added")
        fill_out = [sem("fill_out0"), sem("fill_out1")]
        s_turned, s_exp, joining, shifted = map(sem, ("s_turned", "s_exp", "joining", "shifted"))
        weighed, m_turned, m_wT, m_mixed, m_out = map(sem, ("weighed", "m_turned", "m_wT", "m_mixed", "m_out"))
        out_rows = sem("out_rows")
        out_done = [sem("out_done0"), sem("out_done1")]

        TABLE_PART = 800 // (CHUNKS // 2 - 2)
        last_rows = (P - 1) * COLS
        tail = EDGES - last_rows

        def windows(a, start, n):
            return bass.AP(tensor=a.tensor, offset=start, ap=[[COLS, n], [1, COLS + 2]])

        def chunk_cols(n):
            return bass.ds(n * GROUP, GROUP)

        class Steps:

            def __init__(self, eng, s, base=0):
                self.eng, self.s, self.n = eng, s, base

            def do(self, ins):
                ins.then_inc(self.s, 1)
                self.n += 1

            def settle(self):
                self.eng.wait_ge(self.s, self.n)

            def link(self, ins):
                self.do(ins)
                self.settle()

        def bc(ap, axis, n):
            a = ap.unsqueeze(axis)
            shape = list(a.shape)
            shape[axis] = n
            return a.broadcast_to(shape)

        block = ctx.enter_context(nc.Block())

        @block.sync
        def _(sp):
            sp.wait_ge(prefilled, 7)
            for tile, a in ((src_i, src), (dist, ew)):
                whole = a[0:last_rows].rearrange("(p c) -> p c", c=COLS)
                sp.dma_start(tile[0:112, :], whole[0:112]).then_inc(edges_in, DMA)
                sp.dma_start(tile[112:P - 1, :], whole[112:P - 1]).then_inc(edges_in, DMA)
                sp.dma_start(tile[P - 1:P, 0:tail], a[last_rows:EDGES].rearrange("(p c) -> p c", p=1)
                             ).then_inc(edges_in, DMA)
            sp.dma_start(dst_ext_i[0:1, 1:], dst[0:COLS + 1].rearrange("(p c) -> p c", p=1)).then_inc(edges_in, DMA)
            sp.dma_start(dst_ext_i[1:113], windows(dst, COLS - 1, 112)).then_inc(edges_in, DMA)
            sp.dma_start(dst_ext_i[113:P - 1], windows(dst, 113 * COLS - 1, P - 114)).then_inc(edges_in, DMA)
            sp.dma_start(dst_ext_i[P - 1:P, 0:tail + 1], dst[last_rows - 1:EDGES].rearrange("(p c) -> p c", p=1)
                         ).then_inc(edges_in, DMA)
            whole = attr[0:last_rows].rearrange("(p c) o -> p c o", c=COLS)
            sp.dma_start(vec[0:112], whole[0:112]).then_inc(edges_in, DMA)
            sp.dma_start(vec[112:P - 1], whole[112:P - 1]).then_inc(edges_in, DMA)
            sp.dma_start(vec[P - 1:P, 0:tail], attr[last_rows:EDGES].rearrange("(p c) o -> p c o", p=1)
                         ).then_inc(edges_in, DMA)
            for tile, a in (
                (ident[:], eye), (pos[:], posn), (flip[:], flips),
                (w1c[:], w1.rearrange("one h -> h one")), (b1c[:], b1.rearrange("(h one) -> h one", one=1)),
                (w2raw[0:HIDDEN], w2), (w2raw[HIDDEN:HIDDEN + 1], b2.rearrange("(one r) -> one r", one=1)),
                (fcw_b[:], fcw[0].partition_broadcast(P)), (fcb_b[:], fcb.partition_broadcast(P)),
                (bias_b[:], bias.partition_broadcast(P)), (wstk_raw[:], w.rearrange("h f o -> (h f) o")),
                *((wrep[32 * t:32 * t + 32], w.rearrange("h f o -> f h o")) for t in range(4)),
            ):
                sp.dma_start(tile, a).then_inc(weights_in, DMA)
            sp.wait_ge(edge_vals, 1)
            sp.dma_start(key_pad[0:1].rearrange("(a b) -> a b", a=1), before[:]).then_inc(before_out, DMA)
            sp.wait_ge(before_out, DMA)

            def sorted_pairs(stored, loaded, ext, payload):
                sp.dma_start(key_pad[1:1 + P * SORT_COLS].rearrange("(p c) -> p c", c=SORT_COLS),
                             skey[:, SORT_END]).then_inc(stored, DMA)
                sp.dma_start(pay_dram.rearrange("(p c) -> p c", c=SORT_COLS), spay[:, SORT_END]
                             ).then_inc(stored, DMA)
                sp.wait_ge(stored, 2 * DMA)
                sp.dma_start(ext, windows(key_pad, 0, P)).then_inc(loaded, DMA)
                sp.dma_start(payload, pay_dram[0:SLOTS].rearrange("(p c) -> p c", c=COLS)).then_inc(loaded, DMA)
                sp.wait_ge(loaded, 2 * DMA)

            sp.wait_ge(flagged, 1)
            with sp.If(sp.value_load(flag[:], min_val=0, max_val=1) > 0):
                sp.wait_ge(r_built, 1)
                sp.dma_start(records.rearrange("(p c) k -> p c k", c=COLS), record).then_inc(r_record_out, DMA)
                sp.wait_ge(r_sorting, SORT_STEPS)
                sorted_pairs(r_stored, r_order_in, dst_ext[:], pay[:])
                sp.wait_ge(r_record_out, DMA)
                sp.sem_inc(r_record_there, 1)

            sp.wait_ge(dist_copied, 1)
            for j in range(2):
                sp.dma_start(dist_row[98 * j:98 * j + 98], distT[0:98, j]).then_inc(dist_stored, DMA)
            sp.wait_ge(dist_stored, 2 * DMA)

            def dist_load(n, b):
                if not isinstance(n, int) or n >= 2:
                    sp.wait_ge(hid_ready, n - 1)
                sp.dma_start(distb[:, b], dist_row[chunk_cols(n)].rearrange("c p -> (c p)")
                             .partition_broadcast(HIDDEN)).then_inc(dist_bc[b], DMA)

            dist_load(0, 0)
            dist_load(1, 1)
            table = nodes1[0:NODES].rearrange("(a b) d -> a (b d)", a=800)
            nodes0 = x.rearrange("(a b) d -> a (b d)", a=800)
            with sp.Fori(1, CHUNKS // 2 - 1) as i:
                dist_load(2 * i, 0)
                dist_load(2 * i + 1, 1)
                part = bass.ds((i - 1) * TABLE_PART, TABLE_PART)
                sp.dma_start(table[part], nodes0[part]).then_inc(copied, DMA)
            dist_load(CHUNKS - 2, 0)
            dist_load(CHUNKS - 1, 1)
            sp.dma_start(nodes1[NODES:NODES + SLOTS].rearrange("(a b) d -> a (b d)", a=784),
                         x[0:SLOTS].rearrange("(a b) d -> a (b d)", a=784)).then_inc(copied, DMA)

            sp.wait_ge(sorting, SORT_STEPS)
            sorted_pairs(sorted_out, srcorder_in, key_ext[:], pay[:])

            rows_in = nodes1[0:NODES].rearrange("(p r) d -> p (r d)", p=FILL_P)
            rows_to = out.rearrange("(p r) d -> p (r d)", p=FILL_P)
            width = FILL_ROWS * FEAT

            def fill_load(m, b):
                sp.dma_start(fill[:, b], rows_in[:, bass.ds(m * width, width)]).then_inc(fill_in[b], DMA)

            def fill_store(m, b):
                sp.wait_ge(fill_added, m + 1)
                sp.dma_start(rows_to[:, bass.ds(m * width, width)], fill[:, b]).then_inc(fill_out[b], DMA)

            for b in range(2):
                sp.wait_ge(rows_out[b], GATHERED * CHUNKS // 2)
            sp.wait_ge(posted, 2 * CHUNKS)
            sp.wait_ge(reduced, 2 * CHUNKS)
            fill_load(0, 0)
            fill_load(1, 1)
            with sp.Fori(0, FILLS // 2 - 1) as i:
                for b in range(2):
                    fill_store(2 * i + b, b)
                    sp.wait_ge(fill_out[b], DMA * (i + 1))
                    fill_load(2 * i + 2 + b, b)
            for b in range(2):
                fill_store(FILLS - 2 + b, b)
            for b in range(2):
                sp.wait_ge(fill_out[b], DMA * FILLS // 2)
                sp.wait_ge(out_done[b], GATHERED * CHUNKS // 2)

        @block.gpsimd
        def _(pool):
            pool.memset(src_i[:], NODES).then_inc(prefilled, 1)
            pool.memset(dst_ext_i[:], NODES).then_inc(prefilled, 1)
            pool.memset(dist[:], 0.0).then_inc(prefilled, 1)
            pool.memset(vec[:], 1.0).then_inc(prefilled, 1)
            pool.memset(eps[:], EPS).then_inc(prefilled, 1)
            pool.wait_ge(prefilled, 5)
            pool.memset(hidden[HIDDEN:HIDDEN + 1], 1.0).then_inc(prefilled, 1)
            pool.wait_ge(prefilled, 6)
            pool.memset(dst_ext_i[0:1, 0:1], -1).then_inc(prefilled, 1)
            pool.memset(before[:], -1.0).then_inc(edge_vals, 1)
            bound = pool.to_reg(NODES - 1)
            count = [0]

            def stages(n, base, *copies):
                for k, (b, which, idx) in enumerate(copies):
                    pool.tensor_copy(stage[:, b, which], idx[:, chunk_cols(n)]).then_inc(staged, 1)
                pool.wait_ge(staged, base + len(copies) * (n + 1))
                pool.sem_inc(pool_turn, 1)

            pool.wait_ge(flagged, 1)
            with pool.If(pool.value_load(flag[:], min_val=0, max_val=1) > 0):
                pool.wait_ge(r_indexed, 1)
                pool.wait_ge(r_record_there, 1)

                def gather_records(n, b, rounds):
                    if not isinstance(n, int) or n >= 2:
                        pool.wait_ge(r_in[b], GATHERED * rounds)
                        pool.wait_ge(r_unpacked, n - 1)
                        pool.sem_inc(pool_turn, 1)
                    pool.tensor_copy(stage[:, b, 0], idx_out[:, chunk_cols(n)]).then_inc(r_staged, 1)
                    pool.wait_ge(r_staged, n + 1)
                    pool.sem_inc(pool_turn, 1)
                    for t in range(GROUP):
                        pool.indirect_dma_start(record_ring[:, b, t], None, records,
                                                bass.IndirectOffsetOnAxis(ap=stage[:, b, 0, t:t + 1], axis=0)
                                                ).then_inc(r_in[b], DMA)

                gather_records(0, 0, 0)
                gather_records(1, 1, 0)
                with pool.Fori(1, CHUNKS // 2) as i:
                    gather_records(2 * i, 0, i)
                    gather_records(2 * i + 1, 1, i)
                for b in range(2):
                    pool.wait_ge(r_in[b], GATHERED * CHUNKS // 2)

            pool.wait_ge(idx_src_ready, 1)

            def gather_x(n, b, rounds):
                if not isinstance(n, int) or n >= 2:
                    pool.wait_ge(x_in[b], GATHERED * rounds)
                    pool.wait_ge(centered, n - 1)
                pool.sem_inc(pool_turn, 1)
                stages(n, 0, (b, 0, idx_src))
                for t in range(GROUP):
                    pool.indirect_dma_start(xring[:, b, t], None, x,
                                            bass.IndirectOffsetOnAxis(ap=stage[:, b, 0, t:t + 1], axis=0)
                                            ).then_inc(x_in[b], DMA)

            gather_x(0, 0, 0)
            gather_x(1, 1, 0)
            with pool.Fori(1, CHUNKS // 2) as i:
                gather_x(2 * i, 0, i)
                gather_x(2 * i + 1, 1, i)

            pool.wait_ge(copied, (CHUNKS // 2 - 1) * DMA)
            for b in range(2):
                pool.wait_ge(x_in[b], GATHERED * CHUNKS // 2)
            pool.wait_ge(idx_ready, 1)

            def add_rows(n, b):
                stages(n, CHUNKS, (b, 0, idx_dst))
                pool.wait_ge(rows_ready, n + 1)
                pool.sem_inc(pool_turn, 1)
                for t in range(GROUP):
                    pool.indirect_dma_start(nodes1, bass.IndirectOffsetOnAxis(ap=stage[:, b, 0, t:t + 1], axis=0),
                                            rowring[:, b, t], None, compute_op=ALU.add).then_inc(rows_out[b], DMA)

            def add_rows_again(n, b, rounds):
                pool.wait_ge(rows_out[b], GATHERED * rounds)
                pool.sem_inc(pool_turn, 1)
                add_rows(n, b)

            add_rows(0, 0)
            add_rows(1, 1)
            with pool.Fori(1, CHUNKS // 2) as i:
                add_rows_again(2 * i, 0, i)
                add_rows_again(2 * i + 1, 1, i)

            for b in range(2):
                pool.wait_ge(rows_out[b], GATHERED * CHUNKS // 2)
            pool.wait_ge(idx_ready, 3)
            pool.wait_ge(posted, 2 * CHUNKS)
            pool.wait_ge(spread, CHUNKS)

            def gather_l(n, b, rounds):
                if not isinstance(n, int) or n >= 2:
                    pool.wait_ge(l_in[b], 2 * GATHERED * rounds)
                    pool.wait_ge(l_centered, n - 1)
                    pool.wait_ge(l_based, n - 1)
                pool.sem_inc(pool_turn, 1)
                stages(n, 2 * CHUNKS, (b, 0, idx_src), (b, 1, idx_dst_s))
                for k in range(2):
                    for t in range(GROUP):
                        pool.indirect_dma_start(lring[:, b, k * GROUP + t], None, nodes1,
                                                bass.IndirectOffsetOnAxis(ap=stage[:, b, k, t:t + 1], axis=0)
                                                ).then_inc(l_in[b], DMA)

            gather_l(0, 0, 0)
            gather_l(1, 1, 0)
            with pool.Fori(1, CHUNKS // 2) as i:
                gather_l(2 * i, 0, i)
                gather_l(2 * i + 1, 1, i)

            for b in range(2):
                pool.wait_ge(l_in[b], GATHERED * CHUNKS)
                pool.wait_ge(fill_out[b], DMA * FILLS // 2)
            pool.wait_ge(idx_ready, 4)

            def put_rows(n, b):
                stages(n, 4 * CHUNKS, (b, 0, idx_out))
                pool.wait_ge(out_rows, n + 1)
                pool.sem_inc(pool_turn, 1)
                for t in range(GROUP):
                    pool.indirect_dma_start(out, bass.IndirectOffsetOnAxis(ap=stage[:, b, 0, t:t + 1], axis=0),
                                            rowring[:, b, t], None, bounds_check=bound, oob_is_err=False
                                            ).then_inc(out_done[b], DMA)

            def put_rows_again(n, b, rounds):
                pool.wait_ge(out_done[b], GATHERED * rounds)
                pool.sem_inc(pool_turn, 1)
                put_rows(n, b)

            put_rows(0, 0)
            put_rows(1, 1)
            with pool.Fori(1, CHUNKS // 2) as i:
                put_rows_again(2 * i, 0, i)
                put_rows_again(2 * i + 1, 1, i)

        @block.scalar
        def _(act):
            act.wait_ge(idx_src_ready, 1)
            act.activation(vsq, vec[:], ACT.Square).then_inc(vsq_done, 1)
            act.wait_ge(vnorm, 1)
            act.activation(vn[:, 1], vn[:, 0], ACT.Sqrt).then_inc(vstd, 1)
            act.wait_ge(dist_turned, 1)
            act.activation(distT[0:98], psT[0:98, 0:2 * P].rearrange("p (j c) -> p j c", j=2), ACT.Copy
                           ).then_inc(dist_copied, 1)
            act.wait_ge(weights_in, 15 * DMA)
            act.wait_ge(prefilled, 5)

            def layer0_chunk(n, b, rounds):
                late = not isinstance(n, int) or n >= 2
                act.wait_ge(dist_bc[b], DMA * rounds)
                if late:
                    act.wait_ge(radial_ready, (n - 1) * GROUP)
                act.activation(hidden[0:HIDDEN, b], distb[:, b], ACT.Relu, bias=b1c[:], scale=w1c[:]
                               ).then_inc(hid_ready, 1)
                act.wait_ge(centered, n + 1)
                act.activation(sq[:, b], xc[:, b], ACT.Square).then_inc(squared, 1)
                act.wait_ge(varsummed, n + 1)
                act.activation(std[:, b, 0:GROUP], vsum[:, b, 0:GROUP], ACT.Sqrt, bias=eps[:], scale=1.0 / FEAT
                               ).then_inc(stded, 1)
                act.wait_ge(normed, n + 1)
                if late:
                    act.wait_ge(prod_done, (n - 1) * GROUP)
                f1 = h0[:, b, :, MUL:].rearrange("p t (v o) -> p t v o", o=3)
                act.activation(f1e[:, b, :, :, 0:3], f1, ACT.Copy)
                act.activation(f1e[:, b, :, :, 3:5], f1[:, :, :, 0:2], ACT.Copy)
                act.activation(z[:, b, :, 0:MUL], h0[:, b, :, 0:MUL], ACT.Copy)
                act.activation(V[:, b, :, 0:MUL], f1, ACT.Copy).then_inc(spread, 1)

            layer0_chunk(0, 0, 1)
            layer0_chunk(1, 1, 1)
            with act.Fori(1, CHUNKS // 2) as i:
                layer0_chunk(2 * i, 0, i + 1)
                layer0_chunk(2 * i + 1, 1, i + 1)

            act.wait_ge(fixed, 1)

            def rows(n, b, rounds):
                if not isinstance(n, int) or n >= 2:
                    act.wait_ge(rows_out[b], GATHERED * rounds)
                    act.sem_inc(act_turn, 1)
                act.activation(rowring[:, b], msg[:, chunk_cols(n)], ACT.Copy).then_inc(rows_ready, 1)

            rows(0, 0, 0)
            rows(1, 1, 0)
            with act.Fori(1, CHUNKS // 2) as i:
                rows(2 * i, 0, i)
                rows(2 * i + 1, 1, i)

            def layer1_chunk(n, b):
                act.wait_ge(l_centered, n + 1)
                act.activation(lsq, lxc, ACT.Square).then_inc(l_squared, 1)
                act.wait_ge(l_varsummed, n + 1)
                act.activation(std[:, b], vsum[:, b], ACT.Sqrt, bias=eps[:], scale=1.0 / FEAT).then_inc(l_stded, 1)
                act.wait_ge(l_normed, n + 1)
                act.sem_inc(act_turn, 1)
                act.activation(hd[:, chunk_cols(n)], lh[:, b, GROUP:], ACT.Copy).then_inc(l_saved, 1)
                for g in range(4):
                    act.wait_ge(l_turned, n * 4 + g + 1)
                    if g >= 2:
                        act.wait_ge(l_logits, n * 4 + g - 1)
                    elif not isinstance(n, int) or n >= 1:
                        act.wait_ge(l_logits, n * 4 + g - 1)
                    act.activation(hT[:, g % 2], psM[:, g % 2, 0:2 * P], ACT.Copy).then_inc(l_hT, 1)

            layer1_chunk(0, 0)
            layer1_chunk(1, 1)
            with act.Fori(1, CHUNKS // 2) as i:
                layer1_chunk(2 * i, 0)
                layer1_chunk(2 * i + 1, 1)

            act.wait_ge(shifted, 1)
            act.activation(soft[:, 3], soft[:, 2], ACT.Exp).then_inc(s_exp, 1)

            def mix_chunk(n, b):
                for g in range(4):
                    width = P * min(4, GROUP - 4 * g)
                    act.wait_ge(m_turned, n * 4 + g + 1)
                    if g >= 2 or not isinstance(n, int) or n >= 1:
                        act.wait_ge(m_mixed, n * 4 + g - 1)
                    act.activation(wT[:, g % 2, 0:width], psM[:, g, 0:width], ACT.Copy).then_inc(m_wT, 1)
                act.wait_ge(m_mixed, n * 4 + 4)
                act.sem_inc(act_turn, 1)
                act.activation(msg[:, chunk_cols(n)], psR[:, b, 0:GROUP * FEAT].rearrange("p (t f) -> p t f", f=FEAT),
                               ACT.Copy).then_inc(m_out, 1)

            mix_chunk(0, 0)
            mix_chunk(1, 1)
            with act.Fori(1, CHUNKS // 2) as i:
                mix_chunk(2 * i, 0)
                mix_chunk(2 * i + 1, 1)

        @block.tensor
        def _(pe):
            pe.wait_ge(weights_in, 15 * DMA)
            pe.wait_ge(compared, 1)
            pe.transpose(psT[0:1, 0:P], unsorted[:], ident[:]).then_inc(flag_turned, 1)

            def sort_turns(steps_done, turned):
                for steps, half in SORT_TURNS:
                    pe.wait_ge(steps_done, steps)
                    for k in range(4):
                        part = (skey if k < 2 else spay)[:, half, (k % 2) * P:(k % 2 + 1) * P]
                        turn = pe.transpose(psX[:, k * P:(k + 1) * P], part, ident[:])
                    turn.then_inc(turned, 1)

            pe.wait_ge(flagged, 1)
            with pe.If(pe.value_load(flag[:], min_val=0, max_val=1) > 0):
                sort_turns(r_sorting, r_sort_turned)
            pe.wait_ge(idx_src_ready, 1)
            for j in range(2):
                turn = pe.transpose(psT[0:98, j * P:(j + 1) * P], dist[:, 98 * j:98 * j + 98], ident[:])
            turn.then_inc(dist_turned, 1)
            pe.wait_ge(w2_ready, 1)
            pe.wait_ge(prefilled, 6)

            STEPS24 = [24 * t // HALF for t in range(HALF + 1)]

            def radial(n, b, h, t):
                k = h * HALF + t
                if k == 0:
                    pe.wait_ge(hid_ready, n + 1)
                if not isinstance(n, int) or n * GROUP + k >= 4:
                    pe.wait_ge(prod_done, n * GROUP + k - 3)
                pe.matmul(psM[:, (b * GROUP + k) % 4, 0:RADIAL], hidden[:, b, k * P:(k + 1) * P], w2p[:],
                          start=True, stop=True).then_inc(radial_ready, 1)

            def reduce(hh, par, t):
                if t == 0:
                    pe.wait_ge(preadded, hh + 1)
                    if not isinstance(hh, int) or hh >= 2:
                        pe.wait_ge(posted, hh - 1)
                for k in range(STEPS24[t], STEPS24[t + 1]):
                    if k < W16:
                        mm = pe.matmul(psR[:, par, 0:HALF * W16], ident[:], prodA[:, par, :, k],
                                       start=(k == 0), stop=(k == W16 - 1))
                    else:
                        mm = pe.matmul(psR[:, par, HALF * W16:HALF * (W16 + 3 * MUL)], ident[:],
                                       prodB[:, par, :, k - W16], start=(k == W16), stop=(k == 23))
                if t == HALF - 1:
                    mm.then_inc(reduced, 1)

            def layer0_chunk(n, b):
                for h in range(2):
                    for t in range(HALF):
                        radial(n, b, h, t)
                        if not isinstance(n, int) or 2 * n + h >= 1:
                            reduce(2 * n + h - 1, 1 - h, t)

            layer0_chunk(0, 0)
            layer0_chunk(1, 1)
            with pe.Fori(1, CHUNKS // 2) as i:
                layer0_chunk(2 * i, 0)
                layer0_chunk(2 * i + 1, 1)
            for t in range(HALF):
                reduce(2 * CHUNKS - 1, 1, t)

            def join_runs(step):
                pe.wait_ge(scanned, step + 1)
                pe.transpose(psT[0:FEAT, 0:P], msg[:, COLS - 1, :], ident[:])
                pe.transpose(psT[0:FEAT, P:2 * P], openrep[:], ident[:]).then_inc(ends_turned, 1)
                pe.wait_ge(chained, step + 1)
                pe.transpose(psT[:, 2 * P:2 * P + FEAT], chain[:, 0:P], ident[0:FEAT, 0:FEAT]).then_inc(ends_turned, 1)

            join_runs(0)

            sort_turns(sorting, sort_turned)

            pe.wait_ge(lweights, 1)

            def logits_chunk(n, b):
                starts = (0, 4, 8, GROUP - 4)
                pe.wait_ge(l_normed, n + 1)

                def turn(g):
                    if g >= 2 or not isinstance(n, int) or n >= 1:
                        pe.wait_ge(l_hT, n * 4 + g - 1)
                    for k in range(2):
                        a = lh[:, b, k * GROUP + starts[g]:k * GROUP + starts[g] + 4]
                        t = pe.transpose(psM[:, g % 2, k * P:(k + 1) * P], a.rearrange("p t f -> p (t f)"), ident[:])
                    t.then_inc(l_turned, 1)

                def mix(g):
                    if g == 0 and (not isinstance(n, int) or n >= 2):
                        pe.wait_ge(l_biased, n - 1)
                    pe.wait_ge(l_hT, n * 4 + g + 1)
                    for k in range(2):
                        mm = pe.matmul(psR[:, b, HEADS * starts[g]:HEADS * (starts[g] + 4)],
                                       hT[:, g % 2, k * P:(k + 1) * P], ublk[:, k], start=(k == 0), stop=(k == 1))
                    mm.then_inc(l_logits, 1)

                turn(0)
                for g in range(4):
                    if g < 3:
                        turn(g + 1)
                    mix(g)

            logits_chunk(0, 0)
            logits_chunk(1, 1)
            with pe.Fori(1, CHUNKS // 2) as i:
                logits_chunk(2 * i, 0)
                logits_chunk(2 * i + 1, 1)

            for turn in range(4):
                pe.wait_ge(joining, turn + 1)
                if turn % 2 == 0:
                    for k in range(4):
                        t = pe.transpose(psT[0:HEADS, k * P:(k + 1) * P], ends[:, k], ident[:])
                else:
                    for k in range(2):
                        t = pe.transpose(psT[:, k * HEADS:(k + 1) * HEADS], ladder[:, k, k:k + P],
                                         ident[0:HEADS, 0:HEADS])
                t.then_inc(s_turned, 1)

            def mix_chunk(n, b):
                pe.wait_ge(weighed, n + 1)

                def turn(g):
                    if not isinstance(n, int) or n >= 1:
                        pe.wait_ge(m_wT, n * 4 + g - 3)
                    for k in range(4 * g, min(4 * g + 4, GROUP)):
                        t = pe.transpose(psM[:, g, (k - 4 * g) * P:(k - 4 * g + 1) * P], weighted[:, b, k], ident[:])
                    t.then_inc(m_turned, 1)

                def mix(g):
                    if g == 0 and (not isinstance(n, int) or n >= 2):
                        pe.wait_ge(m_out, n - 1)
                    pe.wait_ge(m_wT, n * 4 + g + 1)
                    for k in range(4 * g, min(4 * g + 4, GROUP)):
                        mm = pe.matmul(psR[:, b, k * FEAT:(k + 1) * FEAT], wT[:, g % 2, (k - 4 * g) * P:(k - 4 * g + 1) * P],
                                       wstk[:], start=True, stop=True)
                    mm.then_inc(m_mixed, 1)

                turn(0)
                for g in range(4):
                    if g < 3:
                        turn(g + 1)
                    mix(g)

            mix_chunk(0, 0)
            mix_chunk(1, 1)
            with pe.Fori(1, CHUNKS // 2) as i:
                mix_chunk(2 * i, 0)
                mix_chunk(2 * i + 1, 1)
            join_runs(1)

        @block.vector
        def _(dve):
            st = Steps(dve, prep)
            TT, TS, STT = dve.tensor_tensor, dve.tensor_scalar, dve.scalar_tensor_tensor

            def late(n, first=2):
                return not isinstance(n, int) or n >= first

            st.do(dve.memset(ones32[:], 1.0))
            st.do(dve.memset(chain[:, 0:1], 0.0))
            dve.wait_ge(edges_in, 13 * DMA)
            dve.tensor_copy(src_f[:], src_i[:]).then_inc(floats, 1)
            dve.tensor_copy(dst_ext[:], dst_ext_i[:]).then_inc(floats, 1)
            dve.tensor_copy(dst_f[:], dst_ext_i[:, 1:COLS + 1]).then_inc(floats, 1)
            dve.wait_ge(floats, 3)
            st.link(TT(idx_tmp[:], dst_ext[:, 1:COLS + 1], dst_ext[:, 2:], ALU.is_gt))
            dve.tensor_reduce(unsorted[:], idx_tmp[:], AX.X, ALU.max).then_inc(compared, 1)
            dve.wait_ge(flag_turned, 1)
            st.link(dve.tensor_reduce(unsorted_1[:], psT[0:1, 0:P], AX.X, ALU.max))
            dve.tensor_copy(flag[:], unsorted_1[:]).then_inc(flagged, 1)

            def sort_pairs(so, turned):
                half = turns = 0
                for kind, arg in SORT_PLAN:
                    key, load = skey[:, half], spay[:, half]
                    if kind == "flip":
                        so.settle()
                        for a, factor in flips_of(arg, key):
                            so.do(TS(a, a, -1.0 if factor is None else flip[:, factor:factor + 1], None, ALU.mult))
                        so.settle()
                    elif kind == "turn":
                        turns += 1
                        dve.wait_ge(turned, turns)
                        so.link(dve.tensor_copy(pairs[:, half].rearrange("p k c -> p (k c)"), psX[:]))
                    else:
                        def pair(a):
                            v = a.rearrange("p (m two d) -> p m two d", two=2, d=arg)
                            return v[:, :, 0], v[:, :, 1]

                        (ka, kb), (pa, pb) = pair(key), pair(load)
                        (ko, kp), (po, pp) = pair(skey[:, 1 - half]), pair(spay[:, 1 - half])
                        g = gt[:].rearrange("p (m d) -> p m d", d=arg)
                        d = dpay[:].rearrange("p (m d) -> p m d", d=arg)
                        n0 = so.n
                        dve.wait_ge(so.s, n0 - 2)
                        so.do(TT(g, ka, kb, ALU.is_gt))
                        so.do(TT(ko, ka, kb, ALU.min))
                        dve.wait_ge(so.s, n0)
                        so.do(TT(d, pb, pa, ALU.subtract))
                        so.do(TT(kp, ka, kb, ALU.max))
                        dve.wait_ge(so.s, n0 + 3)
                        so.do(TT(d, d, g, ALU.mult))
                        dve.wait_ge(so.s, n0 + 5)
                        so.do(TT(po, pa, d, ALU.add))
                        so.do(TT(pp, pb, d, ALU.subtract))
                        half = 1 - half
                assert so.n == SORT_STEPS and half == SORT_END

            dve.wait_ge(weights_in, 15 * DMA)
            dve.wait_ge(flagged, 1)
            with dve.If(dve.value_load(flag[:], min_val=0, max_val=1) > 0):
                rs = Steps(dve, r_sorting)
                rs.do(dve.tensor_copy(skey[:, 0, 0:COLS], dst_f[:]))
                rs.do(dve.memset(skey[:, 0, COLS:], float(NODES)))
                rs.do(TS(spay[:, 0, 0:COLS], pos[:], float(NODES), None, ALU.subtract))
                rs.do(dve.memset(spay[:, 0, COLS:], float(SLOTS - 1)))
                dve.memset(record[:, :, 5:], 0.0)
                dve.tensor_copy(record[:, :, 0], src_f[:])
                dve.tensor_copy(record[:, :, 1], dist[:])
                dve.tensor_copy(record[:, :, 2:5], vec[:]).then_inc(r_built, 1)
                sort_pairs(rs, r_sort_turned)
                dve.wait_ge(r_order_in, 2 * DMA)
                dve.tensor_copy(dst_f[:], dst_ext[:, 1:COLS + 1])
                dve.tensor_copy(idx_out[:], pay[:]).then_inc(r_indexed, 1)
                dve.wait_ge(r_record_there, 1)

                def unpack(n, b, rounds):
                    dve.wait_ge(r_in[b], GATHERED * rounds)
                    TS(record[:, chunk_cols(n)], record_ring[:, b], 1.0, None, ALU.mult).then_inc(r_unpacked, 1)

                with dve.Fori(0, CHUNKS // 2) as i:
                    unpack(2 * i, 0, i + 1)
                    unpack(2 * i + 1, 1, i + 1)
                dve.wait_ge(r_unpacked, CHUNKS)
                dve.tensor_copy(dist[:], record[:, :, 1])
                dve.tensor_copy(vec[:], record[:, :, 2:5])
                dve.tensor_copy(src_f[:], record[:, :, 0]).then_inc(r_unpacked, 1)
                dve.wait_ge(r_unpacked, CHUNKS + 1)
            TS(idx_src[:], src_f[:], float(NODES - 1), None, ALU.min).then_inc(idx_src_ready, 1)

            def block_of(k, n=1):
                a = w2raw[:, k * MUL * MUL:(k + n) * MUL * MUL]
                return a.rearrange("p (u v k) -> p k v u", v=MUL, k=n)

            m01 = w2p[:, 0:NA].rearrange("p (w u) -> p w u", u=W16)
            m23 = w2p[:, NA:].rearrange("p (w u) -> p w u", u=MUL)
            TS(m01[:, 0:MUL, 0:MUL], block_of(0)[:, 0], K_00, None, ALU.mult)
            TS(m01[:, MUL:, 0:MUL], block_of(1)[:, 0], K_01, None, ALU.mult)
            TS(m01[:, 0:MUL, MUL:], block_of(2)[:, 0], K_10, None, ALU.mult)
            TS(m01[:, MUL:, MUL:], block_of(3, 3)[:, 2], K_112R, None, ALU.mult)
            TS(m23[:, MUL:], block_of(3, 3)[:, 1], K_111, None, ALU.mult)
            st.link(TS(w2t[:], block_of(3, 3)[:, 2], K_112I, None, ALU.mult))
            STT(m23[:, 0:MUL], block_of(3, 3)[:, 0], K_110, w2t[:], ALU.mult, ALU.add).then_inc(w2_ready, 1)
            dve.wait_ge(vsq_done, 1)
            dve.tensor_reduce(vn[:, 0], vsq, AX.X, ALU.add).then_inc(vnorm, 1)
            dve.wait_ge(vstd, 1)
            st.link(dve.reciprocal(vn[:, 2], vn[:, 1]))
            st.do(TT(r5[:, :, 0:2], vec[:, :, 1:3], bc(vn[:, 2], 2, 2), ALU.mult))
            st.link(TT(r5[:, :, 2:5], vec[:], bc(vn[:, 2], 2, 3), ALU.mult))

            def center(n, b, rounds):
                dve.wait_ge(x_in[b], GATHERED * rounds)
                dve.tensor_reduce(lsum[:, b, 0:GROUP], xring[:, b], AX.X, ALU.add).then_inc(summed, 1)
                dve.wait_ge(summed, n + 1)
                TS(mean[:, b, 0:GROUP], lsum[:, b, 0:GROUP], 1.0 / FEAT, None, ALU.mult).then_inc(meaned, 1)
                dve.wait_ge(meaned, n + 1)
                TT(xc[:, b], xring[:, b], bc(mean[:, b, 0:GROUP], 2, FEAT), ALU.subtract).then_inc(centered, 1)

            def deviate(n, b):
                dve.wait_ge(squared, n + 1)
                dve.tensor_reduce(vsum[:, b, 0:GROUP], sq[:, b], AX.X, ALU.add).then_inc(varsummed, 1)

            def operands(n, b):
                dve.wait_ge(stded, n + 1)
                dve.reciprocal(rstd[:, b, 0:GROUP], std[:, b, 0:GROUP]).then_inc(rstded, 1)
                dve.wait_ge(rstded, n + 1)
                STT(h0[:, b], xc[:, b], 0.0, bc(rstd[:, b, 0:GROUP], 2, FEAT), ALU.max, ALU.mult).then_inc(normed, 1)
                dve.wait_ge(normed, n + 1)
                f1 = h0[:, b, :, MUL:].rearrange("p t (v o) -> p t v o", o=3)
                r = r5[:, chunk_cols(n)]
                TT(crs[:, 2], f1, bc(r[:, :, 0:3], 2, MUL), ALU.mult).then_inc(dotp, 1)
                dve.wait_ge(spread, n + 1)
                TT(crs[:, 0], f1e[:, b, :, :, 2:5], bc(r[:, :, 1:4], 2, MUL), ALU.mult)
                TT(crs[:, 1], f1e[:, b, :, :, 1:4], bc(r[:, :, 2:5], 2, MUL), ALU.mult).then_inc(crossed, 1)
                dve.wait_ge(dotp, n + 1)
                dve.tensor_reduce(z[:, b, :, MUL:], crs[:, 2], AX.X, ALU.add).then_inc(dotted, 1)
                dve.wait_ge(crossed, n + 1)
                TT(V[:, b, :, MUL:], crs[:, 0], crs[:, 1], ALU.subtract).then_inc(vectored, 1)

            def products(n, b, h):
                if h == 0:
                    dve.wait_ge(dotted, n + 1)
                    dve.wait_ge(vectored, n + 1)
                if late(n, 1):
                    dve.wait_ge(reduced, 2 * n + h - 1)
                for t in range(HALF):
                    k = h * HALF + t
                    bank = (b * GROUP + k) % 4
                    dve.wait_ge(radial_ready, n * GROUP + k + 1)
                    TT(prodA[:, h, t], psM[:, bank, 0:NA].rearrange("p (w u) -> p w u", u=W16),
                       bc(z[:, b, k], 2, W16), ALU.mult)
                    TT(prodB[:, h, t].rearrange("p w (u o) -> p w u o", o=3),
                       bc(psM[:, bank, NA:RADIAL].rearrange("p (w u) -> p w u", u=MUL), 3, 3),
                       bc(V[:, b, k], 2, MUL), ALU.mult).then_inc(prod_done, 1)
                dve.wait_ge(prod_done, n * GROUP + h * HALF + HALF)
                TT(prodB[:, h, :, 0:MUL], prodB[:, h, :, 0:MUL], prodB[:, h, :, MUL:], ALU.add).then_inc(preadded, 1)

            def post(n, h):
                dve.wait_ge(reduced, 2 * n + h + 1)
                cols = bass.ds(n * GROUP + h * HALF, HALF)
                a = psR[:, h, 0:HALF * W16].rearrange("p (t u) -> p t u", u=W16)
                v = psR[:, h, HALF * W16:HALF * (W16 + 3 * MUL)].rearrange("p (t f) -> p t f", f=3 * MUL)
                TT(qr[:, h], bc(a[:, :, MUL:], 3, 3), bc(r5[:, cols, 0:3], 2, MUL), ALU.mult).then_inc(q_done, 1)
                TS(msg[:, cols, 0:MUL], a[:, :, 0:MUL], 1.0, None, ALU.mult)
                dve.wait_ge(q_done, 2 * n + h + 1)
                TT(msg[:, cols, MUL:], qr[:, h].rearrange("p t v o -> p t (v o)"), v, ALU.add).then_inc(posted, 1)

            def layer0_step(n, b, rounds):
                center(n, b, rounds)
                products(n - 1, 1 - b, 0)
                if late(n):
                    post(n - 2, 1)
                deviate(n, b)
                products(n - 1, 1 - b, 1)
                post(n - 1, 0)
                operands(n, b)

            center(0, 0, 1)
            deviate(0, 0)
            operands(0, 0)
            layer0_step(1, 1, 1)
            with dve.Fori(1, CHUNKS // 2) as i:
                layer0_step(2 * i, 0, i + 1)
                layer0_step(2 * i + 1, 1, i + 1)
            products(CHUNKS - 1, 1, 0)
            post(CHUNKS - 2, 1)
            products(CHUNKS - 1, 1, 1)
            post(CHUNKS - 1, 0)
            post(CHUNKS - 1, 1)

            TT(same[:], dst_ext[:, 1:COLS + 1], dst_ext[:, 0:COLS], ALU.is_equal)
            st.link(TT(last[:], dst_ext[:, 1:COLS + 1], dst_ext[:, 2:], ALU.not_equal))
            st.do(TT(idx_tmp[:], dst_f[:], pos[:], ALU.subtract))
            st.link(dve.tensor_tensor_scan(opened[:], same[:], same[:], 1.0, ALU.mult, ALU.mult))
            st.do(TS(openrep[:], ones32[:], opened[:, COLS - 1:], None, ALU.mult))
            st.link(TT(idx_tmp[:], idx_tmp[:], last[:], ALU.mult))
            TT(idx_dst[:], idx_tmp[:], pos[:], ALU.add).then_inc(idx_ready, 1)
            st.settle()

            def sum_segments(step):
                dve.wait_ge(posted, 2 * CHUNKS)
                if step == 1:
                    dve.wait_ge(m_out, CHUNKS)
                for f in range(FEAT):
                    scan = dve.tensor_tensor_scan(msg[:, :, f], same[:], msg[:, :, f], 0.0, ALU.mult, ALU.add)
                scan.then_inc(scanned, 1)
                dve.wait_ge(ends_turned, 2 * step + 1)
                st.link(dve.tensor_copy(openT[:], psT[0:FEAT, P:2 * P]))
                dve.tensor_tensor_scan(chain[:, 1:], openT[:], psT[0:FEAT, 0:P], 0.0, ALU.mult, ALU.add
                                       ).then_inc(chained, 1)
                dve.wait_ge(ends_turned, 2 * step + 2)
                dve.tensor_copy(carry[:], psT[:, 2 * P:2 * P + FEAT]).then_inc(carried, 1)
                dve.wait_ge(carried, step + 1)
                dve.wait_ge(scanned, step + 1)
                for f in range(FEAT):
                    fix = STT(msg[:, :, f], opened[:], carry[:, f:f + 1], msg[:, :, f], ALU.mult, ALU.add)
                fix.then_inc(fixed, 1)

            sum_segments(0)

            for k in range(2):
                st.do(TT(wmul[:, k], wrep[:], bc(fcw_b[:, k * FEAT:(k + 1) * FEAT], 1, HEADS), ALU.mult))
            st.do(dve.memset(ublk[:], 0.0))
            st.link(TS(wstk[:], wstk_raw[:], 1.0 / HEADS, None, ALU.mult))
            st.link(dve.tensor_reduce(u_all[:], wmul[:], AX.X, ALU.add))
            for k in range(2):
                for t in range(4):
                    put = dve.tensor_copy(ublk[32 * t:32 * t + 32, k, HEADS * t:HEADS * (t + 1)],
                                          u_all[32 * t:32 * t + 32, k])
            put.then_inc(lweights, 1)

            so = Steps(dve, sorting)
            so.do(dve.tensor_copy(skey[:, 0, 0:COLS], src_f[:]))
            so.do(dve.memset(skey[:, 0, COLS:], float(NODES)))
            so.do(dve.tensor_copy(spay[:, 0, 0:COLS], dst_f[:]))
            so.do(dve.memset(spay[:, 0, COLS:], float(NODES)))
            sort_pairs(so, sort_turned)

            dve.wait_ge(srcorder_in, 2 * DMA)
            key = key_ext[:, 1:COLS + 1]
            dve.tensor_copy(idx_src[:], key).then_inc(idx_ready, 1)
            dve.tensor_copy(idx_dst_s[:], pay[:]).then_inc(idx_ready, 1)
            TT(same[:], key, key_ext[:, 0:COLS], ALU.is_equal)
            TT(last[:], key, key_ext[:, 2:], ALU.not_equal)
            st.link(TT(more[:], key, key_ext[:, 2:], ALU.is_equal))
            st.do(TS(negs[:, 0], same[:], 1.0, BIG, ALU.subtract, ALU.mult))
            st.do(TS(negs[:, 1], last[:], -BIG, None, ALU.mult))
            st.do(dve.tensor_tensor_scan(opened[:], same[:], same[:], 1.0, ALU.mult, ALU.mult))
            st.do(dve.tensor_tensor_scan(openR[:, ::-1], more[:, ::-1], more[:, ::-1], 1.0, ALU.mult, ALU.mult))
            st.link(TS(idx_tmp[:], more[:], 2.0 * NODES, None, ALU.mult))
            TT(idx_out[:], idx_tmp[:], key, ALU.add).then_inc(idx_ready, 1)
            st.do(TS(openrep[:], ones32[:], opened[:, COLS - 1:], None, ALU.mult))
            st.do(TS(negopen[:, 0], opened[:], 1.0, BIG, ALU.subtract, ALU.mult))
            st.link(TS(negopen[:, 1], openR[:], 1.0, BIG, ALU.subtract, ALU.mult))

            def layer1_chunk(n, b, rounds, filling):
                dve.wait_ge(l_in[b], 2 * GATHERED * rounds)
                dve.tensor_reduce(lsum[:, b], lring[:, b], AX.X, ALU.add).then_inc(l_summed, 1)
                dve.wait_ge(l_summed, n + 1)
                TS(mean[:, b], lsum[:, b], 1.0 / FEAT, None, ALU.mult).then_inc(l_meaned, 1)
                dve.wait_ge(l_meaned, n + 1)
                TT(lxc, lring[:, b], bc(mean[:, b], 2, FEAT), ALU.subtract).then_inc(l_centered, 1)
                TT(xsb[:, chunk_cols(n)], lring[:, b, 0:GROUP], bc(bias_b[:], 1, GROUP), ALU.add).then_inc(l_based, 1)
                if filling:
                    rows = fill[:, b].rearrange("p (r d) -> p r d", d=FEAT)
                    dve.wait_ge(fill_in[b], DMA * rounds)
                    TT(rows, rows, bc(bias_b[0:FILL_P], 1, FILL_ROWS), ALU.add).then_inc(fill_added, 1)
                dve.wait_ge(l_squared, n + 1)
                dve.tensor_reduce(vsum[:, b], lsq, AX.X, ALU.add).then_inc(l_varsummed, 1)
                dve.wait_ge(l_stded, n + 1)
                dve.reciprocal(rstd[:, b], std[:, b]).then_inc(l_rstded, 1)
                dve.wait_ge(l_rstded, n + 1)
                if late(n):
                    dve.wait_ge(l_saved, n - 1)
                    dve.wait_ge(l_turned, 4 * (n - 1))
                STT(lh[:, b], lxc, 0.0, bc(rstd[:, b], 2, FEAT), ALU.max, ALU.mult).then_inc(l_normed, 1)
                dve.wait_ge(l_logits, 4 * (n + 1))
                TS(lgt[:], psR[:, b, 0:GROUP * HEADS], fcb_b[:], None, ALU.add).then_inc(l_biased, 1)
                dve.wait_ge(l_biased, n + 1)
                STT(E[:, chunk_cols(n)].rearrange("p t h -> p (t h)"), lgt[:], 0.2, lgt[:], ALU.mult, ALU.max
                    ).then_inc(l_logged, 1)

            layer1_chunk(0, 0, 1, True)
            layer1_chunk(1, 1, 1, True)
            with dve.Fori(1, FILLS // 2) as i:
                for b in range(2):
                    layer1_chunk(2 * i + b, b, i + 1, True)
            with dve.Fori(FILLS // 2, CHUNKS // 2) as i:
                for b in range(2):
                    layer1_chunk(2 * i + b, b, i + 1, False)
            dve.wait_ge(l_logged, CHUNKS)

            left, right, tmp, prob = (soft[:, k] for k in range(4))

            def both_ways(step, data, mask_l, mask_r, open_l, open_r, start, op0, op1):
                for h in range(HEADS):
                    dve.tensor_tensor_scan(left[:, :, h], mask_l, data[:, :, h], start, op0, op1)
                for h in range(HEADS):
                    scan = dve.tensor_tensor_scan(right[:, ::-1, h], mask_r[:, ::-1], data[:, ::-1, h],
                                                  start, op0, op1)
                st.do(scan)
                st.do(dve.memset(ladder[:, 0, 0:1], start))
                st.do(dve.memset(ladder[:, 1, P:], start))
                st.do(TS(ends[:, 1], ones32[:, 0:HEADS], open_l[:, COLS - 1:], None, ALU.mult))
                st.do(TS(ends[:, 3], ones32[:, 0:HEADS], open_r[:, 0:1], None, ALU.mult))
                st.settle()
                dve.tensor_copy(ends[:, 0], left[:, COLS - 1])
                dve.tensor_copy(ends[:, 2], right[:, 0]).then_inc(joining, 1)
                dve.wait_ge(s_turned, 2 * step + 1)
                st.do(dve.tensor_copy(endT[:, 0], psT[0:HEADS, P:2 * P]))
                st.link(dve.tensor_copy(endT[:, 1], psT[0:HEADS, 3 * P:]))
                dve.tensor_tensor_scan(ladder[:, 0, 1:], endT[:, 0], psT[0:HEADS, 0:P], start, op0, op1)
                dve.tensor_tensor_scan(ladder[:, 1, 0:P][:, ::-1],
                                       endT[:, 1, ::-1], psT[0:HEADS, 2 * P:3 * P][:, ::-1],
                                       start, op0, op1).then_inc(joining, 1)
                dve.wait_ge(s_turned, 2 * step + 2)
                st.link(dve.tensor_copy(join[:], psT[:, 0:2 * HEADS].rearrange("p (k h) -> p k h", k=2)))

            def add_join(k, opens, op0, op1):
                st.link(TT(tmp, bc(join[:, k], 1, COLS), bc(opens, 2, HEADS), op0))
                st.link(TT(left, left, tmp, op1))

            both_ways(0, E, negs[:, 0], negs[:, 1], negopen[:, 0], negopen[:, 1], -BIG, ALU.add, ALU.max)
            st.link(TT(left, left, right, ALU.max))
            add_join(0, negopen[:, 0], ALU.add, ALU.max)
            add_join(1, negopen[:, 1], ALU.add, ALU.max)
            TT(tmp, E, left, ALU.subtract).then_inc(shifted, 1)
            dve.wait_ge(s_exp, 1)
            both_ways(1, prob, same[:], more[:], opened[:], openR[:], 0.0, ALU.mult, ALU.add)
            st.link(TT(right, right, prob, ALU.subtract))
            st.link(TT(left, left, right, ALU.add))
            add_join(0, opened[:], ALU.mult, ALU.add)
            add_join(1, openR[:], ALU.mult, ALU.add)
            st.link(dve.reciprocal(right, left))
            st.link(TT(prob, prob, right, ALU.mult))

            def weigh(n, b):
                if late(n):
                    dve.wait_ge(m_turned, 4 * (n - 1))
                TT(weighted[:, b].rearrange("p t (h f) -> p t h f", h=HEADS), bc(hd[:, chunk_cols(n)], 2, HEADS),
                   bc(prob[:, chunk_cols(n)], 3, FEAT), ALU.mult).then_inc(weighed, 1)

            dve.wait_ge(l_saved, CHUNKS)
            weigh(0, 0)
            weigh(1, 1)
            with dve.Fori(1, CHUNKS // 2) as i:
                weigh(2 * i, 0)
                weigh(2 * i + 1, 1)
            sum_segments(1)
            dve.wait_ge(fixed, 2)

            def out_chunk(n, b, rounds):
                if late(n):
                    dve.wait_ge(out_done[b], GATHERED * rounds)
                TT(rowring[:, b], msg[:, chunk_cols(n)], xsb[:, chunk_cols(n)], ALU.add).then_inc(out_rows, 1)

            out_chunk(0, 0, 0)
            out_chunk(1, 1, 0)
            with dve.Fori(1, CHUNKS // 2) as i:
                out_chunk(2 * i, 0, i)
                out_chunk(2 * i + 1, 1, i)


_INS = ["x", "src", "dst", "edge_attr_3", "edge_weight", "L0_gnn_w1", "L0_gnn_b1", "L0_gnn_w2", "L0_gnn_b2",
        "L1_gnn_w", "L1_gnn_fc_w", "L1_gnn_fc_b", "L1_gnn_bias"]


def shape_constants():
    eye = np.eye(P, dtype=np.float32)
    posn = (NODES + np.arange(SLOTS)).reshape(P, COLS).astype(np.float32)
    p = np.arange(P)
    f = [1.0 - 2.0 * ((p >> b) & 1) for b in range(7)]
    flips = np.stack([f[0], -f[0]] + [f[b] * f[b + 1] for b in range(6)] + [f[6]], 1).astype(np.float32)
    return {"eye": eye, "posn": posn, "flips": flips}


def kernel(**inputs):
    import concourse.bacc as _bacc
    from concourse.bass_utils import run_bass_kernel_spmd as _run

    nc = _bacc.Bacc("TRN2", target_bir_lowering=False, num_devices=1)
    arrays, args = {}, []
    given = {n: np.ascontiguousarray(inputs[n]) for n in _INS}
    for name, a in {**given, **shape_constants()}.items():
        arrays[f"in_{name}_dram"] = a
        args.append(nc.dram_tensor(f"in_{name}_dram", a.shape, mybir.dt.from_np(a.dtype), kind="ExternalInput").ap())
    out = nc.dram_tensor("out_0_dram", (NODES, FEAT), F32, kind="ExternalOutput").ap()
    graph_layers(nc, *args, out)
    r = _run(nc, [arrays], core_ids=[0])
    return r.results[0]["out_0_dram"]
```

```python
from contextlib import ExitStack
from math import sqrt

import numpy as np

import concourse.bass as bass
from concourse import mybir

P = 128
F32 = mybir.dt.float32
I32 = mybir.dt.int32
ALU = mybir.AluOpType
ACT = mybir.ActivationFunctionType
AX = mybir.AxisListType

NODES = 100000
EDGES = 25000
FEAT = 32
MUL = 8
HIDDEN = 64
HEADS = 4
RADIAL = 6 * MUL * MUL
COLS = -(-EDGES // P)
GROUP = 14
HALF = GROUP // 2
CHUNKS = COLS // GROUP
SLOTS = P * COLS
SORT_COLS = 256
SORT_BITS = 15
BIG = 1.0e30
EPS = 1e-5
RECORD = 8
DMA = 16
GATHERED = DMA * GROUP

W16 = 2 * MUL
NA = W16 * W16
NB = W16 * MUL
K_00 = 1 / 4
K_01 = 1 / 4
K_10 = sqrt(3 / 32)
K_110 = 1 / (4 * sqrt(2))
K_111 = sqrt(3) / 8
K_112R = 3 / 8
K_112I = -1 / 8

FILL_P = 80
FILL_ROWS = 125
COPY_PARTS = 5
FILLS = NODES // FILL_P // FILL_ROWS


def sort_plan():
    col_bits = SORT_COLS.bit_length() - 1
    plan, steps, half, turns, copies = [], 4, 0, [], []
    for k in range(1, SORT_BITS + 1):
        plan.append(("flip", k))
        steps += len(flips_of(k))

        def turn():
            plan.append(("turn", None))
            flipped = plan[-2][0] == "flip"
            turns.append((steps - (not flipped), steps - flipped, half))
            return steps + 1

        def compare(distance):
            plan.append(("compare", distance))
            copies.append((steps, half, plan[-2][0] == "turn"))
            return steps + 4, 1 - half

        if k > col_bits:
            steps = turn()
            for j in range(k - 1, col_bits - 1, -1):
                steps, half = compare(1 << (j - col_bits))
            steps = turn()
        for j in range(min(k, col_bits) - 1, -1, -1):
            steps, half = compare(1 << j)
    return plan, steps, half, turns, copies


def flips_of(k, keys=None):
    if keys is None:
        return [None] * (2 if 1 < k <= 8 else 1)
    if k == 1:
        return [(keys.rearrange("p (a u b) -> p a u b", u=2, b=2)[:, :, 1], None)]
    if k < 8:
        v = keys.rearrange("p (a u v b) -> p a u v b", u=2, v=2, b=1 << (k - 1))
        return [(v[:, :, 0, 1], None), (v[:, :, 1, 0], None)]
    if k == 8:
        return [(keys[:, 0:P], 0), (keys[:, P:], 1)]
    return [(keys, k - 7)]


SORT_PLAN, SORT_STEPS, SORT_END, SORT_TURNS, SORT_COPIES = sort_plan()


def graph_layers(nc, x, src, dst, attr, ew, w1, b1, w2, b2, w, fcw, fcb, bias, eye, posn, flips, out):
    assert CHUNKS * GROUP == COLS and CHUNKS % 2 == 0 and FILLS % 2 == 0 and FILLS < CHUNKS
    with ExitStack() as ctx:
        def sb(name, shape, dt=F32):
            return ctx.enter_context(nc.sbuf_tensor(name, shape, dt))

        def sem(name):
            return ctx.enter_context(nc.semaphore(name))

        nodes1 = nc.dram_tensor("nodes1", [NODES + SLOTS, FEAT], F32).ap()
        key_pad = nc.dram_tensor("key_pad", [P * SORT_COLS + 1], F32).ap()
        pay_dram = nc.dram_tensor("pay_dram", [P * SORT_COLS], F32).ap()
        records = nc.dram_tensor("records", [SLOTS, RECORD], F32).ap()
        dist_row = nc.dram_tensor("dist_row", [COLS, P], F32).ap()

        ident = sb("ident", [P, P])
        pos = sb("pos", [P, COLS])
        flip = sb("flip", [P, 9])
        eps = sb("eps", [P, 1])
        ones32 = sb("ones32", [P, FEAT])
        w1c = sb("w1c", [HIDDEN, 1])
        b1c = sb("b1c", [HIDDEN, 1])
        w2raw = sb("w2raw", [HIDDEN + 1, RADIAL])
        w2p = sb("w2p", [HIDDEN + 1, RADIAL])
        w2t = sb("w2t", [HIDDEN + 1, MUL, MUL])
        wrep = sb("wrep", [P, HEADS, FEAT])
        wmul = sb("wmul", [P, 2, HEADS, FEAT])
        fcw_b = sb("fcw_b", [P, 2 * FEAT])
        fcb_b = sb("fcb_b", [P, 1])
        bias_b = sb("bias_b", [P, FEAT])
        u_all = sb("u_all", [P, 2, HEADS])
        ublk = sb("ublk", [P, 2, 4 * HEADS])
        wstk_raw = sb("wstk_raw", [P, FEAT])
        wstk = sb("wstk", [P, FEAT])

        src_i = sb("src_i", [P, COLS], I32)
        dst_ext_i = sb("dst_ext_i", [P, COLS + 2], I32)
        dist = sb("dist", [P, COLS])
        vec = sb("vec", [P, COLS, 3])
        vsq = sb("vsq", [P, COLS, 3])
        vn = sb("vn", [P, 3, COLS])
        src_f = sb("src_f", [P, COLS])
        dst_f = sb("dst_f", [P, COLS])
        dst_ext = sb("dst_ext", [P, COLS + 2])
        idx_src = sb("idx_src", [P, COLS], I32)
        idx_dst = sb("idx_dst", [P, COLS], I32)
        idx_tmp = sb("idx_tmp", [P, COLS])
        r5 = sb("r5", [P, COLS, 5])
        same_d = sb("same_d", [P, COLS])
        same = sb("same", [P, COLS])
        last = sb("last", [P, COLS])
        opened = sb("opened", [P, COLS])
        distT = sb("distT", [P, 2, P])

        stage = sb("stage", [P, 2, 2, GROUP], I32)
        rowring = sb("rowring", [P, 2, GROUP, FEAT])

        def carver(arena):
            at = [0]

            def carve(shape, parts=P):
                n = int(np.prod(shape))
                names = "abcd"[:len(shape)]
                flat = arena[0:parts, at[0]:at[0] + n]
                at[0] += n
                return flat.rearrange(f"p ({' '.join(names)}) -> p {' '.join(names)}",
                                      **dict(zip(names, shape)))
            return carve

        class Sums:

            def __init__(self, parts):
                self.flat = parts
                self.terms, self.run, self.mask = (
                    a.rearrange("p b (f t) -> p b f t", f=FEAT) for a in parts)

        arena0 = sb("arena0", [P, 7504])
        carve = carver(arena0)
        xring = carve([2, GROUP, FEAT])
        xc = carve([2, GROUP, FEAT])
        sq = carve([2, GROUP, FEAT])
        h0 = carve([2, GROUP, FEAT])
        z = carve([2, GROUP, W16])
        V = carve([2, GROUP, W16 * 3]).rearrange("p b t (w o) -> p b t w o", o=3)
        f1e = carve([2, GROUP, MUL * 5]).rearrange("p b t (v o) -> p b t v o", o=5)
        crs = carve([3, GROUP, MUL * 3]).rearrange("p b t (v o) -> p b t v o", o=3)
        carve = carver(arena0)
        lring = carve([2, 2 * GROUP, FEAT])
        hT = carve([2, 2 * P])
        E = carve([COLS, HEADS])
        soft = carve([4, COLS, HEADS])
        wT = carve([2, 4 * P])

        arena1 = sb("arena1", [P, 4 * GROUP * P])
        carve = carver(arena1)
        hidden = carve([2, GROUP * P], HIDDEN + 1)
        distb = carve([2, GROUP * P], HIDDEN)
        carve = carver(arena1)
        lxc = carve([2 * GROUP, FEAT])
        lsq = carve([2 * GROUP, FEAT])
        lh = carve([2, 2 * GROUP, FEAT])
        weighted = carve([2, GROUP, P])
        carve = carver(arena1)
        sums1 = Sums([carve([2, FEAT * GROUP]) for _ in range(3)])
        picks = carve([FEAT, GROUP])

        prods = sb("prods", [P, 2 * HALF * (NA + 3 * NB)])
        prodA = prods[:, 0:2 * HALF * NA].rearrange("p (h t w u) -> p h t w u", h=2, t=HALF, w=W16)
        prodB = prods[:, 2 * HALF * NA:].rearrange("p (h t w u) -> p h t w u", h=2, t=HALF, w=W16)
        vsq = prods[:, 0:3 * COLS].rearrange("p (c o) -> p c o", o=3)
        vn = prods[:, 3 * COLS:6 * COLS].rearrange("p (k c) -> p k c", k=3)
        record = prods[:, 0:RECORD * COLS].rearrange("p (c k) -> p c k", k=RECORD)
        fill = prods[0:FILL_P, 0:2 * FILL_ROWS * FEAT].rearrange("p (b n) -> p b n", b=2)

        mean = sb("mean", [P, 2, 2 * GROUP])
        lsum = sb("lsum", [P, 2, 2 * GROUP])
        vsum = sb("vsum", [P, 2, 2 * GROUP])
        std = sb("std", [P, 2, 2 * GROUP])
        rstd = sb("rstd", [P, 2, 2 * GROUP])
        qr = sb("qr", [P, 2, HALF, MUL, 3])
        hd = sb("hd", [P, COLS, FEAT])
        carve = carver(hd[:].rearrange("p c f -> p (c f)"))
        sums0 = Sums([carve([2, FEAT * GROUP]) for _ in range(3)])
        carry = sb("carry", [P, FEAT])
        openrep = sb("openrep", [P, FEAT])
        openT = sb("openT", [FEAT, P])
        chain = sb("chain", [FEAT, P + 1])

        pairs = sb("pairs", [P, 2, 2, SORT_COLS])
        skey, spay = pairs[:, :, 0], pairs[:, :, 1]
        key_ext = sb("key_ext", [P, COLS + 2])
        pay = sb("pay", [P, COLS])
        idx_dst_s = sb("idx_dst_s", [P, COLS], I32)
        idx_out = sb("idx_out", [P, COLS], I32)
        more = sb("more", [P, COLS])
        negopen = sb("negopen", [P, 2, COLS])
        before = sb("before", [1, 1])
        unsorted = sb("unsorted", [P, 1])
        unsorted_1 = sb("unsorted_1", [1, 1])
        flag = sb("flag", [1, 1], I32)
        record_ring = sb("record_ring", [P, 2, GROUP, RECORD])

        xsb = sb("xsb", [P, COLS, FEAT])
        x_src = xsb
        lend = sb("lend", [P, FEAT])
        ends_in = sb("ends_in", [P, COLS])
        crosses = sb("crosses", [P, 2])
        idx_carry = sb("idx_carry", [P, 2], I32)
        picked = sb("picked", [P, FEAT])
        held = sb("held", [P, FEAT])
        lgt = sb("lgt", [P, GROUP * HEADS])
        negs = sb("negs", [P, 2, COLS])
        openR = sb("openR", [P, COLS])
        ends = sb("ends", [P, 4, HEADS])
        endT = sb("endT", [HEADS, 2, P])
        ladder = sb("ladder", [HEADS, 2, P + 1])
        join = sb("join", [P, 2, HEADS])

        psM = ctx.enter_context(nc.psum_tensor("psM", [P, 4, 512], F32))
        psR = ctx.enter_context(nc.psum_tensor("psR", [P, 2, 512], F32))
        psT = ctx.enter_context(nc.psum_tensor("psT", [P, 512], F32))
        psX = ctx.enter_context(nc.psum_tensor("psX", [P, 512], F32))
        swaps = psR[:, :, 0:P].bitcast(I32)

        prefilled, ids_in, edges_in = map(sem, ("prefilled", "ids_in", "edges_in"))
        sorters_in, weights_in, copied = map(sem, ("sorters_in", "weights_in", "copied"))
        floats, edge_vals = map(sem, ("floats", "edge_vals"))
        before_out, r_record_out, r_record_there = map(sem, ("before_out", "r_record_out", "r_record_there"))
        compared, flag_turned, flagged = map(sem, ("compared", "flag_turned", "flagged"))
        r_pay_copied, pay_copied = sem("r_pay_copied"), sem("pay_copied")
        r_sort_turned, sort_turned = ([sem(f"{n}_{what}") for what in ("keys", "payloads")]
                                      for n in ("r_sort_turned", "sort_turned"))
        r_sorting, r_built, r_stored, r_order_in, r_indexed, r_staged, r_unpacked = map(
            sem, ("r_sorting", "r_built", "r_stored", "r_order_in", "r_indexed", "r_staged",
                  "r_unpacked"))
        r_in = [sem("r_in0"), sem("r_in1")]
        prep, acts = sem("prep"), sem("acts")
        vsq_done, vnorm, vstd, idx_src_ready = map(sem, ("vsq_done", "vnorm", "vstd", "idx_src_ready"))
        w2_ready, lweights = sem("w2_ready"), sem("lweights")
        dist_turned, dist_copied, dist_stored = map(sem, ("dist_turned", "dist_copied", "dist_stored"))
        pool_turn, staged = sem("pool_turn"), sem("staged")
        x_in = [sem("x_in0"), sem("x_in1")]
        summed, meaned, centered, squared, varsummed, stded, rstded, normed = map(
            sem, ("summed", "meaned", "centered", "squared", "varsummed", "stded", "rstded", "normed"))
        spread, dotp, dotted, crossed, vectored = map(sem, ("spread", "dotp", "dotted", "crossed", "vectored"))
        dist_bc = [sem("dist_bc0"), sem("dist_bc1")]
        hid_ready, radial_ready, prod_done, preadded, reduced, q_done, posted = map(
            sem, ("hid_ready", "radial_ready", "prod_done", "preadded", "reduced", "q_done", "posted"))
        x_saved = sem("x_saved")
        masked, joined, summed_up = ([sem(f"{n}{k}") for k in range(2)] for n in ("masked", "joined", "summed_up"))
        ended, ends_turned, chained, carried = map(sem, ("ended", "ends_turned", "chained", "carried"))
        carry_out = [sem("carry_out0"), sem("carry_out1")]
        multiplied, picking, holding = map(sem, ("multiplied", "picking", "holding"))
        act_turn, rows_ready = sem("act_turn"), sem("rows_ready")
        rows_out = [sem("rows_out0"), sem("rows_out1")]
        sorting, sorted_out, srcorder_in, idx_ready = map(
            sem, ("sorting", "sorted_out", "srcorder_in", "idx_ready"))
        l_in = [sem("l_in0"), sem("l_in1")]
        l_summed, l_meaned, l_centered, l_squared, l_varsummed, l_stded, l_rstded, l_normed = map(
            sem, ("l_summed", "l_meaned", "l_centered", "l_squared", "l_varsummed", "l_stded", "l_rstded",
                  "l_normed"))
        l_saved, l_based, l_turned, l_hT, l_logits, l_biased, l_logged = map(
            sem, ("l_saved", "l_based", "l_turned", "l_hT", "l_logits", "l_biased", "l_logged"))
        fill_in = [sem("fill_in0"), sem("fill_in1")]
        fill_added = sem("fill_added")
        fill_out = [sem("fill_out0"), sem("fill_out1")]
        s_turned, s_exp, joining, shifted = map(sem, ("s_turned", "s_exp", "joining", "shifted"))
        weighed, m_turned, m_wT, m_mixed, m_out = map(sem, ("weighed", "m_turned", "m_wT", "m_mixed", "m_out"))
        out_rows = sem("out_rows")
        out_done = [sem("out_done0"), sem("out_done1")]

        last_rows = (P - 1) * COLS
        tail = EDGES - last_rows

        def windows(a, start, n):
            return bass.AP(tensor=a.tensor, offset=start, ap=[[COLS, n], [1, COLS + 2]])

        def chunk_cols(n):
            return bass.ds(n * GROUP, GROUP)

        class Steps:

            def __init__(self, eng, s, base=0):
                self.eng, self.s, self.n = eng, s, base

            def do(self, ins):
                ins.then_inc(self.s, 1)
                self.n += 1

            def settle(self):
                self.eng.wait_ge(self.s, self.n)

            def link(self, ins):
                self.do(ins)
                self.settle()

        def bc(ap, axis, n):
            a = ap.unsqueeze(axis)
            shape = list(a.shape)
            shape[axis] = n
            return a.broadcast_to(shape)

        block = ctx.enter_context(nc.Block())

        @block.sync
        def _(sp):
            for tile, a in ((ident[:], eye), (flip[:], flips)):
                sp.dma_start(tile, a).then_inc(sorters_in, DMA)

            def edge_array(tile, a):
                whole = a[0:last_rows].rearrange("(p c) -> p c", c=COLS)
                sp.dma_start(tile[0:112, :], whole[0:112]).then_inc(ids_in if a is src else edges_in, DMA)
                sp.dma_start(tile[112:P - 1, :], whole[112:P - 1]).then_inc(ids_in if a is src else edges_in, DMA)
                sp.dma_start(tile[P - 1:P, 0:tail], a[last_rows:EDGES].rearrange("(p c) -> p c", p=1)
                             ).then_inc(ids_in if a is src else edges_in, DMA)

            sp.wait_ge(prefilled, 3)
            sp.dma_start(dst_ext_i[0:1, 1:], dst[0:COLS + 1].rearrange("(p c) -> p c", p=1)).then_inc(ids_in, DMA)
            sp.dma_start(dst_ext_i[1:113], windows(dst, COLS - 1, 112)).then_inc(ids_in, DMA)
            sp.dma_start(dst_ext_i[113:P - 1], windows(dst, 113 * COLS - 1, P - 114)).then_inc(ids_in, DMA)
            sp.dma_start(dst_ext_i[P - 1:P, 0:tail + 1], dst[last_rows - 1:EDGES].rearrange("(p c) -> p c", p=1)
                         ).then_inc(ids_in, DMA)
            edge_array(src_i, src)
            sp.wait_ge(prefilled, 5)
            edge_array(dist, ew)
            whole = attr[0:last_rows].rearrange("(p c) o -> p c o", c=COLS)
            sp.dma_start(vec[0:112], whole[0:112]).then_inc(edges_in, DMA)
            sp.dma_start(vec[112:P - 1], whole[112:P - 1]).then_inc(edges_in, DMA)
            sp.dma_start(vec[P - 1:P, 0:tail], attr[last_rows:EDGES].rearrange("(p c) o -> p c o", p=1)
                         ).then_inc(edges_in, DMA)
            for tile, a in (
                (pos[:], posn),
                (w1c[:], w1.rearrange("one h -> h one")), (b1c[:], b1.rearrange("(h one) -> h one", one=1)),
                (w2raw[0:HIDDEN], w2), (w2raw[HIDDEN:HIDDEN + 1], b2.rearrange("(one r) -> one r", one=1)),
                (fcw_b[:], fcw[0].partition_broadcast(P)), (fcb_b[:], fcb.partition_broadcast(P)),
                (bias_b[:], bias.partition_broadcast(P)), (wstk_raw[:], w.rearrange("h f o -> (h f) o")),
                *((wrep[32 * t:32 * t + 32], w.rearrange("h f o -> f h o")) for t in range(4)),
            ):
                sp.dma_start(tile, a).then_inc(weights_in, DMA)
            sp.wait_ge(edge_vals, 1)
            sp.dma_start(key_pad[0:1].rearrange("(a b) -> a b", a=1), before[:]).then_inc(before_out, DMA)
            sp.wait_ge(before_out, DMA)

            def sorted_pairs(stored, loaded, ext, payload):
                sp.dma_start(key_pad[1:1 + P * SORT_COLS].rearrange("(p c) -> p c", c=SORT_COLS),
                             skey[:, SORT_END]).then_inc(stored, DMA)
                sp.dma_start(pay_dram.rearrange("(p c) -> p c", c=SORT_COLS), spay[:, SORT_END]
                             ).then_inc(stored, DMA)
                sp.wait_ge(stored, 2 * DMA)
                sp.dma_start(ext, windows(key_pad, 0, P)).then_inc(loaded, DMA)
                sp.dma_start(payload, pay_dram[0:SLOTS].rearrange("(p c) -> p c", c=COLS)).then_inc(loaded, DMA)
                sp.wait_ge(loaded, 2 * DMA)

            sp.wait_ge(flagged, 1)
            with sp.If(sp.value_load(flag[:], min_val=0, max_val=1) > 0):
                sp.wait_ge(r_built, 1)
                sp.dma_start(records.rearrange("(p c) k -> p c k", c=COLS), record).then_inc(r_record_out, DMA)
                sp.wait_ge(r_sorting, SORT_STEPS)
                sorted_pairs(r_stored, r_order_in, dst_ext[:], pay[:])
                sp.wait_ge(r_record_out, DMA)
                sp.sem_inc(r_record_there, 1)

            sp.wait_ge(dist_copied, 1)
            for j in range(2):
                sp.dma_start(dist_row[98 * j:98 * j + 98], distT[0:98, j]).then_inc(dist_stored, DMA)
            sp.wait_ge(dist_stored, 2 * DMA)

            def dist_load(n, b):
                if not isinstance(n, int) or n >= 2:
                    sp.wait_ge(hid_ready, n - 1)
                sp.dma_start(distb[:, b], dist_row[chunk_cols(n)].rearrange("c p -> (c p)")
                             .partition_broadcast(HIDDEN)).then_inc(dist_bc[b], DMA)

            dist_load(0, 0)
            dist_load(1, 1)
            for part in range(COPY_PARTS):
                rows = bass.ds(part * NODES // COPY_PARTS, NODES // COPY_PARTS)
                if part:
                    sp.wait_ge(sorting, part * SORT_STEPS // COPY_PARTS)
                sp.dma_start(nodes1[rows].rearrange("(a b) d -> a (b d)", a=200),
                             x[rows].rearrange("(a b) d -> a (b d)", a=200)).then_inc(copied, DMA)
            sp.dma_start(nodes1[NODES:NODES + SLOTS].rearrange("(a b) d -> a (b d)", a=784),
                         x[0:SLOTS].rearrange("(a b) d -> a (b d)", a=784)).then_inc(copied, DMA)

            sp.wait_ge(sorting, SORT_STEPS)
            sorted_pairs(sorted_out, srcorder_in, key_ext[:], pay[:])

            with sp.Fori(1, CHUNKS // 2) as i:
                dist_load(2 * i, 0)
                dist_load(2 * i + 1, 1)

            rows_in = nodes1[0:NODES].rearrange("(p r) d -> p (r d)", p=FILL_P)
            rows_to = out.rearrange("(p r) d -> p (r d)", p=FILL_P)
            width = FILL_ROWS * FEAT

            def fill_load(m, b):
                sp.dma_start(fill[:, b], rows_in[:, bass.ds(m * width, width)]).then_inc(fill_in[b], DMA)

            def fill_store(m, b):
                sp.wait_ge(fill_added, m + 1)
                sp.dma_start(rows_to[:, bass.ds(m * width, width)], fill[:, b]).then_inc(fill_out[b], DMA)

            sp.wait_ge(carry_out[0], DMA)
            fill_load(0, 0)
            fill_load(1, 1)
            with sp.Fori(0, FILLS // 2 - 1) as i:
                for b in range(2):
                    fill_store(2 * i + b, b)
                    sp.wait_ge(fill_out[b], DMA * (i + 1))
                    fill_load(2 * i + 2 + b, b)
            for b in range(2):
                fill_store(FILLS - 2 + b, b)
            for b in range(2):
                sp.wait_ge(fill_out[b], DMA * FILLS // 2)
                sp.wait_ge(out_done[b], GATHERED * CHUNKS // 2)
            sp.wait_ge(carry_out[1], DMA)

        @block.gpsimd
        def _(pool):
            pool.memset(src_i[:], NODES).then_inc(prefilled, 1)
            pool.memset(dst_ext_i[:], NODES).then_inc(prefilled, 1)
            pool.wait_ge(prefilled, 2)
            pool.memset(dst_ext_i[0:1, 0:1], -1).then_inc(prefilled, 1)
            pool.memset(before[:], -1.0).then_inc(edge_vals, 1)
            pool.wait_ge(prefilled, 3)
            pool.wait_ge(edge_vals, 1)
            pool.memset(dist[:], 0.0).then_inc(prefilled, 1)
            pool.memset(vec[:], 1.0).then_inc(prefilled, 1)
            pool.memset(eps[:], EPS).then_inc(prefilled, 1)
            pool.wait_ge(prefilled, 6)
            pool.memset(hidden[HIDDEN:HIDDEN + 1], 1.0).then_inc(prefilled, 1)
            pool.wait_ge(prefilled, 7)
            bound = pool.to_reg(NODES - 1)
            count = [0]

            def stages(n, base, *copies):
                for k, (b, which, idx) in enumerate(copies):
                    pool.tensor_copy(stage[:, b, which], idx[:, chunk_cols(n)]).then_inc(staged, 1)
                pool.wait_ge(staged, base + len(copies) * (n + 1))
                pool.sem_inc(pool_turn, 1)

            pool.wait_ge(flagged, 1)
            with pool.If(pool.value_load(flag[:], min_val=0, max_val=1) > 0):
                pool.wait_ge(r_indexed, 1)
                pool.wait_ge(r_record_there, 1)

                def gather_records(n, b, rounds):
                    if not isinstance(n, int) or n >= 2:
                        pool.wait_ge(r_in[b], GATHERED * rounds)
                        pool.wait_ge(r_unpacked, n - 1)
                        pool.sem_inc(pool_turn, 1)
                    pool.tensor_copy(stage[:, b, 0], idx_out[:, chunk_cols(n)]).then_inc(r_staged, 1)
                    pool.wait_ge(r_staged, n + 1)
                    pool.sem_inc(pool_turn, 1)
                    for t in range(GROUP):
                        pool.indirect_dma_start(record_ring[:, b, t], None, records,
                                                bass.IndirectOffsetOnAxis(ap=stage[:, b, 0, t:t + 1], axis=0)
                                                ).then_inc(r_in[b], DMA)

                gather_records(0, 0, 0)
                gather_records(1, 1, 0)
                with pool.Fori(1, CHUNKS // 2) as i:
                    gather_records(2 * i, 0, i)
                    gather_records(2 * i + 1, 1, i)
                for b in range(2):
                    pool.wait_ge(r_in[b], GATHERED * CHUNKS // 2)

            pool.wait_ge(idx_src_ready, 1)

            def gather_x(n, b, rounds):
                if not isinstance(n, int) or n >= 2:
                    pool.wait_ge(x_in[b], GATHERED * rounds)
                    pool.wait_ge(x_saved, n - 1)
                pool.sem_inc(pool_turn, 1)
                stages(n, 0, (b, 0, idx_src))
                for t in range(GROUP):
                    pool.indirect_dma_start(xring[:, b, t], None, x,
                                            bass.IndirectOffsetOnAxis(ap=stage[:, b, 0, t:t + 1], axis=0)
                                            ).then_inc(x_in[b], DMA)

            gather_x(0, 0, 0)
            gather_x(1, 1, 0)
            with pool.Fori(1, CHUNKS // 2) as i:
                gather_x(2 * i, 0, i)
                gather_x(2 * i + 1, 1, i)

            pool.wait_ge(copied, (COPY_PARTS + 1) * DMA)
            for b in range(2):
                pool.wait_ge(x_in[b], GATHERED * CHUNKS // 2)
            pool.wait_ge(idx_ready, 1)

            def add_rows(n, b):
                stages(n, CHUNKS, (b, 0, idx_dst))
                pool.wait_ge(rows_ready, n + 1)
                pool.sem_inc(pool_turn, 1)
                for t in range(GROUP):
                    pool.indirect_dma_start(nodes1, bass.IndirectOffsetOnAxis(ap=stage[:, b, 0, t:t + 1], axis=0),
                                            rowring[:, b, t], None, compute_op=ALU.add).then_inc(rows_out[b], DMA)

            def add_rows_again(n, b, rounds):
                pool.wait_ge(rows_out[b], GATHERED * rounds)
                pool.sem_inc(pool_turn, 1)
                add_rows(n, b)

            add_rows(0, 0)
            add_rows(1, 1)
            with pool.Fori(1, CHUNKS // 2) as i:
                add_rows_again(2 * i, 0, i)
                add_rows_again(2 * i + 1, 1, i)

            for b in range(2):
                pool.wait_ge(rows_out[b], GATHERED * CHUNKS // 2)
            pool.wait_ge(carried, 1)
            pool.indirect_dma_start(nodes1, bass.IndirectOffsetOnAxis(ap=idx_carry[:, 0:1], axis=0), carry[:],
                                    None, compute_op=ALU.add).then_inc(carry_out[0], DMA)

            pool.wait_ge(carry_out[0], DMA)
            pool.wait_ge(idx_ready, 3)

            def gather_l(n, b, rounds):
                if not isinstance(n, int) or n >= 2:
                    pool.wait_ge(l_in[b], 2 * GATHERED * rounds)
                    pool.wait_ge(l_centered, n - 1)
                    pool.wait_ge(l_based, n - 1)
                pool.sem_inc(pool_turn, 1)
                stages(n, 2 * CHUNKS, (b, 0, idx_src), (b, 1, idx_dst_s))
                for k in range(2):
                    for t in range(GROUP):
                        pool.indirect_dma_start(lring[:, b, k * GROUP + t], None, nodes1,
                                                bass.IndirectOffsetOnAxis(ap=stage[:, b, k, t:t + 1], axis=0)
                                                ).then_inc(l_in[b], DMA)

            gather_l(0, 0, 0)
            gather_l(1, 1, 0)
            with pool.Fori(1, CHUNKS // 2) as i:
                gather_l(2 * i, 0, i)
                gather_l(2 * i + 1, 1, i)

            for b in range(2):
                pool.wait_ge(l_in[b], GATHERED * CHUNKS)
                pool.wait_ge(fill_out[b], DMA * FILLS // 2)
            pool.wait_ge(idx_ready, 4)

            def put_rows(n, b):
                stages(n, 4 * CHUNKS, (b, 0, idx_out))
                pool.wait_ge(out_rows, n + 1)
                pool.sem_inc(pool_turn, 1)
                for t in range(GROUP):
                    pool.indirect_dma_start(out, bass.IndirectOffsetOnAxis(ap=stage[:, b, 0, t:t + 1], axis=0),
                                            rowring[:, b, t], None, bounds_check=bound, oob_is_err=False
                                            ).then_inc(out_done[b], DMA)

            def put_rows_again(n, b, rounds):
                pool.wait_ge(out_done[b], GATHERED * rounds)
                pool.sem_inc(pool_turn, 1)
                put_rows(n, b)

            put_rows(0, 0)
            put_rows(1, 1)
            with pool.Fori(1, CHUNKS // 2) as i:
                put_rows_again(2 * i, 0, i)
                put_rows_again(2 * i + 1, 1, i)
            pool.wait_ge(holding, CHUNKS + 1)
            pool.indirect_dma_start(out, bass.IndirectOffsetOnAxis(ap=idx_carry[:, 1:2], axis=0), held[:], None,
                                    bounds_check=bound, oob_is_err=False).then_inc(carry_out[1], DMA)

        @block.scalar
        def _(act):
            def copy_payloads(steps_done, turned, copied_to, between=lambda k: None):
                turns = 0
                for k, (steps, half, after_turn) in enumerate(SORT_COPIES):
                    of = spay[:, half]
                    if after_turn:
                        turns += 1
                        of = psT[:, 0:SORT_COLS]
                        act.wait_ge(turned[1], turns)
                        act.activation(spay[:, half], of, ACT.Copy)
                    else:
                        act.wait_ge(steps_done, steps)
                    act.activation(spay[:, 1 - half], of, ACT.Copy).then_inc(copied_to, 1)
                    between(k)

            act.wait_ge(flagged, 1)
            with act.If(act.value_load(flag[:], min_val=0, max_val=1) > 0):
                copy_payloads(r_sorting, r_sort_turned, r_pay_copied)

            act.wait_ge(idx_src_ready, 1)
            act.wait_ge(edges_in, 6 * DMA)
            act.activation(vsq, vec[:], ACT.Square).then_inc(vsq_done, 1)
            act.wait_ge(dist_turned, 1)
            act.activation(distT[0:98], psT[0:98, 0:2 * P].rearrange("p (j c) -> p j c", j=2), ACT.Copy
                           ).then_inc(dist_copied, 1)

            def save_x(n, b, rounds):
                act.wait_ge(x_in[b], GATHERED * rounds)
                act.sem_inc(act_turn, 1)
                act.activation(x_src[:, chunk_cols(n)], xring[:, b], ACT.Copy).then_inc(x_saved, 1)

            def spread_mask(layer, sums, same, n, b):
                if not isinstance(n, int) or n >= 2:
                    act.wait_ge(summed_up[layer], n - 1)
                    act.sem_inc(act_turn, 1)
                act.activation(sums.mask[:, b, :, 1:], bc(same[:, bass.ds(n * GROUP + 1, GROUP - 1)], 1, FEAT),
                               ACT.Copy).then_inc(masked[layer], 1)

            def sum_rows(n, b, rounds):
                if not isinstance(rounds, int) or rounds > 0:
                    act.wait_ge(rows_out[b], GATHERED * rounds)
                act.wait_ge(summed_up[0], n + 1)
                act.activation(rowring[:, b], sums0.run[:, b].rearrange("p f t -> p t f"), ACT.Copy
                               ).then_inc(rows_ready, 1)

            def layer0_chunk(n, b, rounds):
                late = not isinstance(n, int) or n >= 2
                act.wait_ge(dist_bc[b], DMA * rounds)
                if late:
                    act.wait_ge(radial_ready, (n - 1) * GROUP)
                act.activation(hidden[0:HIDDEN, b], distb[:, b], ACT.Relu, bias=b1c[:], scale=w1c[:]
                               ).then_inc(hid_ready, 1)
                act.wait_ge(centered, n + 1)
                act.activation(sq[:, b], xc[:, b], ACT.Square).then_inc(squared, 1)
                act.wait_ge(varsummed, n + 1)
                act.activation(std[:, b, 0:GROUP], vsum[:, b, 0:GROUP], ACT.Sqrt, bias=eps[:], scale=1.0 / FEAT
                               ).then_inc(stded, 1)
                act.wait_ge(normed, n + 1)
                if late:
                    act.wait_ge(prod_done, (n - 1) * GROUP)
                f1 = h0[:, b, :, MUL:].rearrange("p t (v o) -> p t v o", o=3)
                act.activation(f1e[:, b, :, :, 0:3], f1, ACT.Copy)
                act.activation(f1e[:, b, :, :, 3:5], f1[:, :, :, 0:2], ACT.Copy)
                act.activation(z[:, b, :, 0:MUL], h0[:, b, :, 0:MUL], ACT.Copy)
                act.activation(V[:, b, :, 0:MUL], f1, ACT.Copy).then_inc(spread, 1)
                if late:
                    sum_rows(n - 2, b, rounds - 2)
                spread_mask(0, sums0, same_d, n, b)

            SAVE_AT = {24 + 13 * n: n for n in range(8)}

            def save_between(k):
                if k in SAVE_AT:
                    save_x(SAVE_AT[k], SAVE_AT[k] % 2, SAVE_AT[k] // 2 + 1)

            copy_payloads(sorting, sort_turned, pay_copied, save_between)
            act.wait_ge(vnorm, 1)
            act.activation(vn[:, 1], vn[:, 0], ACT.Sqrt).then_inc(vstd, 1)
            act.wait_ge(weights_in, 13 * DMA)
            act.wait_ge(prefilled, 6)
            act.wait_ge(idx_ready, 1)
            layer0_chunk(0, 0, 1)
            save_x(8, 0, 5)
            save_x(9, 1, 5)
            layer0_chunk(1, 1, 1)
            save_x(10, 0, 6)
            layer0_chunk(2, 0, 2)
            save_x(11, 1, 6)
            layer0_chunk(3, 1, 2)
            save_x(12, 0, 7)
            save_x(13, 1, 7)
            with act.Fori(2, CHUNKS // 2) as i:
                layer0_chunk(2 * i, 0, i + 1)
                layer0_chunk(2 * i + 1, 1, i + 1)
            sum_rows(CHUNKS - 2, 0, CHUNKS // 2 - 1)
            sum_rows(CHUNKS - 1, 1, CHUNKS // 2 - 1)

            def layer1_chunk(n, b):
                act.wait_ge(l_centered, n + 1)
                act.activation(lsq, lxc, ACT.Square).then_inc(l_squared, 1)
                act.wait_ge(l_varsummed, n + 1)
                act.activation(std[:, b], vsum[:, b], ACT.Sqrt, bias=eps[:], scale=1.0 / FEAT).then_inc(l_stded, 1)
                act.wait_ge(l_normed, n + 1)
                act.sem_inc(act_turn, 1)
                act.activation(hd[:, chunk_cols(n)], lh[:, b, GROUP:], ACT.Copy).then_inc(l_saved, 1)
                for g in range(4):
                    act.wait_ge(l_turned, n * 4 + g + 1)
                    if g >= 2:
                        act.wait_ge(l_logits, n * 4 + g - 1)
                    elif not isinstance(n, int) or n >= 1:
                        act.wait_ge(l_logits, n * 4 + g - 1)
                    act.activation(hT[:, g % 2], psM[:, g % 2, 0:2 * P], ACT.Copy).then_inc(l_hT, 1)

            layer1_chunk(0, 0)
            layer1_chunk(1, 1)
            with act.Fori(1, CHUNKS // 2) as i:
                layer1_chunk(2 * i, 0)
                layer1_chunk(2 * i + 1, 1)

            act.wait_ge(shifted, 1)
            act.activation(soft[:, 3], soft[:, 2], ACT.Exp).then_inc(s_exp, 1)

            def mix_chunk(n, b):
                for g in range(4):
                    width = P * min(4, GROUP - 4 * g)
                    act.wait_ge(m_turned, n * 4 + g + 1)
                    if g >= 2 or not isinstance(n, int) or n >= 1:
                        act.wait_ge(m_mixed, n * 4 + g - 1)
                    act.activation(wT[:, g % 2, 0:width], psM[:, g, 0:width], ACT.Copy).then_inc(m_wT, 1)
                act.wait_ge(m_mixed, n * 4 + 4)
                if not isinstance(n, int) or n >= 2:
                    act.wait_ge(summed_up[1], n - 1)
                act.activation(sums1.terms[:, b], psR[:, b, 0:GROUP * FEAT].rearrange("p (t f) -> p f t", f=FEAT),
                               ACT.Copy).then_inc(m_out, 1)
                spread_mask(1, sums1, same, n, b)

            act.wait_ge(weighed, 1)
            mix_chunk(0, 0)
            mix_chunk(1, 1)
            with act.Fori(1, CHUNKS // 2) as i:
                mix_chunk(2 * i, 0)
                mix_chunk(2 * i + 1, 1)

        @block.tensor
        def _(pe):
            pe.wait_ge(sorters_in, 2 * DMA)
            pe.wait_ge(compared, 1)
            pe.transpose(psT[0:1, 0:P], unsorted[:], ident[:]).then_inc(flag_turned, 1)

            def sort_turns(steps_done, turned):
                for key_steps, pay_steps, half in SORT_TURNS:
                    for what, (data, steps) in enumerate(((skey, key_steps), (spay, pay_steps))):
                        pe.wait_ge(steps_done, steps)
                        for k in range(2):
                            turn = pe.transpose((psX, psT)[what][:, k * P:(k + 1) * P],
                                                data[:, half, k * P:(k + 1) * P], ident[:])
                        turn.then_inc(turned[what], 1)

            pe.wait_ge(flagged, 1)
            with pe.If(pe.value_load(flag[:], min_val=0, max_val=1) > 0):
                sort_turns(r_sorting, r_sort_turned)
            pe.wait_ge(idx_src_ready, 1)
            pe.wait_ge(edges_in, 6 * DMA)
            for j in range(2):
                turn = pe.transpose(psT[0:98, j * P:(j + 1) * P], dist[:, 98 * j:98 * j + 98], ident[:])
            turn.then_inc(dist_turned, 1)
            pe.wait_ge(dist_copied, 1)
            sort_turns(sorting, sort_turned)
            pe.wait_ge(w2_ready, 1)
            pe.wait_ge(prefilled, 7)

            LAG = 2
            STEPS24 = [24 * t // HALF for t in range(HALF + 1)]

            def radial(n, b, h, t):
                k = h * HALF + t
                if k == 0:
                    pe.wait_ge(hid_ready, n + 1)
                if not isinstance(n, int) or n * GROUP + k >= 4:
                    pe.wait_ge(prod_done, n * GROUP + k - 3)
                pe.matmul(psM[:, (b * GROUP + k) % 4, 0:RADIAL], hidden[:, b, k * P:(k + 1) * P], w2p[:],
                          start=True, stop=True).then_inc(radial_ready, 1)

            def reduce(hh, par, t):
                if t == 0:
                    pe.wait_ge(preadded, hh + 1)
                    if not isinstance(hh, int) or hh >= 2:
                        pe.wait_ge(posted, hh - 1)
                for k in range(STEPS24[t], STEPS24[t + 1]):
                    if k < W16:
                        mm = pe.matmul(psR[:, par, 0:HALF * W16], ident[:], prodA[:, par, :, k],
                                       start=(k == 0), stop=(k == W16 - 1))
                    else:
                        mm = pe.matmul(psR[:, par, HALF * W16:HALF * (W16 + 3 * MUL)], ident[:],
                                       prodB[:, par, :, k - W16], start=(k == W16), stop=(k == 23))
                if t == HALF - 1:
                    mm.then_inc(reduced, 1)

            def layer0_chunk(n, b):
                for h in range(2):
                    for t in range(HALF):
                        radial(n, b, h, t)
                        if t >= LAG:
                            hh, par, part = 2 * n + h - 1, 1 - h, t - LAG
                        else:
                            hh, par, part = 2 * n + h - 2, h, t - LAG + HALF
                        if not isinstance(hh, int) or hh >= 0:
                            reduce(hh, par, part)

            layer0_chunk(0, 0)
            layer0_chunk(1, 1)
            with pe.Fori(1, CHUNKS // 2) as i:
                layer0_chunk(2 * i, 0)
                layer0_chunk(2 * i + 1, 1)
            for t in range(HALF - LAG, HALF):
                reduce(2 * CHUNKS - 2, 0, t)
            for t in range(HALF):
                reduce(2 * CHUNKS - 1, 1, t)

            def join_runs(step):
                pe.wait_ge(ended, step + 1)
                pe.transpose(psT[0:FEAT, 0:P], lend[:], ident[:])
                pe.transpose(psT[0:FEAT, P:2 * P], openrep[:], ident[:]).then_inc(ends_turned, 1)
                pe.wait_ge(chained, step + 1)
                pe.transpose(psT[:, 2 * P:2 * P + FEAT], chain[:, 0:P], ident[0:FEAT, 0:FEAT]).then_inc(ends_turned, 1)

            join_runs(0)

            pe.wait_ge(lweights, 1)

            def logits_chunk(n, b):
                starts = (0, 4, 8, GROUP - 4)
                pe.wait_ge(l_normed, n + 1)

                def turn(g):
                    if g >= 2 or not isinstance(n, int) or n >= 1:
                        pe.wait_ge(l_hT, n * 4 + g - 1)
                    for k in range(2):
                        a = lh[:, b, k * GROUP + starts[g]:k * GROUP + starts[g] + 4]
                        t = pe.transpose(psM[:, g % 2, k * P:(k + 1) * P], a.rearrange("p t f -> p (t f)"), ident[:])
                    t.then_inc(l_turned, 1)

                def mix(g):
                    if g == 0 and (not isinstance(n, int) or n >= 2):
                        pe.wait_ge(l_biased, n - 1)
                    pe.wait_ge(l_hT, n * 4 + g + 1)
                    for k in range(2):
                        mm = pe.matmul(psR[:, b, HEADS * starts[g]:HEADS * (starts[g] + 4)],
                                       hT[:, g % 2, k * P:(k + 1) * P], ublk[:, k], start=(k == 0), stop=(k == 1))
                    mm.then_inc(l_logits, 1)

                turn(0)
                for g in range(4):
                    if g < 3:
                        turn(g + 1)
                    mix(g)

            logits_chunk(0, 0)
            logits_chunk(1, 1)
            with pe.Fori(1, CHUNKS // 2) as i:
                logits_chunk(2 * i, 0)
                logits_chunk(2 * i + 1, 1)

            for turn in range(4):
                pe.wait_ge(joining, turn + 1)
                if turn % 2 == 0:
                    for k in range(4):
                        t = pe.transpose(psT[0:HEADS, k * P:(k + 1) * P], ends[:, k], ident[:])
                else:
                    for k in range(2):
                        t = pe.transpose(psT[:, k * HEADS:(k + 1) * HEADS], ladder[:, k, k:k + P],
                                         ident[0:HEADS, 0:HEADS])
                t.then_inc(s_turned, 1)

            def mix_chunk(n, b):
                pe.wait_ge(weighed, n + 1)

                def turn(g):
                    if not isinstance(n, int) or n >= 1:
                        pe.wait_ge(m_wT, n * 4 + g - 3)
                    for k in range(4 * g, min(4 * g + 4, GROUP)):
                        t = pe.transpose(psM[:, g, (k - 4 * g) * P:(k - 4 * g + 1) * P], weighted[:, b, k], ident[:])
                    t.then_inc(m_turned, 1)

                def mix(g):
                    if g == 0 and (not isinstance(n, int) or n >= 2):
                        pe.wait_ge(m_out, n - 1)
                    pe.wait_ge(m_wT, n * 4 + g + 1)
                    for k in range(4 * g, min(4 * g + 4, GROUP)):
                        mm = pe.matmul(psR[:, b, k * FEAT:(k + 1) * FEAT], wT[:, g % 2, (k - 4 * g) * P:(k - 4 * g + 1) * P],
                                       wstk[:], start=True, stop=True)
                    mm.then_inc(m_mixed, 1)

                turn(0)
                for g in range(4):
                    if g < 3:
                        turn(g + 1)
                    mix(g)

            mix_chunk(0, 0)
            mix_chunk(1, 1)
            with pe.Fori(1, CHUNKS // 2) as i:
                mix_chunk(2 * i, 0)
                mix_chunk(2 * i + 1, 1)
            join_runs(1)

        @block.vector
        def _(dve):
            st = Steps(dve, prep)
            TT, TS, STT = dve.tensor_tensor, dve.tensor_scalar, dve.scalar_tensor_tensor

            def late(n, first=2):
                return not isinstance(n, int) or n >= first

            st.do(dve.memset(ones32[:], 1.0))
            st.do(dve.memset(chain[:, 0:1], 0.0))
            dve.wait_ge(ids_in, 7 * DMA)
            dve.tensor_copy(src_f[:], src_i[:]).then_inc(floats, 1)
            dve.tensor_copy(dst_ext[:], dst_ext_i[:]).then_inc(floats, 1)
            dve.tensor_copy(dst_f[:], dst_ext_i[:, 1:COLS + 1]).then_inc(floats, 1)
            dve.wait_ge(floats, 3)
            st.link(TT(idx_tmp[:], dst_ext[:, 1:COLS + 1], dst_ext[:, 2:], ALU.is_gt))
            dve.tensor_reduce(unsorted[:], idx_tmp[:], AX.X, ALU.max).then_inc(compared, 1)
            dve.wait_ge(flag_turned, 1)
            st.link(dve.tensor_reduce(unsorted_1[:], psT[0:1, 0:P], AX.X, ALU.max))
            dve.tensor_copy(flag[:], unsorted_1[:]).then_inc(flagged, 1)

            def sort_pairs(so, turned, pay_copies):
                half = turns = compares = 0
                for kind, arg in SORT_PLAN:
                    key, load = skey[:, half], spay[:, half]
                    if kind == "flip":
                        so.settle()
                        for a, factor in flips_of(arg, key):
                            so.do(TS(a, a, -1.0 if factor is None else flip[:, factor:factor + 1], None, ALU.mult))
                        so.settle()
                    elif kind == "turn":
                        turns += 1
                        dve.wait_ge(turned[0], turns)
                        so.link(dve.tensor_copy(key, psX[:, 0:SORT_COLS]))
                    else:
                        def pair(a):
                            v = a.rearrange("p (m two d) -> p m two d", two=2, d=arg)
                            return v[:, :, 0], v[:, :, 1]

                        (ka, kb), (ko, kp) = pair(key), pair(skey[:, 1 - half])
                        g = swaps[:, half].rearrange("p (m d) -> p m d", d=arg)
                        to = spay[:, 1 - half].rearrange("p (m two d) -> p m two d", two=2, d=arg)
                        of = load.rearrange("p (m two d) -> p m two d", two=2, d=arg)
                        n0 = so.n
                        dve.wait_ge(so.s, n0 - 1)
                        so.do(TT(g, ka, kb, ALU.is_gt))
                        so.do(TT(ko, ka, kb, ALU.min))
                        so.do(TT(kp, ka, kb, ALU.max))
                        dve.wait_ge(so.s, n0 + 1)
                        compares += 1
                        dve.wait_ge(pay_copies, compares)
                        so.do(dve.copy_predicated(to, bc(g, 2, 2), of[:, :, ::-1]))
                        half = 1 - half
                assert so.n == SORT_STEPS and half == SORT_END

            dve.wait_ge(sorters_in, 2 * DMA)
            dve.wait_ge(flagged, 1)
            with dve.If(dve.value_load(flag[:], min_val=0, max_val=1) > 0):
                dve.wait_ge(edges_in, 6 * DMA)
                dve.wait_ge(weights_in, 13 * DMA)
                rs = Steps(dve, r_sorting)
                rs.do(dve.tensor_copy(skey[:, 0, 0:COLS], dst_f[:]))
                rs.do(dve.memset(skey[:, 0, COLS:], float(NODES)))
                rs.do(TS(spay[:, 0, 0:COLS], pos[:], float(NODES), None, ALU.subtract))
                rs.do(dve.memset(spay[:, 0, COLS:], float(SLOTS - 1)))
                dve.memset(record[:, :, 5:], 0.0)
                dve.tensor_copy(record[:, :, 0], src_f[:])
                dve.tensor_copy(record[:, :, 1], dist[:])
                dve.tensor_copy(record[:, :, 2:5], vec[:]).then_inc(r_built, 1)
                sort_pairs(rs, r_sort_turned, r_pay_copied)
                dve.wait_ge(r_order_in, 2 * DMA)
                dve.tensor_copy(dst_f[:], dst_ext[:, 1:COLS + 1])
                dve.tensor_copy(idx_out[:], pay[:]).then_inc(r_indexed, 1)
                dve.wait_ge(r_record_there, 1)

                def unpack(n, b, rounds):
                    dve.wait_ge(r_in[b], GATHERED * rounds)
                    TS(record[:, chunk_cols(n)], record_ring[:, b], 1.0, None, ALU.mult).then_inc(r_unpacked, 1)

                with dve.Fori(0, CHUNKS // 2) as i:
                    unpack(2 * i, 0, i + 1)
                    unpack(2 * i + 1, 1, i + 1)
                dve.wait_ge(r_unpacked, CHUNKS)
                dve.tensor_copy(dist[:], record[:, :, 1])
                dve.tensor_copy(vec[:], record[:, :, 2:5])
                dve.tensor_copy(src_f[:], record[:, :, 0]).then_inc(r_unpacked, 1)
                dve.wait_ge(r_unpacked, CHUNKS + 1)
            TS(idx_src[:], src_f[:], float(NODES - 1), None, ALU.min).then_inc(idx_src_ready, 1)
            so = Steps(dve, sorting)
            so.do(dve.tensor_copy(skey[:, 0, 0:COLS], src_f[:]))
            so.do(dve.memset(skey[:, 0, COLS:], float(NODES)))
            so.do(dve.tensor_copy(spay[:, 0, 0:COLS], dst_f[:]))
            so.do(dve.memset(spay[:, 0, COLS:], float(NODES)))
            sort_pairs(so, sort_turned, pay_copied)

            dve.wait_ge(vsq_done, 1)
            dve.tensor_reduce(vn[:, 0], vsq, AX.X, ALU.add).then_inc(vnorm, 1)


            def block_of(k, n=1):
                a = w2raw[:, k * MUL * MUL:(k + n) * MUL * MUL]
                return a.rearrange("p (u v k) -> p k v u", v=MUL, k=n)

            dve.wait_ge(weights_in, 13 * DMA)
            m01 = w2p[:, 0:NA].rearrange("p (w u) -> p w u", u=W16)
            m23 = w2p[:, NA:].rearrange("p (w u) -> p w u", u=MUL)
            TS(m01[:, 0:MUL, 0:MUL], block_of(0)[:, 0], K_00, None, ALU.mult)
            TS(m01[:, MUL:, 0:MUL], block_of(1)[:, 0], K_01, None, ALU.mult)
            TS(m01[:, 0:MUL, MUL:], block_of(2)[:, 0], K_10, None, ALU.mult)
            TS(m01[:, MUL:, MUL:], block_of(3, 3)[:, 2], K_112R, None, ALU.mult)
            TS(m23[:, MUL:], block_of(3, 3)[:, 1], K_111, None, ALU.mult)
            st.link(TS(w2t[:], block_of(3, 3)[:, 2], K_112I, None, ALU.mult))
            STT(m23[:, 0:MUL], block_of(3, 3)[:, 0], K_110, w2t[:], ALU.mult, ALU.add).then_inc(w2_ready, 1)
            dve.wait_ge(vstd, 1)
            st.link(dve.reciprocal(vn[:, 2], vn[:, 1]))
            st.do(TT(r5[:, :, 0:2], vec[:, :, 1:3], bc(vn[:, 2], 2, 2), ALU.mult))
            st.link(TT(r5[:, :, 2:5], vec[:], bc(vn[:, 2], 2, 3), ALU.mult))

            def segments(ext, same, last, opened):
                TT(same, ext[:, 1:COLS + 1], ext[:, 0:COLS], ALU.is_equal)
                st.link(TT(last, ext[:, 1:COLS + 1], ext[:, 2:], ALU.not_equal))
                st.link(dve.tensor_tensor_scan(opened, same, same, 1.0, ALU.mult, ALU.mult))

            segments(dst_ext, same_d[:], last[:], opened[:])
            TT(idx_tmp[:], dst_f[:], pos[:], ALU.subtract)
            TT(ends_in[:], opened[:], last[:], ALU.mult)
            st.link(TS(openrep[:], ones32[:], opened[:, COLS - 1:], None, ALU.mult))
            st.do(dve.tensor_reduce(crosses[:, 0:1], ends_in[:], AX.X, ALU.max))
            st.link(TT(idx_tmp[:], idx_tmp[:], last[:], ALU.mult))
            TT(idx_dst[:], idx_tmp[:], pos[:], ALU.add).then_inc(idx_ready, 1)
            st.link(TT(picked[:, 0:1], dst_f[:, 0:1], pos[:, 0:1], ALU.subtract))
            st.do(STT(idx_carry[:, 0:1], picked[:, 0:1], crosses[:, 0:1], pos[:, 0:1], ALU.mult, ALU.add))
            st.do(dve.memset(sums0.mask[:, :, :, 0:1], 0.0))

            def row_sums(n, b):
                dve.tensor_reduce(lsum[:, b, 0:GROUP], x_src[:, chunk_cols(n)], AX.X, ALU.add).then_inc(summed, 1)

            def row_means(n, b):
                dve.wait_ge(summed, n + 1)
                TS(mean[:, b, 0:GROUP], lsum[:, b, 0:GROUP], 1.0 / FEAT, None, ALU.mult).then_inc(meaned, 1)

            def center(n, b):
                dve.wait_ge(meaned, n + 1)
                TT(xc[:, b], x_src[:, chunk_cols(n)], bc(mean[:, b, 0:GROUP], 2, FEAT), ALU.subtract
                   ).then_inc(centered, 1)

            def deviate(n, b):
                dve.wait_ge(squared, n + 1)
                dve.tensor_reduce(vsum[:, b, 0:GROUP], sq[:, b], AX.X, ALU.add).then_inc(varsummed, 1)

            def invert(n, b):
                dve.wait_ge(stded, n + 1)
                dve.reciprocal(rstd[:, b, 0:GROUP], std[:, b, 0:GROUP]).then_inc(rstded, 1)

            def norm(n, b):
                dve.wait_ge(rstded, n + 1)
                STT(h0[:, b], xc[:, b], 0.0, bc(rstd[:, b, 0:GROUP], 2, FEAT), ALU.max, ALU.mult).then_inc(normed, 1)

            def dot(n, b):
                dve.wait_ge(normed, n + 1)
                f1 = h0[:, b, :, MUL:].rearrange("p t (v o) -> p t v o", o=3)
                TT(crs[:, 2], f1, bc(r5[:, chunk_cols(n), 0:3], 2, MUL), ALU.mult).then_inc(dotp, 1)

            def cross(n, b):
                dve.wait_ge(spread, n + 1)
                TT(crs[:, 0], f1e[:, b, :, :, 2:5], bc(r5[:, chunk_cols(n), 1:4], 2, MUL), ALU.mult)
                TT(crs[:, 1], f1e[:, b, :, :, 1:4], bc(r5[:, chunk_cols(n), 2:5], 2, MUL), ALU.mult
                   ).then_inc(crossed, 1)

            def operands(n, b):
                dve.wait_ge(dotp, n + 1)
                dve.tensor_reduce(z[:, b, :, MUL:], crs[:, 2], AX.X, ALU.add).then_inc(dotted, 1)
                dve.wait_ge(crossed, n + 1)
                TT(V[:, b, :, MUL:], crs[:, 0], crs[:, 1], ALU.subtract).then_inc(vectored, 1)

            def products(n, b, h, between=()):
                if h == 0:
                    dve.wait_ge(dotted, n + 1)
                    dve.wait_ge(vectored, n + 1)
                if late(n, 1):
                    dve.wait_ge(reduced, 2 * n + h - 1)
                for t in range(HALF):
                    k = h * HALF + t
                    bank = (b * GROUP + k) % 4
                    dve.wait_ge(radial_ready, n * GROUP + k + 1)
                    TT(prodA[:, h, t], psM[:, bank, 0:NA].rearrange("p (w u) -> p w u", u=W16),
                       bc(z[:, b, k], 2, W16), ALU.mult)
                    TT(prodB[:, h, t].rearrange("p w (u o) -> p w u o", o=3),
                       bc(psM[:, bank, NA:RADIAL].rearrange("p (w u) -> p w u", u=MUL), 3, 3),
                       bc(V[:, b, k], 2, MUL), ALU.mult).then_inc(prod_done, 1)
                    if t < len(between) and between[t]:
                        between[t]()
                dve.wait_ge(prod_done, n * GROUP + h * HALF + HALF)
                TT(prodB[:, h, :, 0:MUL], prodB[:, h, :, 0:MUL], prodB[:, h, :, MUL:], ALU.add).then_inc(preadded, 1)

            def post(n, b, h):
                dve.wait_ge(reduced, 2 * n + h + 1)
                cols = bass.ds(n * GROUP + h * HALF, HALF)
                terms = sums0.terms[:, b, :, h * HALF:(h + 1) * HALF]
                a = psR[:, h, 0:HALF * W16].rearrange("p (t u) -> p t u", u=W16)
                v = psR[:, h, HALF * W16:HALF * (W16 + 3 * MUL)].rearrange("p (t f) -> p f t", f=3 * MUL)
                TT(qr[:, h], bc(a[:, :, MUL:], 3, 3), bc(r5[:, cols, 0:3], 2, MUL), ALU.mult).then_inc(q_done, 1)
                TS(terms[:, 0:MUL], a[:, :, 0:MUL].rearrange("p t u -> p u t"), 1.0, None, ALU.mult)
                dve.wait_ge(q_done, 2 * n + h + 1)
                TT(terms[:, MUL:], qr[:, h].rearrange("p t v o -> p (v o) t"), v, ALU.add).then_inc(posted, 1)

            def join_chunk(layer, sums, same, n, b):
                if late(n, 1):
                    dve.wait_ge(summed_up[layer], n)
                    STT(sums.terms[:, b, :, 0], sums.run[:, 1 - b, :, GROUP - 1], same[:, bass.ds(n * GROUP, 1)],
                        sums.terms[:, b, :, 0], ALU.mult, ALU.add).then_inc(joined[layer], 1)

            def run_sums(layer, sums, n, b):
                if late(n, 1):
                    dve.wait_ge(joined[layer], n)
                dve.wait_ge(masked[layer], n + 1)
                dve.tensor_tensor_scan(sums.flat[1][:, b], sums.flat[2][:, b], sums.flat[0][:, b], 0.0,
                                       ALU.mult, ALU.add).then_inc(summed_up[layer], 1)

            def sum_terms0(n, b):
                dve.wait_ge(posted, 2 * n + 2)
                join_chunk(0, sums0, same_d, n, b)

            def sum_chunk0(n, b):
                if late(n):
                    dve.wait_ge(rows_ready, n - 1)
                run_sums(0, sums0, n, b)

            def layer0_step(n, b, prepare=True, back=True):
                products(n - 1, 1 - b, 0, (
                    prepare and (lambda: row_sums(n, b)), prepare and (lambda: row_means(n, b)),
                    prepare and (lambda: center(n, b)), back and (lambda: post(n - 2, b, 0)),
                ))
                products(n - 1, 1 - b, 1, (
                    prepare and (lambda: deviate(n, b)), back and (lambda: post(n - 2, b, 1)),
                    prepare and (lambda: invert(n, b)), prepare and (lambda: norm(n, b)),
                    back and (lambda: sum_terms0(n - 2, b)), prepare and (lambda: dot(n, b)),
                    back and (lambda: sum_chunk0(n - 2, b)),
                ))
                if prepare:
                    cross(n, b)
                    operands(n, b)

            dve.wait_ge(x_saved, 1)
            for step in (row_sums, row_means, center, deviate, invert, norm, dot, cross, operands):
                step(0, 0)
            dve.wait_ge(x_saved, 2)
            layer0_step(1, 1, back=False)
            dve.wait_ge(x_saved, 3)
            layer0_step(2, 0)
            dve.wait_ge(x_saved, 4)
            layer0_step(3, 1)
            dve.wait_ge(x_saved, CHUNKS)
            with dve.Fori(2, CHUNKS // 2) as i:
                layer0_step(2 * i, 0)
                layer0_step(2 * i + 1, 1)
            layer0_step(CHUNKS, 0, prepare=False)
            for h in range(2):
                post(CHUNKS - 1, 1, h)
            sum_terms0(CHUNKS - 1, 1)
            sum_chunk0(CHUNKS - 1, 1)

            def carry_over(layer, sums):
                dve.wait_ge(summed_up[layer], CHUNKS)
                dve.tensor_copy(lend[:], sums.run[:, 1, :, GROUP - 1]).then_inc(ended, 1)
                dve.wait_ge(ends_turned, 2 * layer + 1)
                st.link(dve.tensor_copy(openT[:], psT[0:FEAT, P:2 * P]))
                dve.tensor_tensor_scan(chain[:, 1:], openT[:], psT[0:FEAT, 0:P], 0.0, ALU.mult, ALU.add
                                       ).then_inc(chained, 1)
                dve.wait_ge(ends_turned, 2 * layer + 2)
                dve.tensor_copy(carry[:], psT[:, 2 * P:2 * P + FEAT]).then_inc(carried, 1)

            carry_over(0, sums0)

            for k in range(2):
                st.do(TT(wmul[:, k], wrep[:], bc(fcw_b[:, k * FEAT:(k + 1) * FEAT], 1, HEADS), ALU.mult))
            st.do(dve.memset(ublk[:], 0.0))
            st.link(TS(wstk[:], wstk_raw[:], 1.0 / HEADS, None, ALU.mult))
            st.link(dve.tensor_reduce(u_all[:], wmul[:], AX.X, ALU.add))
            for k in range(2):
                for t in range(4):
                    put = dve.tensor_copy(ublk[32 * t:32 * t + 32, k, HEADS * t:HEADS * (t + 1)],
                                          u_all[32 * t:32 * t + 32, k])
            put.then_inc(lweights, 1)

            dve.wait_ge(srcorder_in, 2 * DMA)
            key = key_ext[:, 1:COLS + 1]
            dve.tensor_copy(idx_src[:], key).then_inc(idx_ready, 1)
            dve.tensor_copy(idx_dst_s[:], pay[:]).then_inc(idx_ready, 1)
            segments(key_ext, same[:], last[:], opened[:])
            st.link(TT(more[:], key, key_ext[:, 2:], ALU.is_equal))
            st.do(TS(negs[:, 0], same[:], 1.0, BIG, ALU.subtract, ALU.mult))
            st.do(TS(negs[:, 1], last[:], -BIG, None, ALU.mult))
            st.link(TT(ends_in[:], opened[:], last[:], ALU.mult))
            st.do(dve.tensor_reduce(crosses[:, 1:2], ends_in[:], AX.X, ALU.max))
            st.do(TT(idx_tmp[:], last[:], ends_in[:], ALU.subtract))
            st.link(dve.tensor_tensor_scan(openR[:, ::-1], more[:, ::-1], more[:, ::-1], 1.0, ALU.mult, ALU.mult))
            st.link(TS(idx_tmp[:], idx_tmp[:], 1.0, -2.0 * NODES, ALU.subtract, ALU.mult))
            st.do(TS(picked[:, 0:1], crosses[:, 1:2], 1.0, -2.0 * NODES, ALU.subtract, ALU.mult))
            TT(idx_out[:], idx_tmp[:], key, ALU.add).then_inc(idx_ready, 1)
            st.settle()
            st.do(TT(idx_carry[:, 1:2], picked[:, 0:1], key[:, 0:1], ALU.add))
            st.do(TS(openrep[:], ones32[:], opened[:, COLS - 1:], None, ALU.mult))
            st.do(TS(negopen[:, 0], opened[:], 1.0, BIG, ALU.subtract, ALU.mult))
            st.link(TS(negopen[:, 1], openR[:], 1.0, BIG, ALU.subtract, ALU.mult))

            def layer1_chunk(n, b, rounds, filling):
                dve.wait_ge(l_in[b], 2 * GATHERED * rounds)
                dve.tensor_reduce(lsum[:, b], lring[:, b], AX.X, ALU.add).then_inc(l_summed, 1)
                dve.wait_ge(l_summed, n + 1)
                TS(mean[:, b], lsum[:, b], 1.0 / FEAT, None, ALU.mult).then_inc(l_meaned, 1)
                dve.wait_ge(l_meaned, n + 1)
                TT(lxc, lring[:, b], bc(mean[:, b], 2, FEAT), ALU.subtract).then_inc(l_centered, 1)
                TT(xsb[:, chunk_cols(n)], lring[:, b, 0:GROUP], bc(bias_b[:], 1, GROUP), ALU.add).then_inc(l_based, 1)
                if filling:
                    rows = fill[:, b].rearrange("p (r d) -> p r d", d=FEAT)
                    dve.wait_ge(fill_in[b], DMA * rounds)
                    TT(rows, rows, bc(bias_b[0:FILL_P], 1, FILL_ROWS), ALU.add).then_inc(fill_added, 1)
                dve.wait_ge(l_squared, n + 1)
                dve.tensor_reduce(vsum[:, b], lsq, AX.X, ALU.add).then_inc(l_varsummed, 1)
                dve.wait_ge(l_stded, n + 1)
                dve.reciprocal(rstd[:, b], std[:, b]).then_inc(l_rstded, 1)
                dve.wait_ge(l_rstded, n + 1)
                if late(n):
                    dve.wait_ge(l_saved, n - 1)
                    dve.wait_ge(l_turned, 4 * (n - 1))
                STT(lh[:, b], lxc, 0.0, bc(rstd[:, b], 2, FEAT), ALU.max, ALU.mult).then_inc(l_normed, 1)
                dve.wait_ge(l_logits, 4 * (n + 1))
                TS(lgt[:], psR[:, b, 0:GROUP * HEADS], fcb_b[:], None, ALU.add).then_inc(l_biased, 1)
                dve.wait_ge(l_biased, n + 1)
                STT(E[:, chunk_cols(n)].rearrange("p t h -> p (t h)"), lgt[:], 0.2, lgt[:], ALU.mult, ALU.max
                    ).then_inc(l_logged, 1)

            layer1_chunk(0, 0, 1, True)
            layer1_chunk(1, 1, 1, True)
            with dve.Fori(1, FILLS // 2) as i:
                for b in range(2):
                    layer1_chunk(2 * i + b, b, i + 1, True)
            with dve.Fori(FILLS // 2, CHUNKS // 2) as i:
                for b in range(2):
                    layer1_chunk(2 * i + b, b, i + 1, False)
            dve.wait_ge(l_logged, CHUNKS)

            left, right, tmp, prob = (soft[:, k] for k in range(4))

            def both_ways(step, data, mask_l, mask_r, open_l, open_r, start, op0, op1):
                for h in range(HEADS):
                    dve.tensor_tensor_scan(left[:, :, h], mask_l, data[:, :, h], start, op0, op1)
                for h in range(HEADS):
                    scan = dve.tensor_tensor_scan(right[:, ::-1, h], mask_r[:, ::-1], data[:, ::-1, h],
                                                  start, op0, op1)
                st.do(scan)
                st.do(dve.memset(ladder[:, 0, 0:1], start))
                st.do(dve.memset(ladder[:, 1, P:], start))
                st.do(TS(ends[:, 1], ones32[:, 0:HEADS], open_l[:, COLS - 1:], None, ALU.mult))
                st.do(TS(ends[:, 3], ones32[:, 0:HEADS], open_r[:, 0:1], None, ALU.mult))
                st.settle()
                dve.tensor_copy(ends[:, 0], left[:, COLS - 1])
                dve.tensor_copy(ends[:, 2], right[:, 0]).then_inc(joining, 1)
                dve.wait_ge(s_turned, 2 * step + 1)
                st.do(dve.tensor_copy(endT[:, 0], psT[0:HEADS, P:2 * P]))
                st.link(dve.tensor_copy(endT[:, 1], psT[0:HEADS, 3 * P:]))
                dve.tensor_tensor_scan(ladder[:, 0, 1:], endT[:, 0], psT[0:HEADS, 0:P], start, op0, op1)
                dve.tensor_tensor_scan(ladder[:, 1, 0:P][:, ::-1],
                                       endT[:, 1, ::-1], psT[0:HEADS, 2 * P:3 * P][:, ::-1],
                                       start, op0, op1).then_inc(joining, 1)
                dve.wait_ge(s_turned, 2 * step + 2)
                st.link(dve.tensor_copy(join[:], psT[:, 0:2 * HEADS].rearrange("p (k h) -> p k h", k=2)))

            def add_join(k, opens, op0, op1):
                st.link(TT(tmp, bc(join[:, k], 1, COLS), bc(opens, 2, HEADS), op0))
                st.link(TT(left, left, tmp, op1))

            both_ways(0, E, negs[:, 0], negs[:, 1], negopen[:, 0], negopen[:, 1], -BIG, ALU.add, ALU.max)
            st.link(TT(left, left, right, ALU.max))
            add_join(0, negopen[:, 0], ALU.add, ALU.max)
            add_join(1, negopen[:, 1], ALU.add, ALU.max)
            TT(tmp, E, left, ALU.subtract).then_inc(shifted, 1)
            dve.wait_ge(s_exp, 1)
            both_ways(1, prob, same[:], more[:], opened[:], openR[:], 0.0, ALU.mult, ALU.add)
            st.link(TT(right, right, prob, ALU.subtract))
            st.link(TT(left, left, right, ALU.add))
            add_join(0, opened[:], ALU.mult, ALU.add)
            add_join(1, openR[:], ALU.mult, ALU.add)
            st.link(dve.reciprocal(right, left))
            st.link(TT(prob, prob, right, ALU.mult))

            def weigh(n, b):
                if late(n):
                    dve.wait_ge(m_turned, 4 * (n - 1))
                TT(weighted[:, b].rearrange("p t (h f) -> p t h f", h=HEADS), bc(hd[:, chunk_cols(n)], 2, HEADS),
                   bc(prob[:, chunk_cols(n)], 3, FEAT), ALU.mult).then_inc(weighed, 1)

            def finish(n, b, rounds):
                dve.wait_ge(m_out, n + 1)
                join_chunk(1, sums1, same, n, b)
                run_sums(1, sums1, n, b)
                if not isinstance(rounds, int) or rounds > 0:
                    dve.wait_ge(out_done[b], GATHERED * rounds)
                dve.wait_ge(summed_up[1], n + 1)
                TT(rowring[:, b], sums1.run[:, b].rearrange("p f t -> p t f"), xsb[:, chunk_cols(n)], ALU.add
                   ).then_inc(out_rows, 1)
                dve.wait_ge(out_rows, n + 1)
                TT(picks, rowring[:, b].rearrange("p t f -> p f t"), bc(ends_in[:, chunk_cols(n)], 1, FEAT), ALU.mult
                   ).then_inc(multiplied, 1)
                dve.wait_ge(multiplied, n + 1)
                dve.tensor_reduce(picked[:], picks, AX.X, ALU.add).then_inc(picking, 1)
                dve.wait_ge(picking, n + 1)
                if late(n, 1):
                    dve.wait_ge(holding, n)
                    TT(held[:], held[:], picked[:], ALU.add).then_inc(holding, 1)
                else:
                    dve.tensor_copy(held[:], picked[:]).then_inc(holding, 1)

            dve.wait_ge(l_saved, CHUNKS)
            dve.memset(sums1.mask[:, :, :, 0:1], 0.0)
            weigh(0, 0)
            weigh(1, 1)
            finish(0, 0, 0)
            weigh(2, 0)
            finish(1, 1, 0)
            with dve.Fori(1, CHUNKS // 2 - 1) as i:
                weigh(2 * i + 1, 1)
                finish(2 * i, 0, i)
                weigh(2 * i + 2, 0)
                finish(2 * i + 1, 1, i)
            weigh(CHUNKS - 1, 1)
            finish(CHUNKS - 2, 0, CHUNKS // 2 - 1)
            finish(CHUNKS - 1, 1, CHUNKS // 2 - 1)
            carry_over(1, sums1)
            dve.wait_ge(carried, 2)
            dve.wait_ge(holding, CHUNKS)
            TT(held[:], held[:], carry[:], ALU.add).then_inc(holding, 1)


_INS = ["x", "src", "dst", "edge_attr_3", "edge_weight", "L0_gnn_w1", "L0_gnn_b1", "L0_gnn_w2", "L0_gnn_b2",
        "L1_gnn_w", "L1_gnn_fc_w", "L1_gnn_fc_b", "L1_gnn_bias"]


def shape_constants():
    eye = np.eye(P, dtype=np.float32)
    posn = (NODES + np.arange(SLOTS)).reshape(P, COLS).astype(np.float32)
    p = np.arange(P)
    f = [1.0 - 2.0 * ((p >> b) & 1) for b in range(7)]
    flips = np.stack([f[0], -f[0]] + [f[b] * f[b + 1] for b in range(6)] + [f[6]], 1).astype(np.float32)
    return {"eye": eye, "posn": posn, "flips": flips}


def kernel(**inputs):
    import concourse.bacc as _bacc
    from concourse.bass_utils import run_bass_kernel_spmd as _run

    nc = _bacc.Bacc("TRN2", target_bir_lowering=False, num_devices=1)
    arrays, args = {}, []
    given = {n: np.ascontiguousarray(inputs[n]) for n in _INS}
    for name, a in {**given, **shape_constants()}.items():
        arrays[f"in_{name}_dram"] = a
        args.append(nc.dram_tensor(f"in_{name}_dram", a.shape, mybir.dt.from_np(a.dtype), kind="ExternalInput").ap())
    out = nc.dram_tensor("out_0_dram", (NODES, FEAT), F32, kind="ExternalOutput").ap()
    graph_layers(nc, *args, out)
    r = _run(nc, [arrays], core_ids=[0])
    return r.results[0]["out_0_dram"]
```

```python
from contextlib import ExitStack
from math import sqrt

import numpy as np

import concourse.bass as bass
from concourse import mybir

P = 128
F32 = mybir.dt.float32
I32 = mybir.dt.int32
ALU = mybir.AluOpType
ACT = mybir.ActivationFunctionType
AX = mybir.AxisListType

NODES = 100000
EDGES = 25000
FEAT = 32
MUL = 8
HIDDEN = 64
HEADS = 4
RADIAL = 6 * MUL * MUL
COLS = -(-EDGES // P)
GROUP = 14
HALF = GROUP // 2
CHUNKS = COLS // GROUP
SLOTS = P * COLS
SORT_COLS = 256
SORT_BITS = 15
BIG = 1.0e30
EPS = 1e-5
RECORD = 8
DMA = 16
GATHERED = DMA * GROUP

W16 = 2 * MUL
NA = W16 * W16
NB = W16 * MUL
K_00 = 1 / 4
K_01 = 1 / 4
K_10 = sqrt(3 / 32)
K_110 = 1 / (4 * sqrt(2))
K_111 = sqrt(3) / 8
K_112R = 3 / 8
K_112I = -1 / 8

FILL_P = 80
FILL_ROWS = 125
SOFT_START = (-BIG, -BIG, 0.0, 0.0)
JOIN_START = (-BIG, -BIG, 0.0, 1.0)
COPY_PARTS = 5
FILLS = NODES // FILL_P // FILL_ROWS


def sort_plan():
    col_bits = SORT_COLS.bit_length() - 1
    plan, steps, half, turns, copies = [], 4, 0, [], []
    for k in range(1, SORT_BITS + 1):
        plan.append(("flip", k))
        steps += len(flips_of(k))

        def turn():
            plan.append(("turn", None))
            flipped = plan[-2][0] == "flip"
            turns.append((steps - (not flipped), steps - flipped, half))
            return steps + 1

        def compare(distance):
            plan.append(("compare", distance))
            copies.append((steps, half, plan[-2][0] == "turn"))
            return steps + 4, 1 - half

        if k > col_bits:
            steps = turn()
            for j in range(k - 1, col_bits - 1, -1):
                steps, half = compare(1 << (j - col_bits))
            steps = turn()
        for j in range(min(k, col_bits) - 1, -1, -1):
            steps, half = compare(1 << j)
    return plan, steps, half, turns, copies


def flips_of(k, keys=None):
    if keys is None:
        return [None] * (2 if 1 < k <= 8 else 1)
    if k == 1:
        return [(keys.rearrange("p (a u b) -> p a u b", u=2, b=2)[:, :, 1], None)]
    if k < 8:
        v = keys.rearrange("p (a u v b) -> p a u v b", u=2, v=2, b=1 << (k - 1))
        return [(v[:, :, 0, 1], None), (v[:, :, 1, 0], None)]
    if k == 8:
        return [(keys[:, 0:P], 0), (keys[:, P:], 1)]
    return [(keys, k - 7)]


SORT_PLAN, SORT_STEPS, SORT_END, SORT_TURNS, SORT_COPIES = sort_plan()


def graph_layers(nc, x, src, dst, attr, ew, w1, b1, w2, b2, w, fcw, fcb, bias, eye, posn, flips, out):
    assert EDGES < SLOTS and CHUNKS * GROUP == COLS and CHUNKS % 2 == 0 and FILLS % 2 == 0 and FILLS < CHUNKS
    with ExitStack() as ctx:
        def sb(name, shape, dt=F32):
            return ctx.enter_context(nc.sbuf_tensor(name, shape, dt))

        def sem(name):
            return ctx.enter_context(nc.semaphore(name))

        nodes1 = nc.dram_tensor("nodes1", [NODES + SLOTS, FEAT], F32).ap()
        key_pad = nc.dram_tensor("key_pad", [P * SORT_COLS + 1], F32).ap()
        pay_dram = nc.dram_tensor("pay_dram", [P * SORT_COLS], F32).ap()
        records = nc.dram_tensor("records", [SLOTS, RECORD], F32).ap()
        dist_row = nc.dram_tensor("dist_row", [COLS, P], F32).ap()

        ident = sb("ident", [P, P])
        pos = sb("pos", [P, COLS])
        flip = sb("flip", [P, 9])
        eps = sb("eps", [P, 1])
        ones32 = sb("ones32", [P, FEAT])
        w1c = sb("w1c", [HIDDEN, 1])
        b1c = sb("b1c", [HIDDEN, 1])
        w2raw = sb("w2raw", [HIDDEN + 1, RADIAL])
        w2p = sb("w2p", [HIDDEN + 1, RADIAL])
        w2t = sb("w2t", [HIDDEN + 1, MUL, MUL])
        wrep = sb("wrep", [P, HEADS, FEAT])
        wmul = sb("wmul", [P, 2, HEADS, FEAT])
        fcw_b = sb("fcw_b", [P, 2 * FEAT])
        fcb_b = sb("fcb_b", [P, 1])
        bias_b = sb("bias_b", [P, FEAT])
        u_all = sb("u_all", [P, 2, HEADS])
        ublk = sb("ublk", [P, 2, 4 * HEADS])
        wstk_raw = sb("wstk_raw", [P, FEAT])
        wstk = sb("wstk", [P, FEAT])

        src_i = sb("src_i", [P, COLS], I32)
        dst_ext_i = sb("dst_ext_i", [P, COLS + 2], I32)
        dist = sb("dist", [P, COLS])
        vec = sb("vec", [P, COLS, 3])
        src_f = sb("src_f", [P, COLS])
        dst_f = sb("dst_f", [P, COLS])
        dst_ext = sb("dst_ext", [P, COLS + 2])
        idx_src = sb("idx_src", [P, COLS], I32)
        idx_dst = sb("idx_dst", [P, COLS], I32)
        idx_tmp = sb("idx_tmp", [P, COLS])
        r5 = sb("r5", [P, COLS, 5])
        same_d = sb("same_d", [P, COLS])
        same = sb("same", [P, COLS])
        last = sb("last", [P, COLS])
        opened = sb("opened", [P, COLS])
        distT = sb("distT", [P, 2, P])

        stage_x = sb("stage_x", [P, 2, GROUP], I32)
        stage_add = sb("stage_add", [P, 2, GROUP], I32)
        stage_l = sb("stage_l", [P, 2, 2, GROUP], I32)
        stage_out = sb("stage_out", [P, 2, GROUP], I32)
        rowring = sb("rowring", [P, 2, GROUP, FEAT])

        def carver(arena):
            at = [0]

            def carve(shape, parts=P):
                n = int(np.prod(shape))
                names = "abcd"[:len(shape)]
                flat = arena[0:parts, at[0]:at[0] + n]
                at[0] += n
                return flat.rearrange(f"p ({' '.join(names)}) -> p {' '.join(names)}",
                                      **dict(zip(names, shape)))
            return carve

        class Sums:

            def __init__(self, parts):
                self.flat = parts
                self.terms, self.run, self.mask = (
                    a.rearrange("p b (f t) -> p b f t", f=FEAT) for a in parts)

        arena0 = sb("arena0", [P, 7504])
        carve = carver(arena0)
        xring = carve([2, GROUP, FEAT])
        xc = carve([2, GROUP, FEAT])
        sq = carve([2, GROUP, FEAT])
        h0 = carve([2, GROUP, FEAT])
        z = carve([2, GROUP, W16])
        V = carve([2, GROUP, W16 * 3]).rearrange("p b t (w o) -> p b t w o", o=3)
        f1e = carve([2, GROUP, MUL * 5]).rearrange("p b t (v o) -> p b t v o", o=5)
        crs = carve([3, GROUP, MUL * 3]).rearrange("p b t (v o) -> p b t v o", o=3)
        carve = carver(arena0)
        lring = carve([2, 2 * GROUP, FEAT])
        hT = carve([2, 2 * P])
        E = carve([COLS, HEADS])
        soft = carve([4, COLS, HEADS])
        wT = carve([2, 4 * P])

        arena1 = sb("arena1", [P, 4 * GROUP * P])
        carve = carver(arena1)
        hidden = carve([2, GROUP * P], HIDDEN + 1)
        distb = carve([2, GROUP * P], HIDDEN)
        carve = carver(arena1)
        lxc = carve([2 * GROUP, FEAT])
        lsq = carve([2 * GROUP, FEAT])
        lh = carve([2, 2 * GROUP, FEAT])
        weighted = carve([2, GROUP, P])
        carve = carver(arena1)
        sums1 = Sums([carve([2, FEAT * GROUP]) for _ in range(3)])
        picks = carve([FEAT, GROUP])

        prods = sb("prods", [P, 2 * HALF * (NA + 3 * NB)])
        prodA = prods[:, 0:2 * HALF * NA].rearrange("p (h t w u) -> p h t w u", h=2, t=HALF, w=W16)
        prodB = prods[:, 2 * HALF * NA:].rearrange("p (h t w u) -> p h t w u", h=2, t=HALF, w=W16)
        vsq = prods[:, 0:3 * COLS].rearrange("p (c o) -> p c o", o=3)
        vn = prods[:, 3 * COLS:6 * COLS].rearrange("p (k c) -> p k c", k=3)
        record = prods[:, 0:RECORD * COLS].rearrange("p (c k) -> p c k", k=RECORD)
        fill = prods[0:FILL_P, 0:2 * FILL_ROWS * FEAT].rearrange("p (b n) -> p b n", b=2)

        mean = sb("mean", [P, 2, 2 * GROUP])
        lsum = sb("lsum", [P, 2, 2 * GROUP])
        vsum = sb("vsum", [P, 2, 2 * GROUP])
        std = sb("std", [P, 2, 2 * GROUP])
        rstd = sb("rstd", [P, 2, 2 * GROUP])
        qr = sb("qr", [P, 2, HALF, MUL, 3])
        hd = sb("hd", [P, COLS, FEAT])
        carve = carver(hd[:].rearrange("p c f -> p (c f)"))
        sums0 = Sums([carve([2, FEAT * GROUP]) for _ in range(3)])
        carry = sb("carry", [P, FEAT])
        openrep = sb("openrep", [P, FEAT])
        openT = sb("openT", [FEAT, P])
        chain = sb("chain", [FEAT, P + 1])

        pairs = sb("pairs", [P, 2, 2, SORT_COLS])
        skey, spay = pairs[:, :, 0], pairs[:, :, 1]
        key_ext = sb("key_ext", [P, COLS + 2])
        pay = sb("pay", [P, COLS])
        idx_dst_s = sb("idx_dst_s", [P, COLS], I32)
        idx_out = sb("idx_out", [P, COLS], I32)
        more = sb("more", [P, COLS])
        negopen = sb("negopen", [P, 2, COLS])
        before = sb("before", [1, 1])
        unsorted = sb("unsorted", [P, 1])
        unsorted_1 = sb("unsorted_1", [1, 1])
        flag = sb("flag", [1, 1], I32)
        record_ring = sb("record_ring", [P, 2, GROUP, RECORD])

        xsb = sb("xsb", [P, COLS, FEAT])
        x_src = xsb
        lend = sb("lend", [P, FEAT])
        ends_in = sb("ends_in", [P, COLS])
        crosses = sb("crosses", [P, 2])
        idx_carry = sb("idx_carry", [P, 2], I32)
        picked = sb("picked", [P, FEAT])
        held = sb("held", [P, FEAT])
        lgt = sb("lgt", [P, GROUP * HEADS])
        negs = sb("negs", [P, 2, COLS])
        openR = sb("openR", [P, COLS])
        open4 = sb("open4", [P, 4, HEADS])
        openT4 = sb("openT4", [HEADS, 4, P])
        ladder = sb("ladder", [HEADS, 4, P + 1])
        join = sb("join", [P, 4, HEADS])
        shares = sb("shares", [P, 2, GROUP, HEADS])

        psM = ctx.enter_context(nc.psum_tensor("psM", [P, 4, 512], F32))
        psR = ctx.enter_context(nc.psum_tensor("psR", [P, 2, 512], F32))
        psT = ctx.enter_context(nc.psum_tensor("psT", [P, 512], F32))
        psX = ctx.enter_context(nc.psum_tensor("psX", [P, 512], F32))
        swaps = psR[:, :, 0:P].bitcast(I32)

        prefilled, ids_in, edges_in = map(sem, ("prefilled", "ids_in", "edges_in"))
        sorters_in, weights_in, copied = map(sem, ("sorters_in", "weights_in", "copied"))
        floats, edge_vals = map(sem, ("floats", "edge_vals"))
        before_out, r_record_out, r_record_there = map(sem, ("before_out", "r_record_out", "r_record_there"))
        compared, flag_turned, flagged = map(sem, ("compared", "flag_turned", "flagged"))
        r_pay_copied, pay_copied = sem("r_pay_copied"), sem("pay_copied")
        r_sort_turned, sort_turned = ([sem(f"{n}_{what}") for what in ("keys", "payloads")]
                                      for n in ("r_sort_turned", "sort_turned"))
        r_sorting, r_built, r_stored, r_order_in, r_indexed, r_staged, r_unpacked = map(
            sem, ("r_sorting", "r_built", "r_stored", "r_order_in", "r_indexed", "r_staged",
                  "r_unpacked"))
        r_in = [sem("r_in0"), sem("r_in1")]
        prep = sem("prep")
        vsq_done, vnorm, vstd, idx_src_ready = map(sem, ("vsq_done", "vnorm", "vstd", "idx_src_ready"))
        w2_ready, lweights = sem("w2_ready"), sem("lweights")
        dist_turned, dist_copied, dist_stored = map(sem, ("dist_turned", "dist_copied", "dist_stored"))
        pool_turn, staged = sem("pool_turn"), sem("staged")
        x_in = [sem("x_in0"), sem("x_in1")]
        summed, meaned, centered, squared, stded, rstded, normed = map(
            sem, ("summed", "meaned", "centered", "squared", "stded", "rstded", "normed"))
        spread, dotp, dotted, crossed, vectored = map(sem, ("spread", "dotp", "dotted", "crossed", "vectored"))
        dist_bc = [sem("dist_bc0"), sem("dist_bc1")]
        hid_ready, radial_ready, prod_done, preadded, reduced, q_done, posted = map(
            sem, ("hid_ready", "radial_ready", "prod_done", "preadded", "reduced", "q_done", "posted"))
        x_saved = sem("x_saved")
        masked, joined, summed_up = ([sem(f"{n}{k}") for k in range(2)] for n in ("masked", "joined", "summed_up"))
        ended, ends_turned, chained, carried = map(sem, ("ended", "ends_turned", "chained", "carried"))
        carry_out = [sem("carry_out0"), sem("carry_out1")]
        multiplied, picking, holding = map(sem, ("multiplied", "picking", "holding"))
        act_turn, rows_ready, l_staged = sem("act_turn"), sem("rows_ready"), sem("l_staged")
        rows_out = [sem("rows_out0"), sem("rows_out1")]
        sorting, sorted_out, srcorder_in, idx_ready = map(
            sem, ("sorting", "sorted_out", "srcorder_in", "idx_ready"))
        l_in = [sem("l_in0"), sem("l_in1")]
        l_summed, l_meaned, l_centered, l_squared, l_varsummed, l_stded, l_rstded, l_normed = map(
            sem, ("l_summed", "l_meaned", "l_centered", "l_squared", "l_varsummed", "l_stded", "l_rstded",
                  "l_normed"))
        l_saved, l_based, l_turned, l_hT, l_logits, l_biased, l_logged = map(
            sem, ("l_saved", "l_based", "l_turned", "l_hT", "l_logits", "l_biased", "l_logged"))
        fill_in = [sem("fill_in0"), sem("fill_in1")]
        fill_added = sem("fill_added")
        fill_out = [sem("fill_out0"), sem("fill_out1")]
        running, opens_ready, opens_turned = map(sem, ("running", "opens_ready", "opens_turned"))
        s_turned, s_exp, joining, shifted = map(sem, ("s_turned", "s_exp", "joining", "shifted"))
        inverted, shared = sem("inverted"), sem("shared")
        weighed, m_turned, m_wT, m_mixed, m_out = map(sem, ("weighed", "m_turned", "m_wT", "m_mixed", "m_out"))
        out_rows = sem("out_rows")
        out_done = [sem("out_done0"), sem("out_done1")]

        last_rows = (P - 1) * COLS
        tail = EDGES - last_rows

        def windows(a, start, n):
            return bass.AP(tensor=a.tensor, offset=start, ap=[[COLS, n], [1, COLS + 2]])

        def chunk_cols(n):
            return bass.ds(n * GROUP, GROUP)

        class Steps:

            def __init__(self, eng, s, base=0):
                self.eng, self.s, self.n = eng, s, base

            def do(self, ins):
                ins.then_inc(self.s, 1)
                self.n += 1

            def settle(self):
                self.eng.wait_ge(self.s, self.n)

            def link(self, ins):
                self.do(ins)
                self.settle()

        def bc(ap, axis, n):
            a = ap.unsqueeze(axis)
            shape = list(a.shape)
            shape[axis] = n
            return a.broadcast_to(shape)

        block = ctx.enter_context(nc.Block())

        @block.sync
        def _(sp):
            for tile, a in ((ident[:], eye), (flip[:], flips)):
                sp.dma_start(tile, a).then_inc(sorters_in, DMA)

            def edge_array(tile, a):
                whole = a[0:last_rows].rearrange("(p c) -> p c", c=COLS)
                sp.dma_start(tile[0:112, :], whole[0:112]).then_inc(ids_in if a is src else edges_in, DMA)
                sp.dma_start(tile[112:P - 1, :], whole[112:P - 1]).then_inc(ids_in if a is src else edges_in, DMA)
                sp.dma_start(tile[P - 1:P, 0:tail], a[last_rows:EDGES].rearrange("(p c) -> p c", p=1)
                             ).then_inc(ids_in if a is src else edges_in, DMA)

            sp.wait_ge(prefilled, 3)
            sp.dma_start(dst_ext_i[0:1, 1:], dst[0:COLS + 1].rearrange("(p c) -> p c", p=1)).then_inc(ids_in, DMA)
            sp.dma_start(dst_ext_i[1:113], windows(dst, COLS - 1, 112)).then_inc(ids_in, DMA)
            sp.dma_start(dst_ext_i[113:P - 1], windows(dst, 113 * COLS - 1, P - 114)).then_inc(ids_in, DMA)
            sp.dma_start(dst_ext_i[P - 1:P, 0:tail + 1], dst[last_rows - 1:EDGES].rearrange("(p c) -> p c", p=1)
                         ).then_inc(ids_in, DMA)
            edge_array(src_i, src)
            sp.wait_ge(prefilled, 5)
            edge_array(dist, ew)
            whole = attr[0:last_rows].rearrange("(p c) o -> p c o", c=COLS)
            sp.dma_start(vec[0:112], whole[0:112]).then_inc(edges_in, DMA)
            sp.dma_start(vec[112:P - 1], whole[112:P - 1]).then_inc(edges_in, DMA)
            sp.dma_start(vec[P - 1:P, 0:tail], attr[last_rows:EDGES].rearrange("(p c) o -> p c o", p=1)
                         ).then_inc(edges_in, DMA)
            for tile, a in (
                (pos[:], posn),
                (w1c[:], w1.rearrange("one h -> h one")), (b1c[:], b1.rearrange("(h one) -> h one", one=1)),
                (w2raw[0:HIDDEN], w2), (w2raw[HIDDEN:HIDDEN + 1], b2.rearrange("(one r) -> one r", one=1)),
                (fcw_b[:], fcw[0].partition_broadcast(P)), (fcb_b[:], fcb.partition_broadcast(P)),
                (bias_b[:], bias.partition_broadcast(P)), (wstk_raw[:], w.rearrange("h f o -> (h f) o")),
                *((wrep[32 * t:32 * t + 32], w.rearrange("h f o -> f h o")) for t in range(4)),
            ):
                sp.dma_start(tile, a).then_inc(weights_in, DMA)
            sp.wait_ge(edge_vals, 1)
            sp.dma_start(key_pad[0:1].rearrange("(a b) -> a b", a=1), before[:]).then_inc(before_out, DMA)
            sp.wait_ge(before_out, DMA)

            def sorted_pairs(stored, loaded, ext, payload):
                sp.dma_start(key_pad[1:1 + P * SORT_COLS].rearrange("(p c) -> p c", c=SORT_COLS),
                             skey[:, SORT_END]).then_inc(stored, DMA)
                sp.dma_start(pay_dram.rearrange("(p c) -> p c", c=SORT_COLS), spay[:, SORT_END]
                             ).then_inc(stored, DMA)
                sp.wait_ge(stored, 2 * DMA)
                sp.dma_start(ext, windows(key_pad, 0, P)).then_inc(loaded, DMA)
                sp.dma_start(payload, pay_dram[0:SLOTS].rearrange("(p c) -> p c", c=COLS)).then_inc(loaded, DMA)
                sp.wait_ge(loaded, 2 * DMA)

            sp.wait_ge(flagged, 1)
            with sp.If(sp.value_load(flag[:], min_val=0, max_val=1) > 0):
                sp.wait_ge(r_built, 1)
                sp.dma_start(records.rearrange("(p c) k -> p c k", c=COLS), record).then_inc(r_record_out, DMA)
                sp.wait_ge(r_sorting, SORT_STEPS)
                sorted_pairs(r_stored, r_order_in, dst_ext[:], pay[:])
                sp.wait_ge(r_record_out, DMA)
                sp.sem_inc(r_record_there, 1)

            sp.wait_ge(dist_copied, 1)
            for j in range(2):
                sp.dma_start(dist_row[98 * j:98 * j + 98], distT[0:98, j]).then_inc(dist_stored, DMA)
            sp.wait_ge(dist_stored, 2 * DMA)

            def dist_load(n, b):
                if not isinstance(n, int) or n >= 2:
                    sp.wait_ge(hid_ready, n - 1)
                sp.dma_start(distb[:, b], dist_row[chunk_cols(n)].rearrange("c p -> (c p)")
                             .partition_broadcast(HIDDEN)).then_inc(dist_bc[b], DMA)

            dist_load(0, 0)
            dist_load(1, 1)
            for part in range(COPY_PARTS):
                rows = bass.ds(part * NODES // COPY_PARTS, NODES // COPY_PARTS)
                if part:
                    sp.wait_ge(sorting, part * SORT_STEPS // COPY_PARTS)
                sp.dma_start(nodes1[rows].rearrange("(a b) d -> a (b d)", a=200),
                             x[rows].rearrange("(a b) d -> a (b d)", a=200)).then_inc(copied, DMA)
            sp.dma_start(nodes1[NODES:NODES + SLOTS].rearrange("(a b) d -> a (b d)", a=784),
                         x[0:SLOTS].rearrange("(a b) d -> a (b d)", a=784)).then_inc(copied, DMA)

            sp.wait_ge(sorting, SORT_STEPS)
            sorted_pairs(sorted_out, srcorder_in, key_ext[:], pay[:])

            with sp.Fori(1, CHUNKS // 2) as i:
                dist_load(2 * i, 0)
                dist_load(2 * i + 1, 1)

            rows_in = nodes1[0:NODES].rearrange("(p r) d -> p (r d)", p=FILL_P)
            rows_to = out.rearrange("(p r) d -> p (r d)", p=FILL_P)
            width = FILL_ROWS * FEAT

            def fill_load(m, b):
                sp.dma_start(fill[:, b], rows_in[:, bass.ds(m * width, width)]).then_inc(fill_in[b], DMA)

            def fill_store(m, b):
                sp.wait_ge(fill_added, m + 1)
                sp.dma_start(rows_to[:, bass.ds(m * width, width)], fill[:, b]).then_inc(fill_out[b], DMA)

            sp.wait_ge(carry_out[0], DMA)
            fill_load(0, 0)
            fill_load(1, 1)
            with sp.Fori(0, FILLS // 2 - 1) as i:
                for b in range(2):
                    fill_store(2 * i + b, b)
                    sp.wait_ge(fill_out[b], DMA * (i + 1))
                    fill_load(2 * i + 2 + b, b)
            for b in range(2):
                fill_store(FILLS - 2 + b, b)
            for b in range(2):
                sp.wait_ge(fill_out[b], DMA * FILLS // 2)
                sp.wait_ge(out_done[b], GATHERED * CHUNKS // 2)
            sp.wait_ge(carry_out[1], DMA)

        @block.gpsimd
        def _(pool):
            pool.memset(src_i[:], NODES).then_inc(prefilled, 1)
            pool.memset(dst_ext_i[:], NODES).then_inc(prefilled, 1)
            pool.wait_ge(prefilled, 2)
            pool.memset(dst_ext_i[0:1, 0:1], -1).then_inc(prefilled, 1)
            pool.memset(before[:], -1.0).then_inc(edge_vals, 1)
            pool.wait_ge(prefilled, 3)
            pool.wait_ge(edge_vals, 1)
            pool.memset(dist[:], 0.0).then_inc(prefilled, 1)
            pool.memset(vec[:], 1.0).then_inc(prefilled, 1)
            pool.memset(eps[:], EPS).then_inc(prefilled, 1)
            pool.wait_ge(prefilled, 6)
            pool.memset(hidden[HIDDEN:HIDDEN + 1], 1.0).then_inc(prefilled, 1)
            pool.wait_ge(prefilled, 7)
            bound = pool.to_reg(NODES - 1)

            pool.wait_ge(flagged, 1)
            with pool.If(pool.value_load(flag[:], min_val=0, max_val=1) > 0):
                pool.wait_ge(r_indexed, 1)
                pool.wait_ge(r_record_there, 1)

                def gather_records(n, b, rounds):
                    if not isinstance(n, int) or n >= 2:
                        pool.wait_ge(r_in[b], GATHERED * rounds)
                        pool.wait_ge(r_unpacked, n - 1)
                        pool.sem_inc(pool_turn, 1)
                    pool.tensor_copy(stage_x[:, b], idx_out[:, chunk_cols(n)]).then_inc(r_staged, 1)
                    pool.wait_ge(r_staged, n + 1)
                    pool.sem_inc(pool_turn, 1)
                    for t in range(GROUP):
                        pool.indirect_dma_start(record_ring[:, b, t], None, records,
                                                bass.IndirectOffsetOnAxis(ap=stage_x[:, b, t:t + 1], axis=0)
                                                ).then_inc(r_in[b], DMA)

                gather_records(0, 0, 0)
                gather_records(1, 1, 0)
                with pool.Fori(1, CHUNKS // 2) as i:
                    gather_records(2 * i, 0, i)
                    gather_records(2 * i + 1, 1, i)
                for b in range(2):
                    pool.wait_ge(r_in[b], GATHERED * CHUNKS // 2)

            pool.wait_ge(idx_src_ready, 1)
            for b in range(2):
                pool.tensor_copy(stage_x[:, b], idx_src[:, chunk_cols(b)]).then_inc(staged, 1)
            pool.wait_ge(staged, 2)

            def gather_x(n, b):
                if not isinstance(n, int) or n >= 2:
                    pool.wait_ge(x_saved, n - 1)
                pool.sem_inc(pool_turn, 1)
                for t in range(GROUP):
                    pool.indirect_dma_start(xring[:, b, t], None, x,
                                            bass.IndirectOffsetOnAxis(ap=stage_x[:, b, t:t + 1], axis=0)
                                            ).then_inc(x_in[b], DMA)

            gather_x(0, 0)
            gather_x(1, 1)
            with pool.Fori(1, CHUNKS // 2) as i:
                gather_x(2 * i, 0)
                gather_x(2 * i + 1, 1)

            pool.wait_ge(copied, (COPY_PARTS + 1) * DMA)

            def add_rows(n, b):
                pool.wait_ge(rows_ready, n + 1)
                pool.sem_inc(pool_turn, 1)
                for t in range(GROUP):
                    pool.indirect_dma_start(nodes1, bass.IndirectOffsetOnAxis(ap=stage_add[:, b, t:t + 1], axis=0),
                                            rowring[:, b, t], None, compute_op=ALU.add).then_inc(rows_out[b], DMA)

            with pool.Fori(0, CHUNKS // 2) as i:
                add_rows(2 * i, 0)
                add_rows(2 * i + 1, 1)

            for b in range(2):
                pool.wait_ge(rows_out[b], GATHERED * CHUNKS // 2)
            pool.wait_ge(carried, 1)
            pool.indirect_dma_start(nodes1, bass.IndirectOffsetOnAxis(ap=idx_carry[:, 0:1], axis=0), carry[:],
                                    None, compute_op=ALU.add).then_inc(carry_out[0], DMA)

            pool.wait_ge(carry_out[0], DMA)

            def gather_l(n, b):
                if not isinstance(n, int) or n >= 2:
                    pool.wait_ge(l_centered, n - 1)
                    pool.wait_ge(l_based, n - 1)
                pool.wait_ge(l_staged, n + 1)
                pool.sem_inc(pool_turn, 1)
                for k in range(2):
                    for t in range(GROUP):
                        pool.indirect_dma_start(lring[:, b, k * GROUP + t], None, nodes1,
                                                bass.IndirectOffsetOnAxis(ap=stage_l[:, b, k, t:t + 1], axis=0)
                                                ).then_inc(l_in[b], DMA)

            gather_l(0, 0)
            gather_l(1, 1)
            with pool.Fori(1, CHUNKS // 2) as i:
                gather_l(2 * i, 0)
                gather_l(2 * i + 1, 1)

            for b in range(2):
                pool.wait_ge(fill_out[b], DMA * FILLS // 2)

            def put_rows(n, b):
                pool.wait_ge(out_rows, n + 1)
                pool.sem_inc(pool_turn, 1)
                for t in range(GROUP):
                    pool.indirect_dma_start(out, bass.IndirectOffsetOnAxis(ap=stage_out[:, b, t:t + 1], axis=0),
                                            rowring[:, b, t], None, bounds_check=bound, oob_is_err=False
                                            ).then_inc(out_done[b], DMA)

            with pool.Fori(0, CHUNKS // 2) as i:
                put_rows(2 * i, 0)
                put_rows(2 * i + 1, 1)
            pool.wait_ge(holding, CHUNKS + 1)
            pool.indirect_dma_start(out, bass.IndirectOffsetOnAxis(ap=idx_carry[:, 1:2], axis=0), held[:], None,
                                    bounds_check=bound, oob_is_err=False).then_inc(carry_out[1], DMA)

        @block.scalar
        def _(act):
            def copy_payloads(steps_done, turned, copied_to, between=lambda k: None):
                turns = 0
                for k, (steps, half, after_turn) in enumerate(SORT_COPIES):
                    of = spay[:, half]
                    if after_turn:
                        turns += 1
                        of = psT[:, 0:SORT_COLS]
                        act.wait_ge(turned[1], turns)
                        act.activation(spay[:, half], of, ACT.Copy)
                    else:
                        act.wait_ge(steps_done, steps)
                    act.activation(spay[:, 1 - half], of, ACT.Copy).then_inc(copied_to, 1)
                    between(k)

            act.wait_ge(flagged, 1)
            with act.If(act.value_load(flag[:], min_val=0, max_val=1) > 0):
                copy_payloads(r_sorting, r_sort_turned, r_pay_copied)

            act.wait_ge(idx_src_ready, 1)
            act.wait_ge(edges_in, 6 * DMA)
            act.activation(vsq, vec[:], ACT.Square).then_inc(vsq_done, 1)
            act.wait_ge(dist_turned, 1)
            act.activation(distT[0:98], psT[0:98, 0:2 * P].rearrange("p (j c) -> p j c", j=2), ACT.Copy
                           ).then_inc(dist_copied, 1)

            def save_x(n, b, rounds):
                act.wait_ge(x_in[b], GATHERED * rounds)
                act.sem_inc(act_turn, 1)
                save = act.activation(x_src[:, chunk_cols(n)], xring[:, b], ACT.Copy)
                if n < CHUNKS - 2:
                    save = act.activation(stage_x[:, b], idx_src[:, chunk_cols(n + 2)], ACT.Copy)
                save.then_inc(x_saved, 1)

            def spread_mask(layer, sums, same, n, b):
                if not isinstance(n, int) or n >= 2:
                    act.wait_ge(summed_up[layer], n - 1)
                    act.sem_inc(act_turn, 1)
                act.activation(sums.mask[:, b, :, 1:], bc(same[:, bass.ds(n * GROUP + 1, GROUP - 1)], 1, FEAT),
                               ACT.Copy).then_inc(masked[layer], 1)

            def sum_rows(n, b, rounds):
                if not isinstance(rounds, int) or rounds > 0:
                    act.wait_ge(rows_out[b], GATHERED * rounds)
                act.wait_ge(summed_up[0], n + 1)
                act.activation(rowring[:, b], sums0.run[:, b].rearrange("p f t -> p t f"), ACT.Copy)
                act.activation(stage_add[:, b], idx_dst[:, chunk_cols(n)], ACT.Copy).then_inc(rows_ready, 1)

            def row_sums(n, b):
                if isinstance(n, int):
                    act.wait_ge(x_saved, n + 1)
                if not isinstance(n, int) or n >= 2:
                    act.wait_ge(squared, n - 1)
                    act.sem_inc(act_turn, 1)
                for t in range(GROUP):
                    total = act.activation(sq[:, b, t], x_src[:, n * GROUP + t], ACT.Copy,
                                           accum_out=lsum[:, b, t:t + 1])
                total.then_inc(summed, 1)

            def layer0_chunk(n, b, rounds):
                late = not isinstance(n, int) or n >= 2
                act.wait_ge(dist_bc[b], DMA * rounds)
                if late:
                    act.wait_ge(radial_ready, (n - 1) * GROUP)
                act.activation(hidden[0:HIDDEN, b], distb[:, b], ACT.Relu, bias=b1c[:], scale=w1c[:]
                               ).then_inc(hid_ready, 1)
                if not isinstance(n, int) or 0 < n < CHUNKS - 1:
                    row_sums(n + 1, 1 - b)
                act.wait_ge(centered, n + 1)
                for t in range(GROUP):
                    square = act.activation(sq[:, b, t], xc[:, b, t], ACT.Square, accum_out=vsum[:, b, t:t + 1])
                square.then_inc(squared, 1)
                act.wait_ge(squared, n + 1)
                act.activation(std[:, b, 0:GROUP], vsum[:, b, 0:GROUP], ACT.Sqrt, bias=eps[:], scale=1.0 / FEAT
                               ).then_inc(stded, 1)
                if isinstance(n, int) and n == 0:
                    row_sums(n + 1, 1 - b)
                act.wait_ge(normed, n + 1)
                if late:
                    act.wait_ge(prod_done, (n - 1) * GROUP)
                f1 = h0[:, b, :, MUL:].rearrange("p t (v o) -> p t v o", o=3)
                act.activation(f1e[:, b, :, :, 0:3], f1, ACT.Copy)
                act.activation(f1e[:, b, :, :, 3:5], f1[:, :, :, 0:2], ACT.Copy)
                act.activation(z[:, b, :, 0:MUL], h0[:, b, :, 0:MUL], ACT.Copy)
                act.activation(V[:, b, :, 0:MUL], f1, ACT.Copy).then_inc(spread, 1)
                if late:
                    sum_rows(n - 2, b, rounds - 2)
                if isinstance(n, int) and n == 0:
                    act.wait_ge(idx_ready, 1)
                spread_mask(0, sums0, same_d, n, b)

            SAVE_AT = {24 + 13 * n: n for n in range(8)}

            def save_between(k):
                if k in SAVE_AT:
                    save_x(SAVE_AT[k], SAVE_AT[k] % 2, SAVE_AT[k] // 2 + 1)

            copy_payloads(sorting, sort_turned, pay_copied, save_between)
            row_sums(0, 0)
            act.wait_ge(vnorm, 1)
            act.activation(vn[:, 1], vn[:, 0], ACT.Sqrt).then_inc(vstd, 1)
            act.wait_ge(weights_in, 13 * DMA)
            act.wait_ge(prefilled, 6)
            layer0_chunk(0, 0, 1)
            save_x(8, 0, 5)
            save_x(9, 1, 5)
            layer0_chunk(1, 1, 1)
            save_x(10, 0, 6)
            layer0_chunk(2, 0, 2)
            save_x(11, 1, 6)
            layer0_chunk(3, 1, 2)
            save_x(12, 0, 7)
            save_x(13, 1, 7)
            act.wait_ge(x_saved, CHUNKS)
            with act.Fori(2, CHUNKS // 2 - 1) as i:
                layer0_chunk(2 * i, 0, i + 1)
                layer0_chunk(2 * i + 1, 1, i + 1)
            layer0_chunk(CHUNKS - 2, 0, CHUNKS // 2)
            layer0_chunk(CHUNKS - 1, 1, CHUNKS // 2)
            sum_rows(CHUNKS - 2, 0, CHUNKS // 2 - 1)
            sum_rows(CHUNKS - 1, 1, CHUNKS // 2 - 1)

            def layer1_chunk(n, b):
                act.wait_ge(l_centered, n + 1)
                act.activation(lsq, lxc, ACT.Square).then_inc(l_squared, 1)
                act.wait_ge(l_varsummed, n + 1)
                act.activation(std[:, b], vsum[:, b], ACT.Sqrt, bias=eps[:], scale=1.0 / FEAT).then_inc(l_stded, 1)
                act.wait_ge(l_normed, n + 1)
                act.sem_inc(act_turn, 1)
                act.activation(hd[:, chunk_cols(n)], lh[:, b, GROUP:], ACT.Copy).then_inc(l_saved, 1)
                for g in range(4):
                    act.wait_ge(l_turned, n * 4 + g + 1)
                    if g >= 2:
                        act.wait_ge(l_logits, n * 4 + g - 1)
                    elif not isinstance(n, int) or n >= 1:
                        act.wait_ge(l_logits, n * 4 + g - 1)
                    act.activation(hT[:, g % 2], psM[:, g % 2, 0:2 * P], ACT.Copy).then_inc(l_hT, 1)

            layer1_chunk(0, 0)
            layer1_chunk(1, 1)
            with act.Fori(1, CHUNKS // 2) as i:
                layer1_chunk(2 * i, 0)
                layer1_chunk(2 * i + 1, 1)

            act.wait_ge(shifted, 1)
            act.activation(soft[:, 3], soft[:, 2], ACT.Exp).then_inc(s_exp, 1)

            def mix_chunk(n, b):
                for g in range(4):
                    width = P * min(4, GROUP - 4 * g)
                    act.wait_ge(m_turned, n * 4 + g + 1)
                    if g >= 2 or not isinstance(n, int) or n >= 1:
                        act.wait_ge(m_mixed, n * 4 + g - 1)
                    act.activation(wT[:, g % 2, 0:width], psM[:, g, 0:width], ACT.Copy).then_inc(m_wT, 1)
                act.wait_ge(m_mixed, n * 4 + 4)
                if not isinstance(n, int) or n >= 2:
                    act.wait_ge(summed_up[1], n - 1)
                act.activation(sums1.terms[:, b], psR[:, b, 0:GROUP * FEAT].rearrange("p (t f) -> p f t", f=FEAT),
                               ACT.Copy).then_inc(m_out, 1)
                spread_mask(1, sums1, same, n, b)

            act.wait_ge(weighed, 1)
            mix_chunk(0, 0)
            mix_chunk(1, 1)
            with act.Fori(1, CHUNKS // 2) as i:
                mix_chunk(2 * i, 0)
                mix_chunk(2 * i + 1, 1)

        @block.tensor
        def _(pe):
            pe.wait_ge(sorters_in, 2 * DMA)
            pe.wait_ge(compared, 1)
            pe.transpose(psT[0:1, 0:P], unsorted[:], ident[:]).then_inc(flag_turned, 1)

            def sort_turns(steps_done, turned):
                for key_steps, pay_steps, half in SORT_TURNS:
                    for what, (data, steps) in enumerate(((skey, key_steps), (spay, pay_steps))):
                        pe.wait_ge(steps_done, steps)
                        for k in range(2):
                            turn = pe.transpose((psX, psT)[what][:, k * P:(k + 1) * P],
                                                data[:, half, k * P:(k + 1) * P], ident[:])
                        turn.then_inc(turned[what], 1)

            pe.wait_ge(flagged, 1)
            with pe.If(pe.value_load(flag[:], min_val=0, max_val=1) > 0):
                sort_turns(r_sorting, r_sort_turned)
            pe.wait_ge(idx_src_ready, 1)
            pe.wait_ge(edges_in, 6 * DMA)
            for j in range(2):
                turn = pe.transpose(psT[0:98, j * P:(j + 1) * P], dist[:, 98 * j:98 * j + 98], ident[:])
            turn.then_inc(dist_turned, 1)
            pe.wait_ge(dist_copied, 1)
            sort_turns(sorting, sort_turned)
            pe.wait_ge(w2_ready, 1)
            pe.wait_ge(prefilled, 7)

            LAG = 2
            STEPS24 = [24 * t // HALF for t in range(HALF + 1)]

            def radial(n, b, h, t):
                k = h * HALF + t
                if k == 0:
                    pe.wait_ge(hid_ready, n + 1)
                if not isinstance(n, int) or n * GROUP + k >= 4:
                    pe.wait_ge(prod_done, n * GROUP + k - 3)
                pe.matmul(psM[:, (b * GROUP + k) % 4, 0:RADIAL], hidden[:, b, k * P:(k + 1) * P], w2p[:],
                          start=True, stop=True).then_inc(radial_ready, 1)

            def reduce(hh, par, t):
                if t == 0:
                    pe.wait_ge(preadded, hh + 1)
                    if not isinstance(hh, int) or hh >= 2:
                        pe.wait_ge(posted, hh - 1)
                for k in range(STEPS24[t], STEPS24[t + 1]):
                    if k < W16:
                        mm = pe.matmul(psR[:, par, 0:HALF * W16], ident[:], prodA[:, par, :, k],
                                       start=(k == 0), stop=(k == W16 - 1))
                    else:
                        mm = pe.matmul(psR[:, par, HALF * W16:HALF * (W16 + 3 * MUL)], ident[:],
                                       prodB[:, par, :, k - W16], start=(k == W16), stop=(k == 23))
                if t == HALF - 1:
                    mm.then_inc(reduced, 1)

            def layer0_chunk(n, b):
                for h in range(2):
                    for t in range(HALF):
                        radial(n, b, h, t)
                        if t >= LAG:
                            hh, par, part = 2 * n + h - 1, 1 - h, t - LAG
                        else:
                            hh, par, part = 2 * n + h - 2, h, t - LAG + HALF
                        if not isinstance(hh, int) or hh >= 0:
                            reduce(hh, par, part)

            layer0_chunk(0, 0)
            layer0_chunk(1, 1)
            with pe.Fori(1, CHUNKS // 2) as i:
                layer0_chunk(2 * i, 0)
                layer0_chunk(2 * i + 1, 1)
            for t in range(HALF - LAG, HALF):
                reduce(2 * CHUNKS - 2, 0, t)
            for t in range(HALF):
                reduce(2 * CHUNKS - 1, 1, t)

            def join_runs(step):
                pe.wait_ge(ended, step + 1)
                pe.transpose(psT[0:FEAT, 0:P], lend[:], ident[:])
                pe.transpose(psT[0:FEAT, P:2 * P], openrep[:], ident[:]).then_inc(ends_turned, 1)
                pe.wait_ge(chained, step + 1)
                pe.transpose(psT[:, 2 * P:2 * P + FEAT], chain[:, 0:P], ident[0:FEAT, 0:FEAT]).then_inc(ends_turned, 1)

            join_runs(0)

            pe.wait_ge(opens_ready, 1)
            for k in range(4):
                t = pe.transpose(psT[0:HEADS, k * P:(k + 1) * P], open4[:, k], ident[:])
            t.then_inc(opens_turned, 1)

            pe.wait_ge(lweights, 1)

            def logits_chunk(n, b):
                starts = (0, 4, 8, GROUP - 4)
                pe.wait_ge(l_normed, n + 1)

                def turn(g):
                    if g >= 2 or not isinstance(n, int) or n >= 1:
                        pe.wait_ge(l_hT, n * 4 + g - 1)
                    for k in range(2):
                        a = lh[:, b, k * GROUP + starts[g]:k * GROUP + starts[g] + 4]
                        t = pe.transpose(psM[:, g % 2, k * P:(k + 1) * P], a.rearrange("p t f -> p (t f)"), ident[:])
                    t.then_inc(l_turned, 1)

                def mix(g):
                    if g == 0 and (not isinstance(n, int) or n >= 2):
                        pe.wait_ge(l_biased, n - 1)
                    pe.wait_ge(l_hT, n * 4 + g + 1)
                    for k in range(2):
                        mm = pe.matmul(psR[:, b, HEADS * starts[g]:HEADS * (starts[g] + 4)],
                                       hT[:, g % 2, k * P:(k + 1) * P], ublk[:, k], start=(k == 0), stop=(k == 1))
                    mm.then_inc(l_logits, 1)

                turn(0)
                for g in range(4):
                    if g < 3:
                        turn(g + 1)
                    mix(g)

            logits_chunk(0, 0)
            logits_chunk(1, 1)
            with pe.Fori(1, CHUNKS // 2) as i:
                logits_chunk(2 * i, 0)
                logits_chunk(2 * i + 1, 1)

            pe.wait_ge(running, CHUNKS)
            for step in range(4):
                if step:
                    pe.wait_ge(joining, 2 * step)
                ends = soft[:, 0, COLS - 1] if step % 2 == 0 else soft[:, 1, 0]
                pe.transpose(psT[0:HEADS, 0:P], ends, ident[:]).then_inc(s_turned, 1)
                pe.wait_ge(joining, 2 * step + 1)
                pe.transpose(psT[:, P:P + HEADS], ladder[:, step, step % 2:step % 2 + P], ident[0:HEADS, 0:HEADS]
                             ).then_inc(s_turned, 1)

            def mix_chunk(n, b):
                pe.wait_ge(weighed, n + 1)

                def turn(g):
                    if not isinstance(n, int) or n >= 1:
                        pe.wait_ge(m_wT, n * 4 + g - 3)
                    for k in range(4 * g, min(4 * g + 4, GROUP)):
                        t = pe.transpose(psM[:, g, (k - 4 * g) * P:(k - 4 * g + 1) * P], weighted[:, b, k], ident[:])
                    t.then_inc(m_turned, 1)

                def mix(g):
                    if g == 0 and (not isinstance(n, int) or n >= 2):
                        pe.wait_ge(m_out, n - 1)
                    pe.wait_ge(m_wT, n * 4 + g + 1)
                    for k in range(4 * g, min(4 * g + 4, GROUP)):
                        mm = pe.matmul(psR[:, b, k * FEAT:(k + 1) * FEAT],
                                       wT[:, g % 2, (k - 4 * g) * P:(k - 4 * g + 1) * P], wstk[:],
                                       start=True, stop=True)
                    mm.then_inc(m_mixed, 1)

                turn(0)
                for g in range(4):
                    if g < 3:
                        turn(g + 1)
                    mix(g)

            mix_chunk(0, 0)
            mix_chunk(1, 1)
            with pe.Fori(1, CHUNKS // 2) as i:
                mix_chunk(2 * i, 0)
                mix_chunk(2 * i + 1, 1)
            join_runs(1)

        @block.vector
        def _(dve):
            st = Steps(dve, prep)
            TT, TS, STT = dve.tensor_tensor, dve.tensor_scalar, dve.scalar_tensor_tensor

            def late(n, first=2):
                return not isinstance(n, int) or n >= first

            st.do(dve.memset(ones32[:], 1.0))
            st.do(dve.memset(chain[:, 0:1], 0.0))
            dve.wait_ge(ids_in, 7 * DMA)
            dve.tensor_copy(src_f[:], src_i[:]).then_inc(floats, 1)
            dve.tensor_copy(dst_ext[:], dst_ext_i[:]).then_inc(floats, 1)
            dve.tensor_copy(dst_f[:], dst_ext_i[:, 1:COLS + 1]).then_inc(floats, 1)
            dve.wait_ge(floats, 3)
            st.link(TT(idx_tmp[:], dst_ext[:, 1:COLS + 1], dst_ext[:, 2:], ALU.is_gt))
            dve.tensor_reduce(unsorted[:], idx_tmp[:], AX.X, ALU.max).then_inc(compared, 1)
            dve.wait_ge(flag_turned, 1)
            st.link(dve.tensor_reduce(unsorted_1[:], psT[0:1, 0:P], AX.X, ALU.max))
            dve.tensor_copy(flag[:], unsorted_1[:]).then_inc(flagged, 1)

            def sort_pairs(so, turned, pay_copies):
                half = turns = compares = 0
                for kind, arg in SORT_PLAN:
                    key, load = skey[:, half], spay[:, half]
                    if kind == "flip":
                        so.settle()
                        for a, factor in flips_of(arg, key):
                            so.do(TS(a, a, -1.0 if factor is None else flip[:, factor:factor + 1], None, ALU.mult))
                        so.settle()
                    elif kind == "turn":
                        turns += 1
                        dve.wait_ge(turned[0], turns)
                        so.link(dve.tensor_copy(key, psX[:, 0:SORT_COLS]))
                    else:
                        def pair(a):
                            v = a.rearrange("p (m two d) -> p m two d", two=2, d=arg)
                            return v[:, :, 0], v[:, :, 1]

                        (ka, kb), (ko, kp) = pair(key), pair(skey[:, 1 - half])
                        g = swaps[:, half].rearrange("p (m d) -> p m d", d=arg)
                        to = spay[:, 1 - half].rearrange("p (m two d) -> p m two d", two=2, d=arg)
                        of = load.rearrange("p (m two d) -> p m two d", two=2, d=arg)
                        n0 = so.n
                        dve.wait_ge(so.s, n0 - 1)
                        so.do(TT(g, ka, kb, ALU.is_gt))
                        so.do(TT(ko, ka, kb, ALU.min))
                        so.do(TT(kp, ka, kb, ALU.max))
                        dve.wait_ge(so.s, n0 + 1)
                        compares += 1
                        dve.wait_ge(pay_copies, compares)
                        so.do(dve.copy_predicated(to, bc(g, 2, 2), of[:, :, ::-1]))
                        half = 1 - half
                assert so.n == SORT_STEPS and half == SORT_END

            dve.wait_ge(sorters_in, 2 * DMA)
            dve.wait_ge(flagged, 1)
            with dve.If(dve.value_load(flag[:], min_val=0, max_val=1) > 0):
                dve.wait_ge(edges_in, 6 * DMA)
                dve.wait_ge(weights_in, 13 * DMA)
                rs = Steps(dve, r_sorting)
                rs.do(dve.tensor_copy(skey[:, 0, 0:COLS], dst_f[:]))
                rs.do(dve.memset(skey[:, 0, COLS:], float(NODES)))
                rs.do(TS(spay[:, 0, 0:COLS], pos[:], float(NODES), None, ALU.subtract))
                rs.do(dve.memset(spay[:, 0, COLS:], float(SLOTS - 1)))
                dve.memset(record[:, :, 5:], 0.0)
                dve.tensor_copy(record[:, :, 0], src_f[:])
                dve.tensor_copy(record[:, :, 1], dist[:])
                dve.tensor_copy(record[:, :, 2:5], vec[:]).then_inc(r_built, 1)
                sort_pairs(rs, r_sort_turned, r_pay_copied)
                dve.wait_ge(r_order_in, 2 * DMA)
                dve.tensor_copy(dst_f[:], dst_ext[:, 1:COLS + 1])
                dve.tensor_copy(idx_out[:], pay[:]).then_inc(r_indexed, 1)
                dve.wait_ge(r_record_there, 1)

                def unpack(n, b, rounds):
                    dve.wait_ge(r_in[b], GATHERED * rounds)
                    TS(record[:, chunk_cols(n)], record_ring[:, b], 1.0, None, ALU.mult).then_inc(r_unpacked, 1)

                with dve.Fori(0, CHUNKS // 2) as i:
                    unpack(2 * i, 0, i + 1)
                    unpack(2 * i + 1, 1, i + 1)
                dve.wait_ge(r_unpacked, CHUNKS)
                dve.tensor_copy(dist[:], record[:, :, 1])
                dve.tensor_copy(vec[:], record[:, :, 2:5])
                dve.tensor_copy(src_f[:], record[:, :, 0]).then_inc(r_unpacked, 1)
                dve.wait_ge(r_unpacked, CHUNKS + 1)
            TS(idx_src[:], src_f[:], float(NODES - 1), None, ALU.min).then_inc(idx_src_ready, 1)
            so = Steps(dve, sorting)
            so.do(dve.tensor_copy(skey[:, 0, 0:COLS], src_f[:]))
            so.do(dve.memset(skey[:, 0, COLS:], float(NODES)))
            so.do(dve.tensor_copy(spay[:, 0, 0:COLS], dst_f[:]))
            so.do(dve.memset(spay[:, 0, COLS:], float(NODES)))
            sort_pairs(so, sort_turned, pay_copied)

            dve.wait_ge(vsq_done, 1)
            dve.tensor_reduce(vn[:, 0], vsq, AX.X, ALU.add).then_inc(vnorm, 1)


            def block_of(k, n=1):
                a = w2raw[:, k * MUL * MUL:(k + n) * MUL * MUL]
                return a.rearrange("p (u v k) -> p k v u", v=MUL, k=n)

            dve.wait_ge(weights_in, 13 * DMA)
            m01 = w2p[:, 0:NA].rearrange("p (w u) -> p w u", u=W16)
            m23 = w2p[:, NA:].rearrange("p (w u) -> p w u", u=MUL)
            TS(m01[:, 0:MUL, 0:MUL], block_of(0)[:, 0], K_00, None, ALU.mult)
            TS(m01[:, MUL:, 0:MUL], block_of(1)[:, 0], K_01, None, ALU.mult)
            TS(m01[:, 0:MUL, MUL:], block_of(2)[:, 0], K_10, None, ALU.mult)
            TS(m01[:, MUL:, MUL:], block_of(3, 3)[:, 2], K_112R, None, ALU.mult)
            TS(m23[:, MUL:], block_of(3, 3)[:, 1], K_111, None, ALU.mult)
            st.link(TS(w2t[:], block_of(3, 3)[:, 2], K_112I, None, ALU.mult))
            STT(m23[:, 0:MUL], block_of(3, 3)[:, 0], K_110, w2t[:], ALU.mult, ALU.add).then_inc(w2_ready, 1)
            def row_means(n, b):
                dve.wait_ge(summed, n + 1)
                TS(mean[:, b, 0:GROUP], lsum[:, b, 0:GROUP], 1.0 / FEAT, None, ALU.mult).then_inc(meaned, 1)

            def center(n, b):
                dve.wait_ge(meaned, n + 1)
                TT(xc[:, b], x_src[:, chunk_cols(n)], bc(mean[:, b, 0:GROUP], 2, FEAT), ALU.subtract
                   ).then_inc(centered, 1)

            def invert(n, b):
                dve.wait_ge(stded, n + 1)
                dve.reciprocal(rstd[:, b, 0:GROUP], std[:, b, 0:GROUP]).then_inc(rstded, 1)

            def norm(n, b):
                dve.wait_ge(rstded, n + 1)
                STT(h0[:, b], xc[:, b], 0.0, bc(rstd[:, b, 0:GROUP], 2, FEAT), ALU.max, ALU.mult).then_inc(normed, 1)

            def dot(n, b):
                dve.wait_ge(normed, n + 1)
                f1 = h0[:, b, :, MUL:].rearrange("p t (v o) -> p t v o", o=3)
                TT(crs[:, 2], f1, bc(r5[:, chunk_cols(n), 0:3], 2, MUL), ALU.mult).then_inc(dotp, 1)

            def cross(n, b):
                dve.wait_ge(spread, n + 1)
                TT(crs[:, 0], f1e[:, b, :, :, 2:5], bc(r5[:, chunk_cols(n), 1:4], 2, MUL), ALU.mult)
                TT(crs[:, 1], f1e[:, b, :, :, 1:4], bc(r5[:, chunk_cols(n), 2:5], 2, MUL), ALU.mult
                   ).then_inc(crossed, 1)

            def operands(n, b):
                dve.wait_ge(dotp, n + 1)
                dve.tensor_reduce(z[:, b, :, MUL:], crs[:, 2], AX.X, ALU.add).then_inc(dotted, 1)
                dve.wait_ge(crossed, n + 1)
                TT(V[:, b, :, MUL:], crs[:, 0], crs[:, 1], ALU.subtract).then_inc(vectored, 1)

            def products(n, b, h, between=()):
                if h == 0:
                    dve.wait_ge(dotted, n + 1)
                    dve.wait_ge(vectored, n + 1)
                if late(n, 1):
                    dve.wait_ge(reduced, 2 * n + h - 1)
                for t in range(HALF):
                    k = h * HALF + t
                    bank = (b * GROUP + k) % 4
                    dve.wait_ge(radial_ready, n * GROUP + k + 1)
                    TT(prodA[:, h, t], psM[:, bank, 0:NA].rearrange("p (w u) -> p w u", u=W16),
                       bc(z[:, b, k], 2, W16), ALU.mult)
                    TT(prodB[:, h, t].rearrange("p w (u o) -> p w u o", o=3),
                       bc(psM[:, bank, NA:RADIAL].rearrange("p (w u) -> p w u", u=MUL), 3, 3),
                       bc(V[:, b, k], 2, MUL), ALU.mult).then_inc(prod_done, 1)
                    if t < len(between) and between[t]:
                        between[t]()
                dve.wait_ge(prod_done, n * GROUP + h * HALF + HALF)
                TT(prodB[:, h, :, 0:MUL], prodB[:, h, :, 0:MUL], prodB[:, h, :, MUL:], ALU.add).then_inc(preadded, 1)

            def post(n, b, h):
                dve.wait_ge(reduced, 2 * n + h + 1)
                cols = bass.ds(n * GROUP + h * HALF, HALF)
                terms = sums0.terms[:, b, :, h * HALF:(h + 1) * HALF]
                a = psR[:, h, 0:HALF * W16].rearrange("p (t u) -> p t u", u=W16)
                v = psR[:, h, HALF * W16:HALF * (W16 + 3 * MUL)].rearrange("p (t f) -> p f t", f=3 * MUL)
                TT(qr[:, h], bc(a[:, :, MUL:], 3, 3), bc(r5[:, cols, 0:3], 2, MUL), ALU.mult).then_inc(q_done, 1)
                TS(terms[:, 0:MUL], a[:, :, 0:MUL].rearrange("p t u -> p u t"), 1.0, None, ALU.mult)
                dve.wait_ge(q_done, 2 * n + h + 1)
                TT(terms[:, MUL:], qr[:, h].rearrange("p t v o -> p (v o) t"), v, ALU.add).then_inc(posted, 1)

            def join_chunk(layer, sums, same, n, b):
                if late(n, 1):
                    dve.wait_ge(summed_up[layer], n)
                    STT(sums.terms[:, b, :, 0], sums.run[:, 1 - b, :, GROUP - 1], same[:, bass.ds(n * GROUP, 1)],
                        sums.terms[:, b, :, 0], ALU.mult, ALU.add).then_inc(joined[layer], 1)

            def run_sums(layer, sums, n, b):
                if late(n, 1):
                    dve.wait_ge(joined[layer], n)
                dve.wait_ge(masked[layer], n + 1)
                dve.tensor_tensor_scan(sums.flat[1][:, b], sums.flat[2][:, b], sums.flat[0][:, b], 0.0,
                                       ALU.mult, ALU.add).then_inc(summed_up[layer], 1)

            def sum_terms0(n, b):
                dve.wait_ge(posted, 2 * n + 2)
                join_chunk(0, sums0, same_d, n, b)

            def sum_chunk0(n, b):
                if late(n):
                    dve.wait_ge(rows_ready, n - 1)
                run_sums(0, sums0, n, b)

            def layer0_step(n, b, prepare=True, back=True):
                products(n - 1, 1 - b, 0, (
                    prepare and (lambda: row_means(n, b)), prepare and (lambda: center(n, b)), None,
                    back and (lambda: post(n - 2, b, 0)),
                ))
                products(n - 1, 1 - b, 1, (
                    back and (lambda: post(n - 2, b, 1)), prepare and (lambda: invert(n, b)),
                    prepare and (lambda: norm(n, b)), back and (lambda: sum_terms0(n - 2, b)),
                    prepare and (lambda: dot(n, b)), None, back and (lambda: sum_chunk0(n - 2, b)),
                ))
                if prepare:
                    cross(n, b)
                    operands(n, b)

            row_means(0, 0)
            center(0, 0)

            dve.wait_ge(vstd, 1)
            st.link(dve.reciprocal(vn[:, 2], vn[:, 1]))
            st.do(TT(r5[:, :, 0:2], vec[:, :, 1:3], bc(vn[:, 2], 2, 2), ALU.mult))
            st.link(TT(r5[:, :, 2:5], vec[:], bc(vn[:, 2], 2, 3), ALU.mult))

            def segments(ext, same, last, opened):
                TT(same, ext[:, 1:COLS + 1], ext[:, 0:COLS], ALU.is_equal)
                st.link(TT(last, ext[:, 1:COLS + 1], ext[:, 2:], ALU.not_equal))
                st.link(dve.tensor_tensor_scan(opened, same, same, 1.0, ALU.mult, ALU.mult))

            segments(dst_ext, same_d[:], last[:], opened[:])
            TT(idx_tmp[:], dst_f[:], pos[:], ALU.subtract)
            TT(ends_in[:], opened[:], last[:], ALU.mult)
            st.link(TS(openrep[:], ones32[:], opened[:, COLS - 1:], None, ALU.mult))
            st.do(dve.tensor_reduce(crosses[:, 0:1], ends_in[:], AX.X, ALU.max))
            st.link(TT(idx_tmp[:], idx_tmp[:], last[:], ALU.mult))
            TT(idx_dst[:], idx_tmp[:], pos[:], ALU.add).then_inc(idx_ready, 1)
            st.link(TT(picked[:, 0:1], dst_f[:, 0:1], pos[:, 0:1], ALU.subtract))
            st.do(STT(idx_carry[:, 0:1], picked[:, 0:1], crosses[:, 0:1], pos[:, 0:1], ALU.mult, ALU.add))
            st.do(dve.memset(sums0.mask[:, :, :, 0:1], 0.0))

            for step in (invert, norm, dot, cross, operands):
                step(0, 0)
            layer0_step(1, 1, back=False)
            layer0_step(2, 0)
            layer0_step(3, 1)
            with dve.Fori(2, CHUNKS // 2) as i:
                layer0_step(2 * i, 0)
                layer0_step(2 * i + 1, 1)
            layer0_step(CHUNKS, 0, prepare=False)
            for h in range(2):
                post(CHUNKS - 1, 1, h)
            sum_terms0(CHUNKS - 1, 1)
            sum_chunk0(CHUNKS - 1, 1)

            def carry_over(layer, sums):
                dve.wait_ge(summed_up[layer], CHUNKS)
                dve.tensor_copy(lend[:], sums.run[:, 1, :, GROUP - 1]).then_inc(ended, 1)
                dve.wait_ge(ends_turned, 2 * layer + 1)
                st.link(dve.tensor_copy(openT[:], psT[0:FEAT, P:2 * P]))
                dve.tensor_tensor_scan(chain[:, 1:], openT[:], psT[0:FEAT, 0:P], 0.0, ALU.mult, ALU.add
                                       ).then_inc(chained, 1)
                dve.wait_ge(ends_turned, 2 * layer + 2)
                dve.tensor_copy(carry[:], psT[:, 2 * P:2 * P + FEAT]).then_inc(carried, 1)

            carry_over(0, sums0)

            for k in range(2):
                st.do(TT(wmul[:, k], wrep[:], bc(fcw_b[:, k * FEAT:(k + 1) * FEAT], 1, HEADS), ALU.mult))
            st.do(dve.memset(ublk[:], 0.0))
            st.link(TS(wstk[:], wstk_raw[:], 1.0 / HEADS, None, ALU.mult))
            st.link(dve.tensor_reduce(u_all[:], wmul[:], AX.X, ALU.add))
            for k in range(2):
                for t in range(4):
                    put = dve.tensor_copy(ublk[32 * t:32 * t + 32, k, HEADS * t:HEADS * (t + 1)],
                                          u_all[32 * t:32 * t + 32, k])
            put.then_inc(lweights, 1)

            dve.wait_ge(srcorder_in, 2 * DMA)
            key = key_ext[:, 1:COLS + 1]
            dve.tensor_copy(idx_src[:], key).then_inc(idx_ready, 1)
            dve.tensor_copy(idx_dst_s[:], pay[:]).then_inc(idx_ready, 1)
            segments(key_ext, same[:], last[:], opened[:])
            st.link(TT(more[:], key, key_ext[:, 2:], ALU.is_equal))
            st.do(TS(negs[:, 0], same[:], 1.0, BIG, ALU.subtract, ALU.mult))
            st.do(TS(negs[:, 1], last[:], -BIG, None, ALU.mult))
            st.link(TT(ends_in[:], opened[:], last[:], ALU.mult))
            st.do(dve.tensor_reduce(crosses[:, 1:2], ends_in[:], AX.X, ALU.max))
            st.do(TT(idx_tmp[:], last[:], ends_in[:], ALU.subtract))
            st.link(dve.tensor_tensor_scan(openR[:, ::-1], more[:, ::-1], more[:, ::-1], 1.0, ALU.mult, ALU.mult))
            st.link(TS(idx_tmp[:], idx_tmp[:], 1.0, -2.0 * NODES, ALU.subtract, ALU.mult))
            st.do(TS(picked[:, 0:1], crosses[:, 1:2], 1.0, -2.0 * NODES, ALU.subtract, ALU.mult))
            TT(idx_out[:], idx_tmp[:], key, ALU.add).then_inc(idx_ready, 1)
            st.settle()
            st.do(TT(idx_carry[:, 1:2], picked[:, 0:1], key[:, 0:1], ALU.add))
            st.do(TS(openrep[:], ones32[:], opened[:, COLS - 1:], None, ALU.mult))
            st.do(TS(negopen[:, 0], opened[:], 1.0, BIG, ALU.subtract, ALU.mult))
            st.link(TS(negopen[:, 1], openR[:], 1.0, BIG, ALU.subtract, ALU.mult))

            for k, whole in enumerate((negopen[:, 0, COLS - 1:], negopen[:, 1, 0:1], opened[:, COLS - 1:],
                                       openR[:, 0:1])):
                st.do(TS(open4[:, k], ones32[:, 0:HEADS], whole, None, ALU.mult))
                st.do(dve.memset(ladder[:, k, 0:1] if k % 2 == 0 else ladder[:, k, P:], JOIN_START[k]))
            st.settle()
            dve.sem_inc(opens_ready, 1)
            dve.wait_ge(opens_turned, 1)
            st.link(dve.tensor_copy(openT4[:].rearrange("h k p -> h (k p)"), psT[0:HEADS]))

            def stage_rows(n, b):
                dve.tensor_copy(stage_l[:, b, 0], idx_src[:, chunk_cols(n)])
                dve.tensor_copy(stage_l[:, b, 1], idx_dst_s[:, chunk_cols(n)]).then_inc(l_staged, 1)

            dve.wait_ge(idx_ready, 3)
            stage_rows(0, 0)
            stage_rows(1, 1)

            def layer1_chunk(n, b, rounds, filling, staging=True):
                dve.wait_ge(l_in[b], 2 * GATHERED * rounds)
                dve.tensor_reduce(lsum[:, b], lring[:, b], AX.X, ALU.add).then_inc(l_summed, 1)
                if staging:
                    stage_rows(n + 2, b)
                dve.wait_ge(l_summed, n + 1)
                TS(mean[:, b], lsum[:, b], 1.0 / FEAT, None, ALU.mult).then_inc(l_meaned, 1)
                dve.wait_ge(l_meaned, n + 1)
                TT(lxc, lring[:, b], bc(mean[:, b], 2, FEAT), ALU.subtract).then_inc(l_centered, 1)
                TT(xsb[:, chunk_cols(n)], lring[:, b, 0:GROUP], bc(bias_b[:], 1, GROUP), ALU.add).then_inc(l_based, 1)
                if filling:
                    rows = fill[:, b].rearrange("p (r d) -> p r d", d=FEAT)
                    dve.wait_ge(fill_in[b], DMA * rounds)
                    TT(rows, rows, bc(bias_b[0:FILL_P], 1, FILL_ROWS), ALU.add).then_inc(fill_added, 1)
                dve.wait_ge(l_squared, n + 1)
                dve.tensor_reduce(vsum[:, b], lsq, AX.X, ALU.add).then_inc(l_varsummed, 1)
                dve.wait_ge(l_stded, n + 1)
                dve.reciprocal(rstd[:, b], std[:, b]).then_inc(l_rstded, 1)
                dve.wait_ge(l_rstded, n + 1)
                if late(n):
                    dve.wait_ge(l_saved, n - 1)
                    dve.wait_ge(l_turned, 4 * (n - 1))
                STT(lh[:, b], lxc, 0.0, bc(rstd[:, b], 2, FEAT), ALU.max, ALU.mult).then_inc(l_normed, 1)
                dve.wait_ge(l_logits, 4 * (n + 1))
                TS(lgt[:], psR[:, b, 0:GROUP * HEADS], fcb_b[:], None, ALU.add).then_inc(l_biased, 1)
                dve.wait_ge(l_biased, n + 1)
                STT(E[:, chunk_cols(n)].rearrange("p t h -> p (t h)"), lgt[:], 0.2, lgt[:], ALU.mult, ALU.max
                    ).then_inc(l_logged, 1)
                dve.wait_ge(l_logged, n + 1)
                if late(n, 1):
                    dve.wait_ge(running, n)
                for h in range(HEADS):
                    start = soft[:, 0, bass.ds(n * GROUP - 1, 1), h] if late(n, 1) else SOFT_START[0]
                    maxima = dve.tensor_tensor_scan(soft[:, 0, chunk_cols(n), h], negs[:, 0, chunk_cols(n)],
                                                    E[:, chunk_cols(n), h], start, ALU.add, ALU.max)
                maxima.then_inc(running, 1)

            layer1_chunk(0, 0, 1, True)
            layer1_chunk(1, 1, 1, True)
            with dve.Fori(1, FILLS // 2) as i:
                for b in range(2):
                    layer1_chunk(2 * i + b, b, i + 1, True)
            with dve.Fori(FILLS // 2, CHUNKS // 2 - 1) as i:
                for b in range(2):
                    layer1_chunk(2 * i + b, b, i + 1, False)
            for b in range(2):
                layer1_chunk(CHUNKS - 2 + b, b, CHUNKS // 2, False, staging=False)

            dve.wait_ge(idx_ready, 4)
            run, back, shift, prob = (soft[:, k] for k in range(4))

            def heads(scan):
                for h in range(HEADS):
                    last_one = scan(h)
                return last_one

            def join_ends(step, op0, op1):
                dve.wait_ge(s_turned, 2 * step + 1)
                if step % 2 == 0:
                    dve.tensor_tensor_scan(ladder[:, step, 1:], openT4[:, step], psT[0:HEADS, 0:P],
                                           JOIN_START[step], op0, op1).then_inc(joining, 1)
                else:
                    dve.tensor_tensor_scan(ladder[:, step, 0:P][:, ::-1], openT4[:, step, ::-1],
                                           psT[0:HEADS, 0:P][:, ::-1], JOIN_START[step], op0, op1
                                           ).then_inc(joining, 1)
                dve.wait_ge(s_turned, 2 * step + 2)
                st.link(dve.tensor_copy(join[:, step], psT[:, P:P + HEADS]))

            def add_join(step, values, opens, op0, op1):
                return heads(lambda h: STT(values[:, :, h], opens, join[:, step, h:h + 1], values[:, :, h], op0, op1))

            def from_right(mask, data, step, op0, op1):
                heads(lambda h: dve.tensor_tensor_scan(back[:, ::-1, h], mask[:, ::-1], data[:, ::-1, h],
                                                       SOFT_START[step], op0, op1)).then_inc(joining, 1)

            join_ends(0, ALU.add, ALU.max)
            st.link(add_join(0, run, negopen[:, 0], ALU.add, ALU.max))
            from_right(negs[:, 1], run, 1, ALU.add, ALU.max)
            join_ends(1, ALU.add, ALU.max)
            st.link(add_join(1, back, negopen[:, 1], ALU.add, ALU.max))
            TT(shift, E, back, ALU.subtract).then_inc(shifted, 1)
            dve.wait_ge(s_exp, 1)
            heads(lambda h: dve.tensor_tensor_scan(run[:, :, h], same[:], prob[:, :, h], 0.0, ALU.mult, ALU.add)
                  ).then_inc(joining, 1)
            join_ends(2, ALU.mult, ALU.add)
            st.link(add_join(2, run, opened[:], ALU.mult, ALU.add))
            st.link(TT(shift, run, bc(last[:], 2, HEADS), ALU.mult))
            from_right(more[:], shift, 3, ALU.mult, ALU.add)
            join_ends(3, ALU.mult, ALU.add)
            st.link(add_join(3, back, openR[:], ALU.mult, ALU.add))

            def weigh(n, b):
                dve.reciprocal(shares[:, b], back[:, chunk_cols(n)]).then_inc(inverted, 1)
                dve.wait_ge(inverted, n + 1)
                TT(shares[:, b], shares[:, b], prob[:, chunk_cols(n)], ALU.mult).then_inc(shared, 1)
                dve.wait_ge(shared, n + 1)
                if late(n):
                    dve.wait_ge(m_turned, 4 * (n - 1))
                TT(weighted[:, b].rearrange("p t (h f) -> p t h f", h=HEADS), bc(hd[:, chunk_cols(n)], 2, HEADS),
                   bc(shares[:, b], 3, FEAT), ALU.mult).then_inc(weighed, 1)

            def finish(n, b, rounds):
                dve.wait_ge(m_out, n + 1)
                join_chunk(1, sums1, same, n, b)
                run_sums(1, sums1, n, b)
                if not isinstance(rounds, int) or rounds > 0:
                    dve.wait_ge(out_done[b], GATHERED * rounds)
                dve.wait_ge(summed_up[1], n + 1)
                TT(rowring[:, b], sums1.run[:, b].rearrange("p f t -> p t f"), xsb[:, chunk_cols(n)], ALU.add)
                dve.tensor_copy(stage_out[:, b], idx_out[:, chunk_cols(n)]).then_inc(out_rows, 1)
                dve.wait_ge(out_rows, n + 1)
                TT(picks, rowring[:, b].rearrange("p t f -> p f t"), bc(ends_in[:, chunk_cols(n)], 1, FEAT), ALU.mult
                   ).then_inc(multiplied, 1)
                dve.wait_ge(multiplied, n + 1)
                dve.tensor_reduce(picked[:], picks, AX.X, ALU.add).then_inc(picking, 1)
                dve.wait_ge(picking, n + 1)
                if late(n, 1):
                    dve.wait_ge(holding, n)
                    TT(held[:], held[:], picked[:], ALU.add).then_inc(holding, 1)
                else:
                    dve.tensor_copy(held[:], picked[:]).then_inc(holding, 1)

            dve.wait_ge(l_saved, CHUNKS)
            dve.memset(sums1.mask[:, :, :, 0:1], 0.0)
            weigh(0, 0)
            weigh(1, 1)
            finish(0, 0, 0)
            weigh(2, 0)
            finish(1, 1, 0)
            with dve.Fori(1, CHUNKS // 2 - 1) as i:
                weigh(2 * i + 1, 1)
                finish(2 * i, 0, i)
                weigh(2 * i + 2, 0)
                finish(2 * i + 1, 1, i)
            weigh(CHUNKS - 1, 1)
            finish(CHUNKS - 2, 0, CHUNKS // 2 - 1)
            finish(CHUNKS - 1, 1, CHUNKS // 2 - 1)
            carry_over(1, sums1)
            dve.wait_ge(carried, 2)
            dve.wait_ge(holding, CHUNKS)
            TT(held[:], held[:], carry[:], ALU.add).then_inc(holding, 1)


_INS = ["x", "src", "dst", "edge_attr_3", "edge_weight", "L0_gnn_w1", "L0_gnn_b1", "L0_gnn_w2", "L0_gnn_b2",
        "L1_gnn_w", "L1_gnn_fc_w", "L1_gnn_fc_b", "L1_gnn_bias"]


def shape_constants():
    eye = np.eye(P, dtype=np.float32)
    posn = (NODES + np.arange(SLOTS)).reshape(P, COLS).astype(np.float32)
    p = np.arange(P)
    f = [1.0 - 2.0 * ((p >> b) & 1) for b in range(7)]
    flips = np.stack([f[0], -f[0]] + [f[b] * f[b + 1] for b in range(6)] + [f[6]], 1).astype(np.float32)
    return {"eye": eye, "posn": posn, "flips": flips}


def kernel(**inputs):
    import concourse.bacc as _bacc
    from concourse.bass_utils import run_bass_kernel_spmd as _run

    nc = _bacc.Bacc("TRN2", target_bir_lowering=False, num_devices=1)
    arrays, args = {}, []
    given = {n: np.ascontiguousarray(inputs[n]) for n in _INS}
    for name, a in {**given, **shape_constants()}.items():
        arrays[f"in_{name}_dram"] = a
        args.append(nc.dram_tensor(f"in_{name}_dram", a.shape, mybir.dt.from_np(a.dtype), kind="ExternalInput").ap())
    out = nc.dram_tensor("out_0_dram", (NODES, FEAT), F32, kind="ExternalOutput").ap()
    graph_layers(nc, *args, out)
    r = _run(nc, [arrays], core_ids=[0])
    return r.results[0]["out_0_dram"]
```
